# Optimizing a Trainium2 kernel written in Bass

```python
import numpy as np
import jax
import jax.numpy as jnp

def _softmax(x, axis=-1):
    return jax.nn.softmax(x, axis=axis)

def _gelu(x):
    return jax.nn.gelu(x, approximate=True)

def _silu(x):
    return jax.nn.silu(x)

def _sigmoid(x):
    return jax.nn.sigmoid(x)

def _layernorm(x, axis=-1, eps=1e-05):
    m = jnp.mean(x, axis=axis, keepdims=True)
    v = jnp.var(x, axis=axis, keepdims=True)
    return (x - m) / jnp.sqrt(v + eps)

def _scatter_add(tgt, idx, src, axis=0):
    return tgt.at[idx].add(src)

def _segment_sum(src, seg, n):
    return jax.ops.segment_sum(src, seg, n)
kernel_name = 'mk_lm_tower_d1_tok_ids1024_r4_885e0d'

def setup_inputs(seed: int=0):
    np.random.seed(seed)
    _w = jnp.asarray

    def _rec_inputs():
        import jax
        import jax.numpy as jnp
        _rk = jax.random.key(seed)
        x = jax.random.randint(jax.random.fold_in(_rk, 1), (4, 2048), 0, 28, jnp.int32)
        mask_BS_i1_0 = jnp.where(jnp.ones((4, 2048), dtype=bool), 1, 0).astype(jnp.int32)
        return (x, mask_BS_i1_0)
    x, mask_BS_i1_0 = _rec_inputs()

    def _L0_tok_setup():
        import jax, jax.numpy as jnp
        import numpy as np
        WINDOW_SIZE = 3
        LN_EPS = 1e-05

        def _sliding_window_features(base_pca, mask_f):
            B, S, F = base_pca.shape
            h = WINDOW_SIZE // 2
            idx = jnp.arange(S)
            start = jnp.maximum(idx - h, 0)
            end = jnp.minimum(idx + h + 1, S)
            masked = base_pca * mask_f[..., None]
            csum = jnp.pad(jnp.cumsum(masked, axis=1), ((0, 0), (1, 0), (0, 0)))
            wsum = csum[:, end, :] - csum[:, start, :]
            mcs = jnp.pad(jnp.cumsum(mask_f, axis=1), ((0, 0), (1, 0)))
            lengths = jnp.maximum(mcs[:, end] - mcs[:, start], 1.0)
            return wsum / lengths[..., None]
        key = jax.random.key(seed)
        ks = jax.random.split(key, 8)
        B, S, V, E = (8, 1024, 28, 256)
        input_ids = jax.random.randint(ks[0], (B, S), 0, V, dtype=jnp.int64)
        attention_mask = jnp.ones((B, S), dtype=jnp.int32)
        emb = jax.random.normal(ks[1], (V, E), dtype=jnp.float32) * 0.02
        emb = emb.at[0].set(0.0)
        pca_lookup = jax.random.normal(ks[2], (V, 20), dtype=jnp.float32)
        proj_w = jax.random.normal(ks[3], (20, E), dtype=jnp.float32) * 0.2
        proj_b = jnp.zeros((E,), dtype=jnp.float32)
        fus_w = jax.random.normal(ks[4], (2 * E, E), dtype=jnp.float32) * 0.02
        fus_b = jnp.zeros((E,), dtype=jnp.float32)
        ln_g = jnp.ones((E,), dtype=jnp.float32)
        ln_b = jnp.zeros((E,), dtype=jnp.float32)
        return {'input_ids': input_ids, 'attention_mask': attention_mask, 'emb': emb, 'pca_lookup': pca_lookup, 'proj_w': proj_w, 'proj_b': proj_b, 'fus_w': fus_w, 'fus_b': fus_b, 'ln_g': ln_g, 'ln_b': ln_b}
    _L0_tok_all = _L0_tok_setup()
    _L0_tok_in = {k: v for k, v in _L0_tok_all.items() if k in ('emb', 'pca_lookup', 'proj_w', 'proj_b', 'fus_w', 'fus_b', 'ln_g', 'ln_b')}
    del _L0_tok_all

    def _L0_attn_setup():
        import jax, jax.numpy as jnp
        import numpy as np
        B, T, D, H = (8, 1024, 256, 16)
        DK = D // H
        CHUNK = 64
        E, TOPK, MULT, CAPF = (8, 2, 4, 1.25)
        HID = D * MULT
        N = B * T
        CAPACITY = int(CAPF * (N / E))

        def rmsnorm(x, scale):
            return x / jnp.sqrt(jnp.mean(x * x, axis=-1, keepdims=True)) * scale

        def apply_rope(x):
            half = x.shape[-1] // 2
            t = x.shape[2]
            inv = 1.0 / 10000.0 ** (jnp.arange(half, dtype=jnp.float32) / half)
            ang = jnp.arange(t, dtype=jnp.float32)[:, None] * inv[None, :]
            sin, cos = (jnp.sin(ang)[None, None], jnp.cos(ang)[None, None])
            x1, x2 = (x[..., :half], x[..., half:])
            return jnp.concatenate([x1 * cos - x2 * sin, x1 * sin + x2 * cos], axis=-1)

        def phi(x):
            return jax.nn.elu(x) + 1.0

        def attention(x, Wq, bq, Wk, bk, Wv, bv, Wg, bg, Wo, bo):
            b, t, c = x.shape
            heads = lambda y: y.reshape(b, t, H, DK).transpose(0, 2, 1, 3)
            q = phi(apply_rope(heads(x @ Wq + bq)))
            k = phi(apply_rope(heads(x @ Wk + bk)))
            v = heads(x @ Wv + bv)
            g = heads(jax.nn.sigmoid(x @ Wg + bg))
            nc = t // CHUNK
            to_chunks = lambda y: y.reshape(b, H, nc, CHUNK, DK).transpose(2, 0, 1, 3, 4)
            qs, ks_, vs, gs = map(to_chunks, (q, k, v, g))
            S0 = jnp.zeros((b, H, DK, DK), x.dtype)
            Z0 = jnp.zeros((b, H, DK), x.dtype)

            def step(carry, inp):
                S, Z = carry
                qc, kc, vc, gc = inp
                S = S + jnp.einsum('bhtd,bhte->bhde', kc, vc)
                Z = Z + kc.sum(axis=2)
                num = jnp.einsum('bhtd,bhde->bhte', qc, S)
                den = jnp.einsum('bhtd,bhd->bht', qc, Z)[..., None] + 1e-06
                return ((S, Z), gc * (num / den))
            _, outs = jax.lax.scan(step, (S0, Z0), (qs, ks_, vs, gs))
            out = outs.transpose(1, 2, 0, 3, 4).reshape(b, H, t, DK)
            out = out.transpose(0, 2, 1, 3).reshape(b, t, c)
            return out @ Wo + bo

        def moe(x, router_W, router_b, W1, b1, W2, b2):
            b, t, c = x.shape
            n = b * t
            xf = x.reshape(n, c)
            probs = jax.nn.softmax(xf @ router_W + router_b, axis=-1)
            topk_probs, topk_idx = jax.lax.top_k(probs, TOPK)
            topk_probs = topk_probs / topk_probs.sum(axis=-1, keepdims=True)
            out = jnp.zeros_like(xf)
            load = []
            for eid in range(E):
                mask = (topk_idx == eid).reshape(-1)
                idx = jnp.nonzero(mask, size=CAPACITY, fill_value=n * TOPK)[0]
                valid = idx < n * TOPK
                idxc = jnp.minimum(idx, n * TOPK - 1)
                tok, choice = (idxc // TOPK, idxc % TOPK)
                h = jax.nn.gelu(xf[tok] @ W1[eid] + b1[eid], approximate=False) @ W2[eid] + b2[eid]
                gate = jnp.where(valid, topk_probs[tok, choice], 0.0)
                out = out.at[tok].add(gate[:, None] * h)
                load.append(jnp.minimum(mask.sum(), CAPACITY).astype(xf.dtype))
            load = jnp.stack(load)
            importance = probs.sum(axis=0)
            importance = importance / importance.sum()
            load = load / load.sum()
            aux = (importance * load).sum() * E ** 2
            return (out.reshape(b, t, c), aux)

        def _reference_tuple_inner(x, norm1_scale, norm2_scale, Wq, bq, Wk, bk, Wv, bv, Wg, bg, Wo, bo, router_W, router_b, W1, b1, W2, b2):
            x = x + attention(rmsnorm(x, norm1_scale), Wq, bq, Wk, bk, Wv, bv, Wg, bg, Wo, bo)
            moe_out, aux = moe(rmsnorm(x, norm2_scale), router_W, router_b, W1, b1, W2, b2)
            return (x + moe_out, aux)
        key = jax.random.key(seed)
        ks = jax.random.split(key, 16)
        s = 0.02
        r = lambda k, shape: jax.random.normal(k, shape, jnp.float32) * s
        return {'x': jax.random.normal(ks[0], (B, T, D), jnp.float32), 'norm1_scale': jnp.ones((D,), jnp.float32), 'norm2_scale': jnp.ones((D,), jnp.float32), 'Wq': r(ks[1], (D, D)), 'bq': jnp.zeros((D,), jnp.float32), 'Wk': r(ks[2], (D, D)), 'bk': jnp.zeros((D,), jnp.float32), 'Wv': r(ks[3], (D, D)), 'bv': jnp.zeros((D,), jnp.float32), 'Wg': r(ks[4], (D, D)), 'bg': jnp.zeros((D,), jnp.float32), 'Wo': r(ks[5], (D, D)), 'bo': jnp.zeros((D,), jnp.float32), 'router_W': r(ks[6], (D, E)), 'router_b': jnp.zeros((E,), jnp.float32), 'W1': r(ks[7], (E, D, HID)), 'b1': jnp.zeros((E, HID), jnp.float32), 'W2': r(ks[8], (E, HID, D)), 'b2': jnp.zeros((E, D), jnp.float32)}
    _L0_attn_all = _L0_attn_setup()
    _L0_attn_in = {k: v for k, v in _L0_attn_all.items() if k in ('norm1_scale', 'norm2_scale', 'Wq', 'bq', 'Wk', 'bk', 'Wv', 'bv', 'Wg', 'bg', 'Wo', 'bo', 'router_W', 'router_b', 'W1', 'b1', 'W2', 'b2')}
    del _L0_attn_all

    def _L0_ffn_setup():
        import jax, jax.numpy as jnp
        import numpy as np
        T, Z, D_DIM = (8, 512, 256)
        N_EXP, P_SLOT, H = (64, 32, 256)
        LN_EPS = 1e-05
        key = jax.random.key(seed)
        k = jax.random.split(key, 5)
        s = 0.02
        return {'x': jax.random.normal(k[0], (T, Z, D_DIM), dtype=jnp.float32), 'phi_w': jax.random.normal(k[1], (N_EXP * P_SLOT, D_DIM), dtype=jnp.float32) * s, 'phi_b': jax.random.normal(k[2], (N_EXP * P_SLOT,), dtype=jnp.float32) * s, 'expert_w': jax.random.normal(k[3], (N_EXP, D_DIM, H), dtype=jnp.float32) * s, 'expert_b': jax.random.normal(k[4], (N_EXP, H), dtype=jnp.float32) * s}
    _L0_ffn_all = _L0_ffn_setup()
    _L0_ffn_in = {k: v for k, v in _L0_ffn_all.items() if k in ('phi_w', 'phi_b', 'expert_w', 'expert_b')}
    del _L0_ffn_all
    return {'x': x, 'mask_BS_i1_0': mask_BS_i1_0, 'L0_tok_emb': _L0_tok_in['emb'], 'L0_tok_pca_lookup': _L0_tok_in['pca_lookup'], 'L0_tok_proj_w': _L0_tok_in['proj_w'], 'L0_tok_proj_b': _L0_tok_in['proj_b'], 'L0_tok_fus_w': _L0_tok_in['fus_w'], 'L0_tok_fus_b': _L0_tok_in['fus_b'], 'L0_tok_ln_g': _L0_tok_in['ln_g'], 'L0_tok_ln_b': _L0_tok_in['ln_b'], 'L0_attn_norm1_scale': _L0_attn_in['norm1_scale'], 'L0_attn_norm2_scale': _L0_attn_in['norm2_scale'], 'L0_attn_Wq': _L0_attn_in['Wq'], 'L0_attn_bq': _L0_attn_in['bq'], 'L0_attn_Wk': _L0_attn_in['Wk'], 'L0_attn_bk': _L0_attn_in['bk'], 'L0_attn_Wv': _L0_attn_in['Wv'], 'L0_attn_bv': _L0_attn_in['bv'], 'L0_attn_Wg': _L0_attn_in['Wg'], 'L0_attn_bg': _L0_attn_in['bg'], 'L0_attn_Wo': _L0_attn_in['Wo'], 'L0_attn_bo': _L0_attn_in['bo'], 'L0_attn_router_W': _L0_attn_in['router_W'], 'L0_attn_router_b': _L0_attn_in['router_b'], 'L0_attn_W1': _L0_attn_in['W1'], 'L0_attn_b1': _L0_attn_in['b1'], 'L0_attn_W2': _L0_attn_in['W2'], 'L0_attn_b2': _L0_attn_in['b2'], 'L0_ffn_phi_w': _L0_ffn_in['phi_w'], 'L0_ffn_phi_b': _L0_ffn_in['phi_b'], 'L0_ffn_expert_w': _L0_ffn_in['expert_w'], 'L0_ffn_expert_b': _L0_ffn_in['expert_b']}

def reference(x, mask_BS_i1_0, L0_tok_emb, L0_tok_pca_lookup, L0_tok_proj_w, L0_tok_proj_b, L0_tok_fus_w, L0_tok_fus_b, L0_tok_ln_g, L0_tok_ln_b, L0_attn_norm1_scale, L0_attn_norm2_scale, L0_attn_Wq, L0_attn_bq, L0_attn_Wk, L0_attn_bk, L0_attn_Wv, L0_attn_bv, L0_attn_Wg, L0_attn_bg, L0_attn_Wo, L0_attn_bo, L0_attn_router_W, L0_attn_router_b, L0_attn_W1, L0_attn_b1, L0_attn_W2, L0_attn_b2, L0_ffn_phi_w, L0_ffn_phi_b, L0_ffn_expert_w, L0_ffn_expert_b):
    import jax
    import jax.numpy as jnp

    def _L0_tok_ref(input_ids, attention_mask, emb, pca_lookup, proj_w, proj_b, fus_w, fus_b, ln_g, ln_b):
        import jax, jax.numpy as jnp
        import numpy as np
        WINDOW_SIZE = 3
        LN_EPS = 1e-05

        def _sliding_window_features(base_pca, mask_f):
            B, S, F = base_pca.shape
            h = WINDOW_SIZE // 2
            idx = jnp.arange(S)
            start = jnp.maximum(idx - h, 0)
            end = jnp.minimum(idx + h + 1, S)
            masked = base_pca * mask_f[..., None]
            csum = jnp.pad(jnp.cumsum(masked, axis=1), ((0, 0), (1, 0), (0, 0)))
            wsum = csum[:, end, :] - csum[:, start, :]
            mcs = jnp.pad(jnp.cumsum(mask_f, axis=1), ((0, 0), (1, 0)))
            lengths = jnp.maximum(mcs[:, end] - mcs[:, start], 1.0)
            return wsum / lengths[..., None]
        token_embeds = emb[input_ids]
        base_pca = pca_lookup[input_ids]
        pca_feat = _sliding_window_features(base_pca, attention_mask.astype(jnp.float32))
        cont = pca_feat @ proj_w + proj_b
        combined = jnp.concatenate([token_embeds, cont], axis=-1)
        fused = combined @ fus_w + fus_b
        mu = jnp.mean(fused, axis=-1, keepdims=True)
        var = jnp.mean(jnp.square(fused - mu), axis=-1, keepdims=True)
        return (fused - mu) * jax.lax.rsqrt(var + LN_EPS) * ln_g + ln_b

    def _L0_attn_ref(x, norm1_scale, norm2_scale, Wq, bq, Wk, bk, Wv, bv, Wg, bg, Wo, bo, router_W, router_b, W1, b1, W2, b2):
        import jax, jax.numpy as jnp
        import numpy as np
        B, T, D, H = (8, 1024, 256, 16)
        DK = D // H
        CHUNK = 64
        E, TOPK, MULT, CAPF = (8, 2, 4, 1.25)
        HID = D * MULT
        N = B * T
        CAPACITY = int(CAPF * (N / E))

        def rmsnorm(x, scale):
            return x / jnp.sqrt(jnp.mean(x * x, axis=-1, keepdims=True)) * scale

        def apply_rope(x):
            half = x.shape[-1] // 2
            t = x.shape[2]
            inv = 1.0 / 10000.0 ** (jnp.arange(half, dtype=jnp.float32) / half)
            ang = jnp.arange(t, dtype=jnp.float32)[:, None] * inv[None, :]
            sin, cos = (jnp.sin(ang)[None, None], jnp.cos(ang)[None, None])
            x1, x2 = (x[..., :half], x[..., half:])
            return jnp.concatenate([x1 * cos - x2 * sin, x1 * sin + x2 * cos], axis=-1)

        def phi(x):
            return jax.nn.elu(x) + 1.0

        def attention(x, Wq, bq, Wk, bk, Wv, bv, Wg, bg, Wo, bo):
            b, t, c = x.shape
            heads = lambda y: y.reshape(b, t, H, DK).transpose(0, 2, 1, 3)
            q = phi(apply_rope(heads(x @ Wq + bq)))
            k = phi(apply_rope(heads(x @ Wk + bk)))
            v = heads(x @ Wv + bv)
            g = heads(jax.nn.sigmoid(x @ Wg + bg))
            nc = t // CHUNK
            to_chunks = lambda y: y.reshape(b, H, nc, CHUNK, DK).transpose(2, 0, 1, 3, 4)
            qs, ks_, vs, gs = map(to_chunks, (q, k, v, g))
            S0 = jnp.zeros((b, H, DK, DK), x.dtype)
            Z0 = jnp.zeros((b, H, DK), x.dtype)

            def step(carry, inp):
                S, Z = carry
                qc, kc, vc, gc = inp
                S = S + jnp.einsum('bhtd,bhte->bhde', kc, vc)
                Z = Z + kc.sum(axis=2)
                num = jnp.einsum('bhtd,bhde->bhte', qc, S)
                den = jnp.einsum('bhtd,bhd->bht', qc, Z)[..., None] + 1e-06
                return ((S, Z), gc * (num / den))
            _, outs = jax.lax.scan(step, (S0, Z0), (qs, ks_, vs, gs))
            out = outs.transpose(1, 2, 0, 3, 4).reshape(b, H, t, DK)
            out = out.transpose(0, 2, 1, 3).reshape(b, t, c)
            return out @ Wo + bo

        def moe(x, router_W, router_b, W1, b1, W2, b2):
            b, t, c = x.shape
            n = b * t
            xf = x.reshape(n, c)
            probs = jax.nn.softmax(xf @ router_W + router_b, axis=-1)
            topk_probs, topk_idx = jax.lax.top_k(probs, TOPK)
            topk_probs = topk_probs / topk_probs.sum(axis=-1, keepdims=True)
            out = jnp.zeros_like(xf)
            load = []
            for eid in range(E):
                mask = (topk_idx == eid).reshape(-1)
                idx = jnp.nonzero(mask, size=CAPACITY, fill_value=n * TOPK)[0]
                valid = idx < n * TOPK
                idxc = jnp.minimum(idx, n * TOPK - 1)
                tok, choice = (idxc // TOPK, idxc % TOPK)
                h = jax.nn.gelu(xf[tok] @ W1[eid] + b1[eid], approximate=False) @ W2[eid] + b2[eid]
                gate = jnp.where(valid, topk_probs[tok, choice], 0.0)
                out = out.at[tok].add(gate[:, None] * h)
                load.append(jnp.minimum(mask.sum(), CAPACITY).astype(xf.dtype))
            load = jnp.stack(load)
            importance = probs.sum(axis=0)
            importance = importance / importance.sum()
            load = load / load.sum()
            aux = (importance * load).sum() * E ** 2
            return (out.reshape(b, t, c), aux)

        def _reference_tuple_inner(x, norm1_scale, norm2_scale, Wq, bq, Wk, bk, Wv, bv, Wg, bg, Wo, bo, router_W, router_b, W1, b1, W2, b2):
            x = x + attention(rmsnorm(x, norm1_scale), Wq, bq, Wk, bk, Wv, bv, Wg, bg, Wo, bo)
            moe_out, aux = moe(rmsnorm(x, norm2_scale), router_W, router_b, W1, b1, W2, b2)
            return (x + moe_out, aux)
        return _reference_tuple_inner(x, norm1_scale, norm2_scale, Wq, bq, Wk, bk, Wv, bv, Wg, bg, Wo, bo, router_W, router_b, W1, b1, W2, b2)[0]

    def _L0_ffn_ref(x, phi_w, phi_b, expert_w, expert_b):
        import jax, jax.numpy as jnp
        import numpy as np
        T, Z, D_DIM = (8, 512, 256)
        N_EXP, P_SLOT, H = (64, 32, 256)
        LN_EPS = 1e-05
        t, z, d = x.shape
        n = expert_w.shape[0]
        p = phi_w.shape[0] // n
        logits = (jnp.einsum('tzd,ed->tze', x, phi_w) + phi_b).reshape(t, z, n, p)
        D = jax.nn.softmax(logits, axis=3)
        C = jax.nn.softmax(logits, axis=2)
        X_tilde = jnp.einsum('tznp,tzd->npd', D, x)
        X_tilde = jnp.clip(X_tilde, -33000.0, 65000.0)
        mu = jnp.mean(X_tilde, axis=-1, keepdims=True)
        var = jnp.mean(jnp.square(X_tilde - mu), axis=-1, keepdims=True)
        X_tilde = (X_tilde - mu) * jax.lax.rsqrt(var + LN_EPS)
        X_tilde = jnp.tanh(X_tilde)
        Y_tilde = jnp.einsum('npd,ndH->npH', X_tilde, expert_w) + expert_b[:, None, :]
        Y = jnp.einsum('tznp,npH->tzH', C, Y_tilde)
        return Y
    h = _L0_tok_ref(x, mask_BS_i1_0, L0_tok_emb, L0_tok_pca_lookup, L0_tok_proj_w, L0_tok_proj_b, L0_tok_fus_w, L0_tok_fus_b, L0_tok_ln_g, L0_tok_ln_b)
    h = h + _L0_attn_ref(_layernorm(h, axis=-1), L0_attn_norm1_scale, L0_attn_norm2_scale, L0_attn_Wq, L0_attn_bq, L0_attn_Wk, L0_attn_bk, L0_attn_Wv, L0_attn_bv, L0_attn_Wg, L0_attn_bg, L0_attn_Wo, L0_attn_bo, L0_attn_router_W, L0_attn_router_b, L0_attn_W1, L0_attn_b1, L0_attn_W2, L0_attn_b2)
    h = h + _L0_ffn_ref(_layernorm(h, axis=-1), L0_ffn_phi_w, L0_ffn_phi_b, L0_ffn_expert_w, L0_ffn_expert_b)
    return h

_drawn_inputs = setup_inputs


def setup_inputs(seed=0):
    import zlib

    import numpy as np

    out = dict(_drawn_inputs(seed))
    spreads = {'L0_tok_proj_b': (0.0, 0.1),
     'L0_tok_fus_b': (0.0, 0.1),
     'L0_tok_ln_g': (1.0, 0.2),
     'L0_tok_ln_b': (0.0, 0.1),
     'L0_attn_norm1_scale': (1.0, 0.6),
     'L0_attn_norm2_scale': (1.0, 0.6),
     'L0_attn_bq': (0.0, 2.0),
     'L0_attn_bk': (0.0, 2.0),
     'L0_attn_bv': (0.0, 0.683),
     'L0_attn_bg': (0.0, 0.8),
     'L0_attn_bo': (0.0, 0.1),
     'L0_attn_router_b': (0.0, 0.277),
     'L0_attn_b1': (0.0, 0.8),
     'L0_attn_b2': (0.0, 0.329)}
    factors = {'L0_attn_Wq': 28.577,
     'L0_attn_Wk': 22.955,
     'L0_attn_Wv': 2.816,
     'L0_attn_Wg': 8.0,
     'L0_ffn_phi_b': 44.34}
    for name, (base, spread) in spreads.items():
        noise = np.random.default_rng([zlib.crc32(name.encode()), seed]).standard_normal(out[name].shape)
        drawn = base * np.exp(spread * noise) if base else spread * noise
        out[name] = jnp.asarray(drawn.astype(out[name].dtype))
    for name, factor in factors.items():
        out[name] = (out[name] * factor).astype(out[name].dtype)
    return out
```

```python
from contextlib import ExitStack

import numpy as np

import concourse.bass as bass
from concourse import mybir

F32 = mybir.dt.float32
F32R = mybir.dt.float32r
BF16 = mybir.dt.bfloat16
I32 = mybir.dt.int32
U32 = mybir.dt.uint32
ALU = mybir.AluOpType
ACT = mybir.ActivationFunctionType
X = mybir.AxisListType.X

P = 128
BATCH, SEQ, D = 4, 2048, 256
N_TOK = BATCH * SEQ
NT = N_TOK // P
TPB = SEQ // P
DH = D // P
VOCAB, N_PCA = 28, 20
HEADS, DK, CHUNK = 16, 16, 64
HPH = HEADS // DH
HALF = DK // 2
K_DVE = 130
N_EXP, HID, TOP = 8, 1024, 2
CAP = int(1.25 * (N_TOK / N_EXP))
N_SLOT = N_EXP * CAP
DROPPED = 1 << 20
SOFT_E, SOFT_P = 64, 32
SOFT = SOFT_E * SOFT_P
EPS = 1e-5
BDW = P + HPH

C_ID, C_TRI, C_BD, C_W8, C_OFF, C_ROW, C_ISB, C_PG = 0, 128, 256, 392, 400, 408, 409, 410
C_END = C_PG + 128


def constant_table():
    t = np.zeros((P, C_END), np.float32)
    p = np.arange(P)
    t[:, C_ID:C_ID + P] = np.eye(P)
    t[:, C_TRI:C_TRI + P] = p[:, None] < p[None, :]
    t[:, C_BD:C_BD + P] = p[:, None] // DK == p[None, :] // DK
    t[:, C_BD + P:C_BD + BDW] = p[:, None] // DK == np.arange(HPH)[None, :]
    t[:, C_W8:C_W8 + N_EXP] = N_EXP - np.arange(N_EXP)
    t[:, C_OFF:C_OFF + N_EXP] = CAP * np.arange(N_EXP)
    t[:, C_ROW] = p % 32
    t[:, C_ISB] = p % 32 == VOCAB
    t[:, C_PG:C_PG + P] = p[:, None] % SOFT_P == p[None, :] % SOFT_P
    return t


def rotary_table():
    inv = (np.float32(1.0) / np.power(np.float32(10000.0), np.arange(HALF, dtype=np.float32) / np.float32(HALF)).astype(np.float32)).astype(np.float32)
    ang = np.arange(SEQ, dtype=np.float32)[:, None] * inv[None, :]
    return np.concatenate([np.cos(ang), np.sin(ang)], axis=1).astype(np.float32)


class Steps:

    def __init__(self, eng, sem):
        self.eng, self.sem, self.base, self.n = eng, sem, 0, 0

    def did(self, ins):
        ins.then_inc(self.sem, 1)
        self.n += 1

    def sync(self):
        self.eng.wait_ge(self.sem, self.base + self.n)

    def link(self, ins):
        self.did(ins)
        self.sync()

    def fence(self):
        self.eng.sem_inc(self.sem, 1)
        self.n += 1


def wait(eng, sem, value):
    if not isinstance(value, int) or value > 0:
        eng.wait_ge(sem, value)


class Scope:

    def __init__(self, ctx, nc, tag):
        self.ctx, self.nc, self.tag = ctx, nc, tag

    def sb(self, name, shape, dt=F32):
        return self.ctx.enter_context(self.nc.sbuf_tensor(f"{self.tag}_{name}", shape, dt))

    def ps(self, name, shape=(P, 512), dt=F32):
        return self.ctx.enter_context(self.nc.psum_tensor(f"{self.tag}_{name}", list(shape), dt))

    def sem(self, name):
        return self.ctx.enter_context(self.nc.semaphore(f"{self.tag}_{name}"))


def features_phase(nc, io, feat_dram, xd_dram, yd_dram):
    with ExitStack() as ctx:
        s = Scope(ctx, nc, "feat")
        ids = s.sb("ids", [P, SEQ], I32)
        msk = s.sb("msk", [P, SEQ], I32)
        cst = s.sb("cst", [P, C_END])
        mpad = s.sb("mpad", [P, SEQ + 2])
        opad = s.sb("opad", [P, SEQ + 2])
        one = s.sb("one", [P, SEQ])
        rlen = s.sb("rlen", [P, SEQ])
        ZT = 8
        zero = s.sb("zero", [P, ZT * D])
        loaded, stored, cleared, filled = s.sem("loaded"), s.sem("stored"), s.sem("cleared"), s.sem("filled")
        padded, one_done, win_done, steps = s.sem("padded"), s.sem("one_done"), s.sem("win_done"), s.sem("steps")
        block = ctx.enter_context(nc.Block())

        @block.sync
        def _(sp):
            sp.dma_start(cst[:], io["consts"]).then_inc(loaded, 16)
            for b in range(BATCH):
                sp.dma_start(ids[32 * b:32 * b + 32, :], io["x"][b:b + 1, :].broadcast_to([32, SEQ])).then_inc(loaded, 16)
                sp.dma_start(msk[32 * b:32 * b + 32, :], io["mask"][b:b + 1, :].broadcast_to([32, SEQ])).then_inc(loaded, 16)
            sp.wait_ge(one_done, 1)
            for b in range(BATCH):
                sp.dma_start(feat_dram[0:32, b * SEQ:(b + 1) * SEQ], one[32 * b:32 * b + 32, :]).then_inc(stored, 16)
            sp.wait_ge(win_done, 1)
            for b in range(BATCH):
                sp.dma_start(feat_dram[32:64, b * SEQ:(b + 1) * SEQ], rlen[32 * b:32 * b + 32, :]).then_inc(stored, 16)
            sp.wait_ge(stored, 16 * 2 * BATCH)

        @block.scalar
        def _(act):
            act.wait_ge(cleared, 1)
            n = N_SLOT // P // ZT
            for k in range(n):
                act.dma_start(xd_dram[k * P * ZT:(k + 1) * P * ZT, :].rearrange("(p a) d -> p (a d)", a=ZT), zero[:]).then_inc(filled, 16)
            act.dma_start(yd_dram[N_SLOT:N_SLOT + 1, :], zero[0:1, 0:D]).then_inc(filled, 16)
            act.wait_ge(filled, 16 * (n + 1))

        @block.vector
        def _(dve):
            st = Steps(dve, steps)
            dve.memset(zero[:], 0.0).then_inc(cleared, 1)
            st.did(dve.memset(mpad[:], 0.0))
            st.did(dve.memset(opad[:], 0.0))
            dve.wait_ge(loaded, 16 * (1 + 2 * BATCH))
            st.sync()
            row, isb = cst[:, C_ROW:C_ROW + 1], cst[:, C_ISB:C_ISB + 1]
            st.did(dve.tensor_copy(mpad[:, 1:SEQ + 1], msk[:]))
            st.link(dve.tensor_scalar(one[:], ids[:], row, None, ALU.is_equal))
            st.link(dve.tensor_tensor(opad[:, 1:SEQ + 1], one[:], mpad[:, 1:SEQ + 1], ALU.mult))
            dve.tensor_scalar(one[:], one[:], isb, None, ALU.max).then_inc(one_done, 1)
            st.link(dve.tensor_tensor(rlen[:], mpad[:, 0:SEQ], mpad[:, 1:SEQ + 1], ALU.add))
            st.link(dve.tensor_tensor(rlen[:], rlen[:], mpad[:, 2:SEQ + 2], ALU.add))
            st.link(dve.tensor_scalar(rlen[:], rlen[:], 1.0, None, ALU.max))
            st.link(dve.reciprocal(rlen[:], rlen[:]))
            st.link(dve.tensor_tensor(mpad[:, 0:SEQ], opad[:, 0:SEQ], opad[:, 1:SEQ + 1], ALU.add))
            st.link(dve.tensor_tensor(mpad[:, 0:SEQ], mpad[:, 0:SEQ], opad[:, 2:SEQ + 2], ALU.add))
            st.link(dve.tensor_tensor(rlen[:], rlen[:], mpad[:, 0:SEQ], ALU.mult))
            dve.tensor_scalar(rlen[:], rlen[:], isb, None, ALU.add).then_inc(win_done, 1)


def split_weights(st, raw, scaled, hi, lo, scale):
    if scale is not None:
        st.link(st.eng.tensor_scalar(scaled, raw, scale, None, ALU.mult))
    else:
        scaled = raw
    st.link(st.eng.tensor_copy(hi, scaled))
    st.did(st.eng.tensor_tensor(lo, scaled, hi.bitcast(F32), ALU.subtract))


def split_product(pe, out, parts, first=True, last=True):
    mm = None
    n = 3 * len(parts)
    i = 0
    for lhs_hi, lhs_lo, rhs_hi, rhs_lo in parts:
        for lhs, rhs in ((lhs_hi, rhs_hi), (lhs_hi, rhs_lo), (lhs_lo, rhs_hi)):
            mm = pe.matmul(out, lhs, rhs, start=first and i == 0, stop=last and i == n - 1)
            i += 1
    return mm


def attention_phase(nc, io, feat_dram, xd_dram, res, gates, rows, debug=None):
    with ExitStack() as ctx:
        s = Scope(ctx, nc, "att")
        sb, ps, sem = s.sb, s.ps, s.sem
        cst = sb("cst", [P, C_END])
        rope = sb("rope", [P, NT, 2 * HALF])
        raw = sb("raw", [P, DH, 4 * D])
        w_hi = sb("w_hi", [P, DH, 4 * D], F32R)
        w_lo = sb("w_lo", [P, DH, 4 * D], F32R)
        raw_o = sb("raw_o", [P, DH, D])
        wo_hi = sb("wo_hi", [P, DH, D], F32R)
        wo_lo = sb("wo_lo", [P, DH, D], F32R)
        sc1 = sb("sc1", [P, DH])
        sc2 = sb("sc2", [P, DH])
        raw_r = sb("raw_r", [P, DH, N_EXP])
        w_r = sb("w_r", [P, DH, N_EXP])
        rb = sb("rb", [P, N_EXP])
        bias = sb("bias", [P, 5 * D])
        bias_hl = sb("bias_hl", [P, 5 * D], F32R)
        ones_f = sb("ones_f", [P, P])
        ones_r = sb("ones_r", [P, P], F32R)
        ones_b = sb("ones_b", [P, P], BF16)
        tri_b = sb("tri_b", [P, P], BF16)
        gain = sb("gain", [P, D])
        shift = sb("shift", [P, D])
        emb = sb("emb", [32, D])
        embT = sb("embT", [P, DH, 32])
        pcaT = sb("pcaT", [N_PCA, VOCAB])
        pjw = sb("pjw", [N_PCA, D])
        contT = sb("contT", [P, DH, 32])
        fus = sb("fus", [P, 2 * DH, D])
        mtab = sb("mtab", [64, D])
        half = sb("half", [P, 1])
        inv_d = sb("inv_d", [P, 1])
        xln = sb("xln", [P, 4, D])
        feat = sb("feat", [64, 2, P])
        n1 = sb("n1", [P, 2, D])
        n1g = sb("n1g", [P, D])
        st1, st2 = sb("st1", [P, 6]), sb("st2", [P, 6])
        mv1, mv2 = sb("mv1", [P, 2, 2]), sb("mv2", [P, 2, 2])
        ve1, ve2, ms1, ms2 = (sb(n, [P, 2]) for n in ("ve1", "ve2", "ms1", "ms2"))
        rs1, rs2, rr1, rr2 = (sb(n, [P, 2]) for n in ("rs1", "rs2", "rr1", "rr2"))
        ssq1, ssq2 = sb("ssq1", [P, 2]), sb("ssq2", [P, 2])
        junk = sb("junk", [P, D])
        xa = sb("xa", [P, 2, D])
        xaT_hi = sb("xaT_hi", [P, DH, P], F32R)
        xaT_lo = sb("xaT_lo", [P, DH, P], F32R)
        ra, rb_, rp, mn = (sb(n, [P, 2 * D]) for n in ("ra", "rb2", "rp", "mn"))
        ex = sb("ex", [P, 2 * D])
        ph = sb("ph", [P, 2, 2 * D])
        v1 = sb("v1", [P, 2, DH, P + 1])
        th = sb("th", [P, 2, D])
        bd = sb("bd", [P, 2, DH, BDW])
        qT = sb("qT", [P, DH, P])
        dn, rdn = sb("dn", [P, DH, HPH]), sb("rdn", [P, DH, HPH])
        avg = sb("avg", [P, D])
        att = sb("att", [P, 2, D])
        atT_hi = sb("atT_hi", [P, DH, P], F32R)
        atT_lo = sb("atT_lo", [P, DH, P], F32R)
        x1 = sb("x1", [P, 2, D])
        xr = sb("xr", [P, 4, D])
        xrT = sb("xrT", [P, 2, DH, P])
        lg, ex_r, prob, eq, prob2, rank, place = (sb(n, [P, 2, N_EXP]) for n in ("lg", "ex_r", "prob", "eq", "prob2", "rank", "place"))
        pick = sb("pick", [P, TOP, 2, N_EXP])
        picked = sb("picked", [P, 2, N_EXP], BF16)
        sel = sb("sel", [P, TOP, 2, N_EXP])
        mx, sm, rsm, kx = (sb(n, [P, 2]) for n in ("mx", "sm", "rsm", "kx"))
        top = sb("top", [P, TOP, 2])
        tsum = sb("tsum", [P, 2])
        trec = sb("trec", [P, 2])
        rowf = sb("rowf", [P, TOP, 2])
        okf = sb("okf", [P, TOP, 2])
        gt = sb("gt", [P, TOP, 2])
        carry = sb("carry", [P, N_EXP])
        srow = sb("srow", [P, 2, TOP, 2], U32)
        p_tok, p_xt, p_qk, p_vg, p_kv, p_num, p_tr, p_wo = (ps(n) for n in ("tok", "xt", "qk", "vg", "kv", "num", "tr", "wo"))

        loaded, loaded2, setup = sem("loaded"), sem("loaded2"), sem("setup")
        su_pe, su_dve, su_fix = sem("su_pe"), sem("su_dve"), sem("su_fix")
        zeroed = sem("zeroed")
        names = ("tok var1 rstd1 norm1 h var2 rstd2 xln ssq1 rr1 xa xaT xaT_hi xaT_lo qk vg mn ex ph vth kv bd tq qT num "
                 "att atT atT_hi atT_lo wo x1 ssq2 rr2 xr xrT_ps xrT logit lread ex_r picked rank_ps rread rows steps psteps fence radd rope_read").split()
        S = {n: sem(n) for n in names}
        feat_in = [sem(f"feat_in{k}") for k in range(2)]
        scattered = [sem(f"scattered{k}") for k in range(4)]
        block = ctx.enter_context(nc.Block())
        ident = cst[:, C_ID:C_ID + P]
        N_LOAD = 16

        def supersteps(eng, step, st=None, per_quad=0, before_batch=None):
            if before_batch is not None:
                before_batch(0)
            for i in range(0, 11):
                step(i, i % 4)

            def run(q, at, base):
                if st is not None:
                    st.base, st.n = base, 0
                for u in range(4):
                    step(at + u, (3 + u) % 4)
                if st is not None:
                    assert st.n == per_quad, (st.n, per_quad)

            def start():
                return 0 if st is None else st.base + st.n

            def settle(value):
                if st is not None:
                    st.base, st.n = value, 0

            s0 = start()
            with eng.Fori(0, 2) as q:
                run(q, q * 4 + 11, q * per_quad + s0)
            settle(s0 + 2 * per_quad)
            s0 = start()
            extra = 0 if st is None or before_batch is None else before_batch.counted
            with eng.Fori(0, 2) as b:
                if before_batch is not None:
                    settle(b * (4 * per_quad + extra) + s0)
                    before_batch(b + 1)
                with eng.Fori(0, 4) as q:
                    run(q, b * 16 + q * 4 + 19, b * (4 * per_quad + extra) + q * per_quad + (s0 + extra))
            settle(s0 + 2 * (4 * per_quad + extra))
            if before_batch is not None:
                before_batch(3)
            s0 = start()
            with eng.Fori(0, 3) as q:
                run(q, q * 4 + 51, q * per_quad + s0)
            settle(s0 + 3 * per_quad)
            for i in range(63, NT + 8):
                step(i, i % 4)

        def has(t):
            return not isinstance(t, int) or 0 <= t < NT

        def pairs(e):
            return (e + 1) // 2

        def rpairs(a):
            return (a - 6) // 2

        def pairs_before(e, u):
            odd = (u - 5) % 2
            return (e - odd) // 2

        @block.sync
        def _(sp):
            def ld(dst, src, to=loaded, strided=False):
                sp.dma_start(dst, src, allow_slow_non_contiguous=strided).then_inc(to, 16)
            ld(cst[:], io["consts"])
            ld(pcaT[:], io["pca"].rearrange("v f -> f v"), strided=True)
            ld(pjw[:], io["proj_w"])
            ld(fus[:], io["fus_w"].rearrange("(k p) n -> p k n", p=P))
            ld(sc1[:], io["norm1"].rearrange("(k p) -> p k", p=P), strided=True)
            ld(sc2[:], io["norm2"].rearrange("(k p) -> p k", p=P), strided=True)
            for n, w in enumerate(("Wq", "Wk", "Wv", "Wg")):
                ld(raw[:, :, n * D:(n + 1) * D], io[w].rearrange("(k p) n -> p k n", p=P))
            ld(raw_o[:], io["Wo"].rearrange("(k p) n -> p k n", p=P))
            ld(raw_r[:], io["router_W"].rearrange("(k p) n -> p k n", p=P))
            for n, w in enumerate(("bq", "bk", "bv", "bg", "bo")):
                for r in (0, 32):
                    ld(bias[r:r + 1, n * D:(n + 1) * D], io[w].rearrange("(a n) -> a n", a=1))
            for dst, w in ((gain, "ln_g"), (shift, "ln_b")):
                ld(dst[:], io[w].rearrange("(a n) -> a n", a=1).broadcast_to([P, D]))
            ld(rb[:], io["router_b"].rearrange("(a n) -> a n", a=1).broadcast_to([P, N_EXP]))
            for b in range(BATCH):
                ld(rope[:, b * TPB:(b + 1) * TPB, :], io["rope"].rearrange("(t p) c -> p t c", p=P))
            sp.wait_ge(su_fix, 1)
            ld(emb[0:VOCAB, :], io["emb"])
            sp.wait_ge(su_fix, 2)
            ld(contT[:, :, VOCAB], io["proj_b"].rearrange("(k p) -> p k", p=P), loaded2, True)
            sp.wait_ge(su_fix, 3)
            ld(mtab[VOCAB:VOCAB + 1, :], io["fus_b"].rearrange("(a n) -> a n", a=1), loaded2)

            def step(i, u):
                if has(i):
                    if not isinstance(i, int) or i >= 2:
                        sp.wait_ge(S["tok"], i - 1)
                    sp.dma_start(feat[:, u % 2, :], feat_dram[:, bass.ds(i * P, P)]).then_inc(feat_in[u % 2], 16)
            supersteps(sp, step)

        N_LOADED = 16 * (7 + 4 + 2 + 10 + 3 + 4)

        @block.tensor
        def _(pe):
            pe.wait_ge(loaded, N_LOADED)
            pe.wait_ge(su_dve, 1)
            for k in range(DH):
                mm = pe.transpose(p_tr[:, 32 * k:32 * k + 32], emb[:, k * P:(k + 1) * P], ident[0:32, 0:32])
            mm.then_inc(su_pe, 1)
            for k in range(DH):
                mm = pe.matmul(p_num[:, 32 * k:32 * k + VOCAB], pjw[:, k * P:(k + 1) * P], pcaT[:], start=True, stop=True)
            mm.then_inc(su_pe, 1)
            pe.wait_ge(su_dve, 2)
            pe.wait_ge(loaded2, 16)
            for k in range(DH):
                mm = pe.matmul(p_wo[0:32, 0:D], embT[:, k, :], fus[:, k, :], start=k == 0, stop=k == DH - 1)
            mm.then_inc(su_pe, 1)
            for k in range(DH):
                mm = pe.matmul(p_xt[0:32, 0:D], contT[:, k, :], fus[:, DH + k, :], start=k == 0, stop=k == DH - 1)
            mm.then_inc(su_pe, 1)
            pe.wait_ge(setup, 1)
            pe.wait_ge(loaded2, 32)

            def kv(t, u, ch):
                pp = u % 2
                if ch == 0:
                    pe.wait_ge(S["ph"], t + 1)
                    pe.wait_ge(S["vth"], t + 1)
                pe.wait_ge(zeroed, 1) if isinstance(t, int) and t == 0 else None
                wait(pe, S["bd"], 2 * t + ch)
                a = CHUNK * ch
                for h in range(DH):
                    mm = pe.matmul(p_kv[:, h * (P + 1):(h + 1) * (P + 1)],
                                   ph[a:a + CHUNK, pp, D + h * P:D + (h + 1) * P], v1[a:a + CHUNK, pp, h, :],
                                   start=False, stop=True, skip_group_check=True)
                mm.then_inc(S["kv"], 1)

            def step(i, u):
                a, b, c, d, e = i, i - 2, i - 3, i - 4, i - 5
                if has(c):
                    kv(c, (u - 3) % 4, 0)
                if has(b):
                    pe.wait_ge(S["xa"], b + 1)
                    wait(pe, S["xaT_lo"], b)
                    wait(pe, S["xrT"], b - 3)
                    for k in range(DH):
                        mm = pe.transpose(p_xt[:, k * P:(k + 1) * P], xa[:, (u - 2) % 2, k * P:(k + 1) * P], ident)
                    mm.then_inc(S["xaT"], 1)
                if has(d):
                    pe.wait_ge(S["att"], d + 1)
                    pe.wait_ge(S["qT"], d + 1)
                    for k in range(DH):
                        mm = pe.transpose(p_tr[:, k * P:(k + 1) * P], att[:, u % 2, k * P:(k + 1) * P], ident)
                    mm.then_inc(S["atT"], 1)
                if has(c):
                    cp = (u - 3) % 2
                    wait(pe, S["atT_lo"], c)
                    for k in range(DH):
                        mm = pe.transpose(p_tr[:, k * P:(k + 1) * P], ph[:, cp, k * P:(k + 1) * P], ident)
                    mm.then_inc(S["tq"], 1)
                    kv(c, (u - 3) % 4, 1)
                def project(q, bank, done):
                    c0 = q * 2 * D
                    pe.matmul(bank[:], ones_r[:], bias_hl[:, c0:c0 + 2 * D], start=True, stop=False)
                    split_product(pe, bank[:], [(xaT_hi[:, k, :], xaT_lo[:, k, :], w_hi[:, k, c0:c0 + 2 * D],
                                                 w_lo[:, k, c0:c0 + 2 * D]) for k in range(DH)],
                                  first=False).then_inc(S[done], 1)
                if has(b):
                    pe.wait_ge(S["xaT_lo"], b + 1)
                    pe.wait_ge(S["xaT_hi"], b + 1)
                    wait(pe, S["rope_read"], b)
                    project(0, p_qk, "qk")
                if has(c):
                    pe.wait_ge(S["qT"], c + 1)
                    pe.wait_ge(S["bd"], 2 * c + 2)
                    wait(pe, S["att"], c)
                    for ch in range(2):
                        for h in range(DH):
                            mm = pe.matmul(p_num[CHUNK * ch:CHUNK * ch + CHUNK, h * BDW:(h + 1) * BDW],
                                           qT[:, h, CHUNK * ch:CHUNK * ch + CHUNK], bd[:, ch, h, :], start=True, stop=True,
                                           skip_group_check=True)
                    mm.then_inc(S["num"], 1)
                if has(e - 1) and u % 2 == 1:
                    pe.wait_ge(S["picked"], pairs(e - 1))
                    wait(pe, S["norm1"], a if not isinstance(a, int) else min(a, NT))
                    o = D + 2 * N_EXP
                    pe.matmul(p_tok[:, o:o + 2 * N_EXP], tri_b[:], picked[:].rearrange("p a b -> p (a b)"), start=True, stop=True)
                    pe.matmul(p_tok[:, o + 2 * N_EXP:o + 4 * N_EXP], ones_b[:], picked[:].rearrange("p a b -> p (a b)"),
                              start=True, stop=True).then_inc(S["rank_ps"], 1)
                if has(a):
                    pe.wait_ge(feat_in[u % 2], (a - u % 2) * 8 + 16)
                    wait(pe, S["norm1"], a)
                    if u % 2 == 0:
                        wait(pe, S["rread"], rpairs(a))
                    pe.matmul(p_tok[:, 0:D], feat[:, u % 2, :], mtab[:], start=True, stop=True).then_inc(S["tok"], 1)
                if has(e):
                    pe.wait_ge(S["xr"], e + 1)
                    wait(pe, S["xaT_lo"], e + 4 if not isinstance(e, int) else min(e + 4, NT))
                    wait(pe, S["xrT"], e)
                    for k in range(DH):
                        mm = pe.transpose(p_xt[:, k * P:(k + 1) * P], xr[:, (u - 5) % 4, k * P:(k + 1) * P], ident)
                    mm.then_inc(S["xrT_ps"], 1)
                if has(b):
                    wait(pe, S["vth"], b)
                    project(1, p_vg, "vg")
                if has(d):
                    pe.wait_ge(S["atT_lo"], d + 1)
                    wait(pe, S["x1"], d)
                    pe.matmul(p_wo[:, 0:D], ones_r[:], bias_hl[:, 4 * D:5 * D], start=True, stop=False)
                    split_product(pe, p_wo[:, 0:D], [(atT_hi[:, k, :], atT_lo[:, k, :], wo_hi[:, k, :], wo_lo[:, k, :])
                                                     for k in range(DH)], first=False).then_inc(S["wo"], 1)
                if has(e) and u % 2 == 0:
                    wait(pe, S["rread"], rpairs(a))
                    pe.wait_ge(S["xrT"], e + 1)
                    wait(pe, S["norm1"], a + 1 if not isinstance(a, int) else min(a + 1, NT))
                    for v in range(2):
                        for k in range(DH):
                            mm = pe.matmul(p_tok[:, D + v * N_EXP:D + (v + 1) * N_EXP], xrT[:, v, k, :], w_r[:, k, :],
                                           start=k == 0, stop=k == DH - 1)
                    mm.then_inc(S["logit"], 1)
            def before(b):
                if isinstance(b, int) and b == 0:
                    return
                pe.wait_ge(zeroed, b + 1)
                pe.sem_inc(S["fence"], 1)
            before.counted = 0
            supersteps(pe, step, before_batch=before)

        @block.scalar
        def _(act):
            act.wait_ge(setup, 1)

            def step(i, u):
                a1, b, c, d, e = i - 1, i - 2, i - 3, i - 4, i - 5
                if has(b):
                    pp = (u - 2) % 2
                    act.wait_ge(S["xaT"], b + 1)
                    wait(act, S["vg"], b)
                    act.copy(xaT_hi[:].rearrange("p k n -> p (k n)"), p_xt[:, 0:D]).then_inc(S["xaT_hi"], 1)
                if has(d):
                    act.wait_ge(S["atT"], d + 1)
                    wait(act, S["wo"], d)
                    act.copy(atT_hi[:].rearrange("p k n -> p (k n)"), p_tr[:, 0:D]).then_inc(S["atT_hi"], 1)
                if has(c):
                    act.wait_ge(S["tq"], c + 1)
                    wait(act, S["num"], c)
                    act.copy(qT[:].rearrange("p k n -> p (k n)"), p_tr[:, 0:D]).then_inc(S["qT"], 1)
                if has(e):
                    ep, slot = (u - 5) % 2, (u - 5) % 4
                    act.wait_ge(S["rr2"], e + 1)
                    wait(act, scattered[slot], (e - slot) * 8)
                    act.activation(xr[:, slot, :], x1[:, ep, :], ACT.Copy, scale=rr2[:, ep:ep + 1]).then_inc(S["xr"], 1)
                if has(e - 1) and u % 2 == 1:
                    act.wait_ge(S["lread"], pairs(e - 1))
                    act.activation(ex_r[:], lg[:], ACT.Exp).then_inc(S["ex_r"], 1)
                if has(a1):
                    pp = (u - 1) % 2
                    act.wait_ge(S["xln"], a1 + 1)
                    act.activation(junk[:], xln[:, (u - 1) % 4, :], ACT.Square, accum_out=ssq1[:, pp:pp + 1]).then_inc(S["ssq1"], 1)
                if has(a1):
                    pp = (u - 1) % 2
                    act.wait_ge(S["rr1"], a1 + 1)
                    wait(act, S["xaT"], a1 - 1)
                    act.activation(xa[:, pp, :], xln[:, (u - 1) % 4, :], ACT.Copy, scale=rr1[:, pp:pp + 1]).then_inc(S["xa"], 1)
                if has(e):
                    act.wait_ge(S["xrT_ps"], e + 1)
                    if not isinstance(e, int) or e >= 2:
                        act.wait_ge(S["logit"], pairs_before(e, u))
                    act.copy(xrT[:, (u - 5) % 2, :, :].rearrange("p k n -> p (k n)"), p_xt[:, 0:D]).then_inc(S["xrT"], 1)
                if has(b):
                    pp = (u - 2) % 2
                    act.wait_ge(S["mn"], b + 1)
                    wait(act, S["ph"], b)
                    act.activation(ex[:], mn[:], ACT.Exp).then_inc(S["ex"], 1)
                    act.wait_ge(S["vg"], b + 1)
                    wait(act, S["kv"], 2 * (b - 1))
                    wait(act, S["att"], b - 1)
                    act.copy(v1[:, pp, :, 0:P], p_vg[:, 0:D].rearrange("p (k n) -> p k n", k=DH))
                    act.activation(th[:, pp, :], p_vg[:, D:2 * D], ACT.Tanh, scale=0.5).then_inc(S["vth"], 1)
                if has(d):
                    pp = u % 2
                    act.wait_ge(S["x1"], d + 1)
                    act.activation(junk[:], x1[:, pp, :], ACT.Square, accum_out=ssq2[:, pp:pp + 1]).then_inc(S["ssq2"], 1)
            supersteps(act, step)

        @block.gpsimd
        def _(pool):
            pst = Steps(pool, S["psteps"])
            pool.wait_ge(setup, 1)

            def rsqrt(out, src):
                return pool.tensor_tensor(out, src, half[:], ALU.pow)

            def step(i, u):
                a, a1, d, e = i, i - 1, i - 4, i - 5
                if has(a1):
                    pp = (u - 1) % 2
                    pool.wait_ge(S["var2"], a1 + 1)
                    rsqrt(rs2[:, pp:pp + 1], ve2[:, pp:pp + 1]).then_inc(S["rstd2"], 1)
                if has(a1):
                    pp = (u - 1) % 2
                    pool.wait_ge(S["ssq1"], a1 + 1)
                    pst.link(pool.tensor_tensor(ms1[:, pp:pp + 1], ssq1[:, pp:pp + 1], inv_d[:], ALU.mult))
                    rsqrt(rr1[:, pp:pp + 1], ms1[:, pp:pp + 1]).then_inc(S["rr1"], 1)
                if has(a):
                    pp = u % 2
                    pool.wait_ge(S["var1"], a + 1)
                    rsqrt(rs1[:, pp:pp + 1], ve1[:, pp:pp + 1]).then_inc(S["rstd1"], 1)
                if has(e - 2 - u % 2):
                    v = u % 2
                    if v == 0:
                        pool.wait_ge(S["rows"], pairs(e - 2))
                        pst.fence()
                    slot = (u - 8) % 4
                    for k in range(TOP):
                        pool.indirect_dma_start(xd_dram, bass.IndirectOffsetOnAxis(ap=srow[:, slot // 2, k, v:v + 1], axis=0),
                                                xr[:, slot, :], None, bounds_check=N_SLOT - 1,
                                                oob_is_err=False).then_inc(scattered[slot], 16)
                if has(a):
                    pp = u % 2
                    pool.wait_ge(S["norm1"], a + 1)
                    pst.link(pool.tensor_tensor(n1g[:], n1[:, pp, :], gain[:], ALU.mult))
                    pool.tensor_tensor(res[:, bass.ds(a, 1), :].rearrange("p a d -> p (a d)"), n1g[:], shift[:], ALU.add).then_inc(S["h"], 1)
                if has(d):
                    pp = u % 2
                    pool.wait_ge(S["ssq2"], d + 1)
                    pst.link(pool.tensor_tensor(ms2[:, pp:pp + 1], ssq2[:, pp:pp + 1], inv_d[:], ALU.mult))
                    rsqrt(rr2[:, pp:pp + 1], ms2[:, pp:pp + 1]).then_inc(S["rr2"], 1)
                    r = res[:, bass.ds(d, 1), :].rearrange("p a d -> p (a d)")
                    pool.tensor_tensor(r, r, x1[:, pp, :], ALU.add).then_inc(S["radd"], 1)
            supersteps(pool, step, pst, per_quad=14)
            for k in range(4):
                pool.wait_ge(scattered[k], 32 * (NT // 4))

        @block.vector
        def _(dve):
            st = Steps(dve, S["steps"])
            for t, v in ((emb, 0.0), (contT, 0.0), (mtab, 0.0), (ones_f, 1.0), (v1, 1.0), (half, -0.5), (inv_d, 1.0 / D),
                         (carry, 0.0), (p_kv, 0.0)):
                st.did(dve.memset(t[:], v))
            st.sync()
            dve.engine_nop().then_inc(su_fix, 1)
            dve.tensor_copy(ones_r[:], ones_f[:]).then_inc(zeroed, 1)
            dve.wait_ge(loaded, N_LOADED)
            st.link(dve.memset(bias_hl[:].bitcast(F32), 0.0))
            st.did(dve.tensor_copy(bias_hl[0:1, :], bias[0:1, :]))
            st.did(dve.tensor_copy(ones_b[:], ones_f[:]))
            st.did(dve.tensor_copy(tri_b[:], cst[:, C_TRI:C_TRI + P]))
            split_weights(st, raw_o[:], None, wo_hi[:], wo_lo[:], None)
            st.sync()
            st.eng = dve
            for k in range(DH):
                st.did(dve.tensor_scalar(w_r[:, k, :], raw_r[:, k, :], sc2[:, k:k + 1], None, ALU.mult))
            st.link(dve.tensor_copy(bias_hl[32:33, :], bias[32:33, :]))
            st.link(dve.tensor_tensor(bias[32:33, :], bias[32:33, :], bias_hl[32:33, :].bitcast(F32), ALU.subtract))
            st.link(dve.tensor_copy(bias_hl[32:33, :], bias[32:33, :]))
            for k in range(DH):
                split_weights(st, raw[:, k, :], raw[:, k, :], w_hi[:, k, :], w_lo[:, k, :], sc1[:, k:k + 1])
            st.sync()
            dve.engine_nop().then_inc(su_dve, 1)
            dve.wait_ge(su_pe, 2)
            st.did(dve.tensor_copy(embT[:].rearrange("p k v -> p (k v)"), p_tr[:, 0:64]))
            st.link(dve.tensor_copy(contT[:, :, 0:VOCAB], p_num[:, 0:64].rearrange("p (k v) -> p k v", k=DH)[:, :, 0:VOCAB]))
            dve.engine_nop().then_inc(su_fix, 1)
            dve.engine_nop().then_inc(su_dve, 1)
            dve.wait_ge(su_pe, 4)
            st.did(dve.tensor_copy(mtab[0:32, :], p_wo[0:32, 0:D]))
            st.link(dve.tensor_copy(mtab[32:64, :], p_xt[0:32, 0:D]))
            dve.engine_nop().then_inc(su_fix, 1)
            dve.engine_nop().then_inc(setup, 1)

            def step(i, u):
                a, a1, b, c, d, e = i, i - 1, i - 2, i - 3, i - 4, i - 5

                def masked_state(ch):
                    dve.wait_ge(S["kv"], 2 * c + 1 + ch)
                    if ch == 0:
                        wait(dve, S["num"], c)
                    v = p_kv[:, 0:DH * (P + 1)].rearrange("p (h n) -> p h n", h=DH)
                    m = cst[:, C_BD:C_BD + BDW].rearrange("p (a n) -> p a n", a=1)
                    dve.tensor_tensor(bd[:, ch, :, 0:P], v[:, :, 0:P], m[:, :, 0:P].broadcast_to([P, DH, P]), ALU.mult)
                    dve.tensor_tensor(bd[:, ch, :, P:BDW], v[:, :, P:P + 1].broadcast_to([P, DH, HPH]),
                                      m[:, :, P:BDW].broadcast_to([P, DH, HPH]), ALU.mult).then_inc(S["bd"], 1)

                def statistics(src, stt, mv, ve, pp, done):
                    st.fence()
                    st.link(dve.bn_stats(stt[:], src))
                    st.fence()
                    st.link(dve.bn_aggr(mv[:, pp, :], stt[:]))
                    dve.tensor_scalar(ve[:, pp:pp + 1], mv[:, pp, 1:2], EPS, None, ALU.add).then_inc(S[done], 1)

                if has(c):
                    masked_state(0)
                if has(b):
                    dve.wait_ge(S["xaT_hi"], b + 1)
                    dve.tensor_tensor(xaT_lo[:].rearrange("p k n -> p (k n)"), p_xt[:, 0:D],
                                      xaT_hi[:].bitcast(F32).rearrange("p k n -> p (k n)"), ALU.subtract).then_inc(S["xaT_lo"], 1)
                if has(d):
                    dve.wait_ge(S["atT_hi"], d + 1)
                    dve.tensor_tensor(atT_lo[:].rearrange("p k n -> p (k n)"), p_tr[:, 0:D],
                                      atT_hi[:].bitcast(F32).rearrange("p k n -> p (k n)"), ALU.subtract).then_inc(S["atT_lo"], 1)
                if has(a1):
                    dve.wait_ge(S["h"], a1 + 1)
                    statistics(res[:, bass.ds(a1, 1), :].rearrange("p a d -> p (a d)"), st2, mv2, ve2, (u - 1) % 2, "var2")
                if has(c):
                    masked_state(1)
                if has(e - 1) and u % 2 == 1:
                    route_choice(e - 1)
                if has(e - 2) and u % 2 == 0:
                    route_rows(e - 2, u - 2)
                if has(a1):
                    pp = (u - 1) % 2
                    dve.wait_ge(S["rstd2"], a1 + 1)
                    dve.tensor_scalar(xln[:, (u - 1) % 4, :], res[:, bass.ds(a1, 1), :].rearrange("p a d -> p (a d)"), mv2[:, pp, 0:1], rs2[:, pp:pp + 1],
                                      ALU.subtract, ALU.mult).then_inc(S["xln"], 1)
                if has(b):
                    pp = (u - 2) % 2
                    dve.wait_ge(S["qk"], b + 1)
                    tab = rope[:, bass.ds(b, 1), :]
                    cos, sin = tab[:, :, 0:HALF], tab[:, :, HALF:2 * HALF]
                    src = p_qk[:].rearrange("p (g h i) -> p g h i", h=2, i=HALF)
                    dst = rb_[:].rearrange("p (g h i) -> p g h i", h=2, i=HALF)
                    G = 2 * HEADS
                    st.did(dve.tensor_tensor(ra[:].rearrange("p (g i) -> p g i", i=HALF), p_qk[:].rearrange("p (g i) -> p g i", i=HALF),
                                             cos.broadcast_to([P, 2 * G, HALF]), ALU.mult))
                    st.did(dve.tensor_tensor(dst[:, :, 0, :], src[:, :, 1, :], sin.broadcast_to([P, G, HALF]), ALU.mult))
                    dve.tensor_tensor(dst[:, :, 1, :], src[:, :, 0, :], sin.broadcast_to([P, G, HALF]), ALU.mult).then_inc(S["rope_read"], 1)
                    st.sync()
                    dve.wait_ge(S["rope_read"], b + 1)
                    av = ra[:].rearrange("p (g h i) -> p g h i", h=2, i=HALF)
                    ov = rp[:].rearrange("p (g h i) -> p g h i", h=2, i=HALF)
                    st.did(dve.tensor_tensor(ov[:, :, 0, :], av[:, :, 0, :], dst[:, :, 0, :], ALU.subtract))
                    st.link(dve.tensor_tensor(ov[:, :, 1, :], av[:, :, 1, :], dst[:, :, 1, :], ALU.add))
                    wait(dve, S["ex"], b)
                    dve.tensor_scalar(mn[:], rp[:], 0.0, None, ALU.min).then_inc(S["mn"], 1)
                if has(a):
                    dve.wait_ge(S["tok"], a + 1)
                    statistics(p_tok[:, 0:D], st1, mv1, ve1, u % 2, "var1")
                if has(c):
                    cp = (u - 3) % 2
                    dve.wait_ge(S["num"], c + 1)
                    nv = p_num[:, 0:DH * BDW].rearrange("p (h n) -> p h n", h=DH)
                    st.link(dve.tensor_scalar(dn[:], nv[:, :, P:BDW], 2.0, 2e-6, ALU.mult, ALU.add))
                    st.link(dve.reciprocal(rdn[:], dn[:]))
                    for h in range(DH):
                        st.did(dve.tensor_tensor(avg[:, h * P:(h + 1) * P].rearrange("p (g i) -> p g i", i=DK),
                                                 nv[:, h, 0:P].rearrange("p (g i) -> p g i", i=DK),
                                                 rdn[:, h, :].rearrange("p (g a) -> p g a", a=1).broadcast_to([P, HPH, DK]), ALU.mult))
                    st.sync()
                    wait(dve, S["atT"], c - 1)
                    dve.scalar_tensor_tensor(att[:, cp, :], th[:, cp, :], 1.0, avg[:], ALU.add, ALU.mult).then_inc(S["att"], 1)
                if has(a):
                    pp = u % 2
                    dve.wait_ge(S["rstd1"], a + 1)
                    wait(dve, S["h"], a - 1)
                    dve.tensor_scalar(n1[:, pp, :], p_tok[:, 0:D], mv1[:, pp, 0:1], rs1[:, pp:pp + 1],
                                      ALU.subtract, ALU.mult).then_inc(S["norm1"], 1)
                if has(b):
                    pp = (u - 2) % 2
                    dve.wait_ge(S["ex"], b + 1)
                    wait(dve, S["tq"], b - 1)
                    wait(dve, S["kv"], 2 * (b - 1))
                    dve.scalar_tensor_tensor(ph[:, pp, :], rp[:], 0.0, ex[:], ALU.max, ALU.add).then_inc(S["ph"], 1)
                if has(d):
                    pp = u % 2
                    dve.wait_ge(S["wo"], d + 1)
                    wait(dve, S["xr"], d - 1)
                    wait(dve, S["radd"], d - 1)
                    dve.tensor_tensor(x1[:, pp, :], p_wo[:, 0:D], xln[:, u % 4, :],
                                      ALU.add).then_inc(S["x1"], 1)
                if has(e) and u % 2 == 0:
                    route_logits(e)

            def spread(t):
                return t.rearrange("p (a n) -> p a n", n=1).broadcast_to([P, 2, N_EXP])

            def route_logits(e):
                rbb = rb[:].rearrange("p (a n) -> p a n", a=1).broadcast_to([P, 2, N_EXP])
                dve.wait_ge(S["logit"], pairs(e))
                st.link(dve.tensor_tensor(lg[:], p_tok[:, D:D + 2 * N_EXP].rearrange("p (a n) -> p a n", a=2), rbb, ALU.add))
                st.link(dve.tensor_reduce(mx[:], lg[:], X, ALU.max))
                dve.tensor_tensor(lg[:], lg[:], spread(mx[:]), ALU.subtract).then_inc(S["lread"], 1)

            def route_choice(e):
                w8 = cst[:, C_W8:C_W8 + N_EXP].rearrange("p (a n) -> p a n", a=1).broadcast_to([P, 2, N_EXP])
                dve.wait_ge(S["ex_r"], pairs(e))
                st.link(dve.tensor_reduce(sm[:], ex_r[:], X, ALU.add))
                st.link(dve.reciprocal(rsm[:], sm[:]))
                st.link(dve.tensor_tensor(prob[:], ex_r[:], spread(rsm[:]), ALU.mult))
                for k, src in ((0, prob), (1, prob2)):
                    st.link(dve.tensor_reduce(top[:, k, :], src[:], X, ALU.max))
                    st.link(dve.tensor_tensor(eq[:], src[:], spread(top[:, k, :]), ALU.is_equal))
                    st.link(dve.tensor_tensor(eq[:], eq[:], w8, ALU.mult))
                    st.link(dve.tensor_reduce(kx[:], eq[:], X, ALU.max))
                    st.link(dve.tensor_tensor(pick[:, k, :, :], eq[:], spread(kx[:]), ALU.is_equal))
                    if k == 0:
                        st.link(dve.scalar_tensor_tensor(prob2[:], pick[:, 0, :, :], -2.0, prob[:], ALU.mult, ALU.add))
                dve.tensor_tensor(picked[:], pick[:, 0, :, :], pick[:, 1, :, :], ALU.add).then_inc(S["picked"], 1)
                st.link(dve.tensor_tensor(tsum[:], top[:, 0, :], top[:, 1, :], ALU.add))
                st.link(dve.reciprocal(trec[:], tsum[:]))
                st.link(dve.tensor_tensor(gt[:], top[:], trec[:].rearrange("p (a n) -> p a n", a=1).broadcast_to([P, TOP, 2]), ALU.mult))

            def route_rows(e, u):
                q = ((u - 5) % 4) // 2
                off = cst[:, C_OFF:C_OFF + N_EXP].rearrange("p (a n) -> p a n", a=1).broadcast_to([P, 2, N_EXP])
                dve.wait_ge(S["rank_ps"], pairs(e))
                o = D + 2 * N_EXP
                pre = p_tok[:, o:o + 2 * N_EXP].rearrange("p (a n) -> p a n", a=2)
                tot = p_tok[:, o + 2 * N_EXP:o + 4 * N_EXP].rearrange("p (a n) -> p a n", a=2)
                st.link(dve.tensor_tensor(rank[:, 0, :], pre[:, 0, :], carry[:], ALU.add))
                st.link(dve.tensor_tensor(carry[:], tot[:, 0, :], carry[:], ALU.add))
                st.link(dve.tensor_tensor(rank[:, 1, :], pre[:, 1, :], carry[:], ALU.add))
                dve.tensor_tensor(carry[:], tot[:, 1, :], carry[:], ALU.add).then_inc(S["rread"], 1)
                st.link(dve.tensor_scalar(place[:], rank[:], float(CAP), float(DROPPED), ALU.is_ge, ALU.mult))
                st.link(dve.tensor_tensor(place[:], place[:], rank[:], ALU.add))
                st.link(dve.tensor_tensor(place[:], place[:], off, ALU.add))
                for k in range(TOP):
                    st.did(dve.tensor_tensor(sel[:, k, :, :], pick[:, k, :, :], place[:], ALU.mult))
                st.sync()
                st.link(dve.tensor_reduce(rowf[:], sel[:], X, ALU.add))
                for v in range(2):
                    wait(dve, scattered[2 * q + v], (e - (u - 5) % 4) * 8)
                dve.tensor_copy(srow[:, q, :, :], rowf[:]).then_inc(S["rows"], 1)
                st.did(dve.tensor_scalar(okf[:], rowf[:], float(N_SLOT), None, ALU.is_lt))
                st.sync()
                t0 = e - 1
                for k in range(TOP):
                    st.did(dve.tensor_tensor(gates[:, k, bass.ds(t0, 2)], gt[:, k, :], okf[:, k, :], ALU.mult))
                    st.did(dve.tensor_scalar(rows[:, k, bass.ds(t0, 2)], rowf[:, k, :], float(N_SLOT), None, ALU.min))

            def before(b):
                if isinstance(b, int) and b == 0:
                    return
                dve.memset(p_kv[:, 0:DH * (P + 1)], 0.0).then_inc(zeroed, 1)
            before.counted = 0
            supersteps(dve, step, st, per_quad=K_DVE, before_batch=before)


class Signals:

    def __init__(self, scope):
        self.scope, self.sems, self.ahead = scope, {}, {}

    def make(self, names, ahead=0):
        for n in names.split():
            self.sems[n], self.ahead[n] = self.scope.sem(n), ahead

    def start(self, eng, names):
        for n in names.split():
            eng.sem_inc(self.sems[n], self.ahead[n])

    def wait(self, eng, name, value):
        eng.wait_ge(self.sems[name], value + self.ahead[name])

    def __getitem__(self, name):
        return self.sems[name]


def expert_phase(nc, io, xd_dram, yd_dram):
    R = 256
    NBE = CAP // R
    BP = 2 * NBE
    HT = HID // P
    with ExitStack() as ctx:
        s = Scope(ctx, nc, "moe")
        ident = s.sb("ident", [P, P])
        sc2 = s.sb("sc2", [P, DH])
        raw = s.sb("raw", [P, 2 * DH * HID])
        w_hi, w_lo = s.sb("w_hi", [P, 2, 2 * DH * HID], F32R), s.sb("w_lo", [P, 2, 2 * DH * HID], F32R)
        b1 = s.sb("b1", [P, 2, HT])
        b2 = s.sb("b2", [P, 2, D])
        xrow = s.sb("xrow", [P, 2, R // P, D])
        xT_hi, xT_lo = s.sb("xT_hi", [P, 2, DH, R], F32R), s.sb("xT_lo", [P, 2, DH, R], F32R)
        hid = s.sb("hid", [P, HT, R])
        h_hi, h_lo = s.sb("h_hi", [P, 2, HT, R], F32R), s.sb("h_lo", [P, 2, HT, R], F32R)
        y = s.sb("y", [P, 2, R // P, D])
        p_x = [s.ps(f"px{k}") for k in range(2)]
        p_h = [s.ps(f"ph{k}") for k in range(4)]
        p_y = [s.ps(f"py{k}") for k in range(2)]
        S = Signals(s)
        S.make("tables w_raw x_in0 x_in1 w_hi w_part vsteps y_st0 y_st1")
        S.make("xT_ps x_hi x_lo hs_lo y_ps y_done y_free", 2)
        S.make("h_ps gelu", 4)
        block = ctx.enter_context(nc.Block())
        HW = DH * HID
        w1 = [w[:, :, 0:HW].rearrange("p e (k n) -> p e k n", k=DH) for w in (w_hi, w_lo)]
        w2 = [w[:, :, HW:2 * HW].rearrange("p e (m n) -> p e m n", m=HT) for w in (w_hi, w_lo)]

        @block.sync
        def _(sp):
            def weights(e, ep):
                sp.dma_start(raw[:, 0:HW].rearrange("p (k n) -> p k n", k=DH),
                             io["W1"][bass.ds(e, 1)].rearrange("a (k p) n -> p (a k) n", p=P)).then_inc(S["w_raw"], 16)
                sp.dma_start(raw[:, HW:2 * HW].rearrange("p (m n) -> p m n", m=HT),
                             io["W2"][bass.ds(e, 1)].rearrange("a (m p) n -> p (a m) n", p=P)).then_inc(S["w_raw"], 16)
                sp.dma_start(b1[:, ep, :], io["b1"][bass.ds(e, 1)].rearrange("a (m p) -> p (a m)", p=P),
                             allow_slow_non_contiguous=True).then_inc(S["w_raw"], 16)
                sp.dma_start(b2[:, ep, :], io["b2"][bass.ds(e, 1)].broadcast_to([P, D])).then_inc(S["w_raw"], 16)

            sp.dma_start(ident[:], io["consts"][:, C_ID:C_ID + P]).then_inc(S["tables"], 16)
            sp.dma_start(sc2[:], io["norm2"].rearrange("(k p) -> p k", p=P), allow_slow_non_contiguous=True).then_inc(S["tables"], 16)
            weights(0, 0)
            with sp.Fori(0, N_EXP // 2) as j:
                for n in range(BP):
                    B, e = j * BP + n, j * 2 + n // NBE
                    S.wait(sp, "xT_ps", B - 1)
                    sp.dma_start(xrow[:, n % 2], xd_dram[bass.ds(B * R, R), :].rearrange("(a p) d -> p a d", p=P)
                                 ).then_inc(S[f"x_in{n % 2}"], 16)
                    if n % NBE == 1:
                        sp.wait_ge(S["w_part"], (e + 1) * 4)
                        S.wait(sp, "y_done", e * NBE)
                        weights((e + 1) % N_EXP, (n // NBE + 1) % 2)

        @block.tensor
        def _(pe):
            S.start(pe, "xT_ps h_ps y_ps")
            pe.wait_ge(S["tables"], 32)

            def transposes(B, n):
                pp = n % 2
                pe.wait_ge(S[f"x_in{pp}"], (B - pp) * 8 + 16)
                S.wait(pe, "x_lo", B - 1)
                for k in range(DH):
                    for r in range(R // P):
                        mm = pe.transpose(p_x[pp][:, k * R + r * P:k * R + (r + 1) * P], xrow[:, pp, r, k * P:(k + 1) * P], ident[:])
                mm.then_inc(S["xT_ps"], 1)

            def first(B, n):
                pp, ep = n % 2, n // NBE
                S.wait(pe, "x_lo", B + 1)
                for m in range(HT):
                    S.wait(pe, "gelu", B * HT + m - 3)
                    c = slice(m * P, (m + 1) * P)
                    split_product(pe, p_h[m % 4][:, 0:R], [(w1[0][:, ep, k, c], w1[1][:, ep, k, c], xT_hi[:, pp, k, :],
                                                            xT_lo[:, pp, k, :]) for k in range(DH)]).then_inc(S["h_ps"], 1)

            def second(B, n):
                pp, ep = n % 2, n // NBE
                S.wait(pe, "hs_lo", B + 1)
                S.wait(pe, "y_done", B - 1)
                for r in range(R // P):
                    c = slice(r * P, (r + 1) * P)
                    mm = split_product(pe, p_y[pp][:, r * D:(r + 1) * D],
                                       [(h_hi[:, pp, m, c], h_lo[:, pp, m, c], w2[0][:, ep, m, :], w2[1][:, ep, m, :])
                                        for m in range(HT)])
                mm.then_inc(S["y_ps"], 1)

            with pe.Fori(0, N_EXP // 2) as j:
                transposes(j * BP, 0)
                for n in range(BP):
                    B = j * BP + n
                    if n % NBE == 0:
                        pe.wait_ge(S["w_part"], (j * 2 + n // NBE) * 4 + 4)
                    if n + 1 < BP:
                        transposes(B + 1, n + 1)
                    first(B, n)
                    if n > 0:
                        second(B - 1, n - 1)
                second(j * BP + BP - 1, BP - 1)

        @block.scalar
        def _(act):
            S.start(act, "x_hi gelu")

            def high(B, n):
                pp = n % 2
                S.wait(act, "xT_ps", B + 1)
                S.wait(act, "h_ps", (B - 1) * HT + 4)
                act.copy(xT_hi[:, pp].rearrange("p k n -> p (k n)"), p_x[pp][:]).then_inc(S["x_hi"], 1)

            with act.Fori(0, N_EXP // 2) as j:
                high(j * BP, 0)
                for n in range(BP):
                    B, pp, ep = j * BP + n, n % 2, n // NBE
                    if n + 1 < BP:
                        high(B + 1, n + 1)
                    if n % NBE == 0:
                        act.wait_ge(S["w_raw"], (j * 2 + ep) * 64 + 64)
                    S.wait(act, "hs_lo", B)
                    for m in range(HT):
                        S.wait(act, "h_ps", B * HT + m + 1)
                        act.activation(hid[:, m, :], p_h[m % 4][:, 0:R], ACT.Gelu, bias=b1[:, ep, m:m + 1]).then_inc(S["gelu"], 1)

        @block.gpsimd
        def _(pool):
            S.start(pool, "y_free")

            def low(e, ep, piece):
                c = slice(piece * HID, (piece + 1) * HID)
                pool.wait_ge(S["w_hi"], e * 4 + piece + 1)
                pool.tensor_tensor(w_lo[:, ep, c], raw[:, c], w_hi[:, ep, c].bitcast(F32), ALU.subtract).then_inc(S["w_part"], 1)

            def store(B, n):
                S.wait(pool, "y_done", B + 1)
                pool.dma_start(yd_dram[bass.ds(B * R, R), :].rearrange("(a p) d -> p a d", p=P), y[:, n % 2]
                               ).then_inc(S[f"y_st{n % 2}"], 16)
                pool.wait_ge(S[f"y_st{n % 2}"], (B - n % 2) * 8 + 16)
                pool.sem_inc(S["y_free"], 1)
            for piece in range(4):
                low(0, 0, piece)
            with pool.Fori(0, N_EXP // 2) as j:
                for n in range(BP):
                    B, e = j * BP + n, j * 2 + n // NBE
                    if n % NBE > 0:
                        low(e + 1, (n // NBE + 1) % 2, n % NBE - 1)
                    if n > 0:
                        store(B - 1, n - 1)
                store(j * BP + BP - 1, BP - 1)

        @block.vector
        def _(dve):
            S.start(dve, "x_lo hs_lo y_done")
            dve.wait_ge(S["tables"], 32)
            st = Steps(dve, S["vsteps"])

            def high(e, ep, piece):
                c = slice(piece * HID, (piece + 1) * HID)
                if piece == 0:
                    dve.wait_ge(S["w_raw"], e * 64 + 64)
                    if not isinstance(e, int):
                        S.wait(dve, "y_ps", (e - 1) * NBE)
                if piece < DH:
                    st.link(dve.tensor_scalar(raw[:, c], raw[:, c], sc2[:, piece:piece + 1], None, ALU.mult))
                dve.tensor_copy(w_hi[:, ep, c], raw[:, c]).then_inc(S["w_hi"], 1)

            def x_low(B, n):
                pp = n % 2
                S.wait(dve, "x_hi", B + 1)
                dve.tensor_tensor(xT_lo[:, pp].rearrange("p k n -> p (k n)"), p_x[pp][:],
                                  xT_hi[:, pp].rearrange("p k n -> p (k n)").bitcast(F32), ALU.subtract).then_inc(S["x_lo"], 1)

            def hidden(B, n):
                pp = n % 2
                S.wait(dve, "y_ps", B - 1)
                for q in range(2):
                    c = slice(q * HT // 2, (q + 1) * HT // 2)
                    S.wait(dve, "gelu", B * HT + (q + 1) * HT // 2)
                    st.link(dve.tensor_copy(h_hi[:, pp, c, :], hid[:, c, :]))
                    lo = dve.tensor_tensor(h_lo[:, pp, c, :], hid[:, c, :], h_hi[:, pp, c, :].bitcast(F32), ALU.subtract)
                lo.then_inc(S["hs_lo"], 1)

            def out_rows(B, n):
                pp, ep = n % 2, n // NBE
                S.wait(dve, "y_ps", B + 1)
                S.wait(dve, "y_free", B - 1)
                dve.tensor_tensor(y[:, pp], p_y[pp][:].rearrange("p (a d) -> p a d", d=D),
                                  b2[:, ep:ep + 1, :].broadcast_to([P, R // P, D]), ALU.add).then_inc(S["y_done"], 1)

            for piece in range(4):
                high(0, 0, piece)
            s0 = st.n
            K = 2 * BP + 2 * DH
            with dve.Fori(0, N_EXP // 2) as j:
                st.base, st.n = j * K + s0, 0
                x_low(j * BP, 0)
                for n in range(BP):
                    B, e = j * BP + n, j * 2 + n // NBE
                    if n + 1 < BP:
                        x_low(B + 1, n + 1)
                    hidden(B, n)
                    if n > 0:
                        out_rows(B - 1, n - 1)
                    if n % NBE > 0:
                        high(e + 1, (n // NBE + 1) % 2, n % NBE - 1)
                out_rows(j * BP + BP - 1, BP - 1)
                assert st.n == K, st.n


def soft_tables_phase(nc, io, phi_hi, phi_lo):
    ST = SOFT // P
    with ExitStack() as ctx:
        s = Scope(ctx, nc, "phi")
        ident, raw = s.sb("ident", [P, P]), s.sb("raw", [P, ST, D])
        banks = [s.ps(f"t{k}") for k in range(4)]
        loaded, turned, high, low = s.sem("loaded"), s.sem("turned"), s.sem("high"), s.sem("low")
        block = ctx.enter_context(nc.Block())
        parts = [(k, q) for k in range(DH) for q in range(ST // 4)]
        cols = lambda n: slice(parts[n][1] * 512, parts[n][1] * 512 + 512)

        @block.sync
        def _(sp):
            sp.dma_start(ident[:], io["consts"][:, C_ID:C_ID + P]).then_inc(loaded, 16)
            sp.dma_start(raw[:], io["phi_w"].rearrange("(j p) d -> p j d", p=P)).then_inc(loaded, 16)

        @block.tensor
        def _(pe):
            pe.wait_ge(loaded, 32)
            for n, (k, q) in enumerate(parts):
                wait(pe, low, n - 3)
                for i in range(4):
                    mm = pe.transpose(banks[n % 4][:, i * P:(i + 1) * P], raw[:, 4 * q + i, k * P:(k + 1) * P], ident[:])
                mm.then_inc(turned, 1)

        @block.scalar
        def _(act):
            for n, (k, q) in enumerate(parts):
                act.wait_ge(turned, n + 1)
                act.copy(phi_hi[:, k, cols(n)], banks[n % 4][:]).then_inc(high, 1)

        @block.vector
        def _(dve):
            for n, (k, q) in enumerate(parts):
                dve.wait_ge(high, n + 1)
                dve.tensor_tensor(phi_lo[:, k, cols(n)], banks[n % 4][:], phi_hi[:, k, cols(n)].bitcast(F32), ALU.subtract).then_inc(low, 1)


def soft_dispatch_phase(nc, io, yd_dram, xT_dram, res, gates, rows, phi_hi, phi_lo, smax, acc, spare):
    G, QS = 4, 512
    QE = QS // SOFT_P
    K = G * SOFT // QS
    NG = NT // G
    QN = SOFT // QS
    LAG = 4
    with ExitStack() as ctx:
        s = Scope(ctx, nc, "disp")
        sb = s.sb
        ident = sb("ident", [P, P])
        ones_r = sb("ones_r", [P, P], F32R)
        ones_f = sb("ones_f", [P, P])
        bias_hl = sb("bias_hl", [P, SOFT], F32R)
        half = sb("half", [P, 1])
        idx = sb("idx", [P, 2, TOP, G], U32)
        yb = sb("yb", [P, 2, TOP, D])
        hb = sb("hb", [P, D])
        st6 = sb("st6", [P, 6])
        mv = sb("mv", [P, 2, 2])
        ve, rs = sb("ve", [P, 2]), sb("rs", [P, 2])
        xn_hi, xn_lo = sb("xn_hi", [P, 2, G, D], F32R), sb("xn_lo", [P, 2, G, D], F32R)
        xT_hi, xT_lo = sb("xT_hi", [P, 2, G, DH, P], F32R), sb("xT_lo", [P, 2, G, DH, P], F32R)
        mb = sb("mb", [P, QE])
        mq = sb("mq", [P, G, SOFT // QS, SOFT_P])
        su, ru = sb("su", [P, QE]), sb("ru", [P, 2, QE])
        d_hi, d_lo = sb("d_hi", [P, 4, QS], F32R), sb("d_lo", [P, 4, QS], F32R)
        sh, e, dd = (spare[:, k * 2 * QS:(k + 1) * 2 * QS].rearrange("p (a n) -> p a n", a=2) for k in range(3))
        xn = spare[:, 6 * QS:6 * QS + 2 * D].rearrange("p (a d) -> p a d", a=2)
        xT = spare[:, 6 * QS + 2 * D:6 * QS + 4 * D].rearrange("p (a k n) -> p a k n", a=2, k=DH)
        brow = spare[:, 0:SOFT]
        p_l = [s.ps(f"l{k}") for k in range(2)]
        p_a = [[s.ps(f"a{k}{q}") for q in range(2)] for k in range(DH)]
        p_t = s.ps("t")
        names = ("loaded setup idx gat0 gat1 h2 var rstd xn xnhi xnlo tps xT32 xThi xTlo xst0 xst1 lps shifted e r d dhi dlo xmm accf steps fence").split()
        S = {n: s.sem(n) for n in names}
        block = ctx.enter_context(nc.Block())

        def over_groups(eng, run, st=None, per=0):
            run(0, 0)
            s0 = 0 if st is None else st.base + st.n
            with eng.Fori(0, NG // 2 - 1) as j:
                if st is not None:
                    st.base, st.n = j * (2 * per) + s0, 0
                run(j * 2 + 1, 1)
                run(j * 2 + 2, 0)
                if st is not None:
                    assert st.n == 2 * per, (st.n, 2 * per)
            if st is not None:
                st.base, st.n = s0 + 2 * per * (NG // 2 - 1), 0
            run(NG - 1, 1)

        def more(g):
            return not isinstance(g, int) or g < NG - 1

        FETCH, RESIDUAL, RSTD, NORMAL, HIGH, TURN, TURNED, LOW, TURNED_LOW = 0, 2, 3, 4, 5, 5, 6, 6, 7

        def at(kk, stage):
            return kk >= stage and (kk - stage) % 2 == 0 and (kk - stage) // 2 < G

        def tile_at(kk, stage):
            return (kk - stage) // 2

        def tile(t):
            return bass.ds(t, 1)

        @block.sync
        def _(sp):
            sp.dma_start(ident[:], io["consts"][:, C_ID:C_ID + P]).then_inc(S["loaded"], 16)
            for r in (0, 32):
                sp.dma_start(brow[r:r + 1, :], io["phi_b"].rearrange("(a n) -> a n", a=1)).then_inc(S["loaded"], 16)

            def store(t, i):
                sp.wait_ge(S["xT32"], t + 1)
                sp.dma_start(xT_dram[:, :, bass.ds(t * P, P)], xT[:, i % 2]).then_inc(S[f"xst{i % 2}"], 16)
            for i in range(G):
                store(i, i)

            def run(g, gp):
                if more(g):
                    for i in range(G):
                        store(g * G + G + i, i)
            over_groups(sp, run)
            for k in range(2):
                sp.wait_ge(S[f"xst{k}"], 16 * (NT // 2))

        @block.tensor
        def _(pe):
            pe.wait_ge(S["setup"], 1)

            def turn(t, i):
                pe.wait_ge(S["xn"], t + 1)
                wait(pe, S["xThi"], t)
                for k in range(DH):
                    mm = pe.transpose(p_t[:, k * P:(k + 1) * P], xn[:, i % 2, k * P:(k + 1) * P], ident[:])
                mm.then_inc(S["tps"], 1)
            for i in range(G):
                turn(i, i)

            def logits(g, gp, kk):
                k = g * K + kk
                Q, i = kk // G, kk % G
                pe.wait_ge(S["xTlo"], g * G + i + 1)
                wait(pe, S["shifted"], k - 1)
                c = slice(Q * QS, (Q + 1) * QS)
                pe.matmul(p_l[kk % 2][:], ones_r[:], bias_hl[:, c], start=True, stop=False)
                split_product(pe, p_l[kk % 2][:], [(xT_hi[:, gp, i, h, :], xT_lo[:, gp, i, h, :], phi_hi[:, h, c], phi_lo[:, h, c])
                                                   for h in range(DH)], first=False).then_inc(S["lps"], 1)

            def gather(g, gp, kk):
                k = g * K + kk
                Q, i = kk // G, kk % G
                q = Q % 2
                pe.wait_ge(S["dlo"], k + 1)
                pe.wait_ge(S["xnlo"], g * G + i + 1)
                if i == 0:
                    wait(pe, S["accf"], g * QN + Q - 1)
                for h in range(DH):
                    c = slice(h * P, (h + 1) * P)
                    mm = split_product(pe, p_a[h][q][:], [(xn_hi[:, gp, i, c], xn_lo[:, gp, i, c], d_hi[:, kk % 4, :], d_lo[:, kk % 4, :])],
                                       first=i == 0, last=i == G - 1)
                mm.then_inc(S["xmm"], 1)

            def run(g, gp):
                for kk in range(K):
                    logits(g, gp, kk)
                    if kk >= LAG:
                        gather(g, gp, kk - LAG)
                    elif not isinstance(g, int) or g > 0:
                        gather(g - 1, 1 - gp, kk - LAG + K)
                    if more(g) and at(kk, TURN):
                        turn(g * G + G + tile_at(kk, TURN), tile_at(kk, TURN))
            over_groups(pe, run)
            for kk in range(K - LAG, K):
                gather(NG - 1, 1, kk)

        @block.scalar
        def _(act):
            act.wait_ge(S["setup"], 1)

            def token_high(t, i, gp):
                act.wait_ge(S["xn"], t + 1)
                wait(act, S["xmm"], (t - i) * 4 - K)
                act.copy(xn_hi[:, gp, i, :], xn[:, i % 2, :]).then_inc(S["xnhi"], 1)

            def turned_high(t, i, gp):
                act.wait_ge(S["tps"], t + 1)
                wait(act, S[f"xst{i % 2}"], (t - i % 2) * 8)
                wait(act, S["xTlo"], t - 1)
                act.copy(xT[:, i % 2].rearrange("p k n -> p (k n)"), p_t[:, 0:D]).then_inc(S["xT32"], 1)
                wait(act, S["lps"], (t - i) * 4 - K)
                act.copy(xT_hi[:, gp, i].rearrange("p k n -> p (k n)"), p_t[:, 0:D]).then_inc(S["xThi"], 1)
            for i in range(G):
                token_high(i, i, 0)
                turned_high(i, i, 0)

            def high(g, kk):
                k = g * K + kk
                act.wait_ge(S["d"], k + 1)
                wait(act, S["xmm"], k - 3)
                act.copy(d_hi[:, kk % 4, :], dd[:, kk % 2, :]).then_inc(S["dhi"], 1)

            def run(g, gp):
                for kk in range(K):
                    k = g * K + kk
                    act.wait_ge(S["shifted"], k + 1)
                    wait(act, S["d"], k - 1)
                    act.activation(e[:, kk % 2, :], sh[:, kk % 2, :], ACT.Exp).then_inc(S["e"], 1)
                    if kk >= 1:
                        high(g, kk - 1)
                    elif not isinstance(g, int) or g > 0:
                        high(g - 1, K - 1)
                    if more(g):
                        if at(kk, HIGH):
                            i = tile_at(kk, HIGH)
                            token_high(g * G + G + i, i, 1 - gp)
                        if at(kk, TURNED):
                            i = tile_at(kk, TURNED)
                            turned_high(g * G + G + i, i, 1 - gp)
            over_groups(act, run)
            high(NG - 1, K - 1)

        @block.gpsimd
        def _(pool):
            pool.wait_ge(S["setup"], 1)

            def fetch(t, i, gp):
                if i == 0:
                    pool.wait_ge(S["idx"], (t + G) // G)
                wait(pool, S["h2"], t - 1)
                pool.sem_inc(S["fence"], 1)
                for k in range(TOP):
                    pool.indirect_dma_start(yb[:, i % 2, k, :], None, yd_dram,
                                            bass.IndirectOffsetOnAxis(ap=idx[:, gp, k, i:i + 1], axis=0),
                                            bounds_check=N_SLOT, oob_is_err=False).then_inc(S[f"gat{i % 2}"], 16)

            def rstd(t, i):
                pool.wait_ge(S["var"], t + 1)
                pool.tensor_tensor(rs[:, i % 2:i % 2 + 1], ve[:, i % 2:i % 2 + 1], half[:], ALU.pow).then_inc(S["rstd"], 1)

            def token_low(t, i, gp):
                pool.wait_ge(S["xnhi"], t + 1)
                pool.tensor_tensor(xn_lo[:, gp, i, :], xn[:, i % 2, :], xn_hi[:, gp, i, :].bitcast(F32), ALU.subtract).then_inc(S["xnlo"], 1)
            for i in range(G):
                fetch(i, i, 0)
                rstd(i, i)
                token_low(i, i, 0)

            def low(g, kk):
                k = g * K + kk
                pool.wait_ge(S["dhi"], k + 1)
                pool.tensor_tensor(d_lo[:, kk % 4, :], dd[:, kk % 2, :], d_hi[:, kk % 4, :].bitcast(F32), ALU.subtract).then_inc(S["dlo"], 1)

            def weight(g, kk):
                k = g * K + kk
                pool.wait_ge(S["r"], k + 1)
                wait(pool, S["dlo"], k - 1)
                pool.tensor_tensor(dd[:, kk % 2, :].rearrange("p (n s) -> p n s", s=SOFT_P), e[:, kk % 2, :].rearrange("p (n s) -> p n s", s=SOFT_P),
                                   ru[:, kk % 2, :].rearrange("p (n a) -> p n a", a=1).broadcast_to([P, QE, SOFT_P]), ALU.mult).then_inc(S["d"], 1)

            def run(g, gp):
                first = isinstance(g, int) and g == 0
                for kk in range(K):
                    if kk >= 1:
                        weight(g, kk - 1)
                    elif not first:
                        weight(g - 1, K - 1)
                    if kk >= 2:
                        low(g, kk - 2)
                    elif not first:
                        low(g - 1, kk - 2 + K)
                    if more(g):
                        t0 = g * G + G
                        if at(kk, FETCH):
                            i = tile_at(kk, FETCH)
                            fetch(t0 + i, i, 1 - gp)
                        if at(kk, RSTD):
                            i = tile_at(kk, RSTD)
                            rstd(t0 + i, i)
                        if at(kk, LOW):
                            i = tile_at(kk, LOW)
                            token_low(t0 + i, i, 1 - gp)
            over_groups(pool, run)
            weight(NG - 1, K - 1)
            low(NG - 1, K - 2)
            low(NG - 1, K - 1)

        @block.vector
        def _(dve):
            st = Steps(dve, S["steps"])
            st.did(dve.memset(acc[:], 0.0))
            st.did(dve.memset(half[:], -0.5))
            st.link(dve.memset(ones_f[:], 1.0))
            st.did(dve.tensor_copy(ones_r[:], ones_f[:]))
            st.link(dve.memset(bias_hl[:].bitcast(F32), 0.0))
            dve.wait_ge(S["loaded"], 48)
            st.did(dve.tensor_copy(bias_hl[0:1, :], brow[0:1, :]))
            st.link(dve.tensor_copy(bias_hl[32:33, :], brow[32:33, :]))
            st.link(dve.tensor_tensor(brow[32:33, :], brow[32:33, :], bias_hl[32:33, :].bitcast(F32), ALU.subtract))
            st.link(dve.tensor_copy(bias_hl[32:33, :], brow[32:33, :]))
            dve.engine_nop().then_inc(S["setup"], 1)

            def indices(g, gp):
                dve.tensor_copy(idx[:, gp], rows[:, :, bass.ds(g * G, G)]).then_inc(S["idx"], 1)

            def residual(t, i):
                pp = i % 2
                r = res[:, tile(t), :].rearrange("p a d -> p (a d)")
                dve.wait_ge(S[f"gat{pp}"], (t - pp) * 16 + 32)
                wait(dve, S["xn"], t - 1)
                st.link(dve.scalar_tensor_tensor(hb[:], yb[:, pp, 0, :], gates[:, 0, tile(t)], r, ALU.mult, ALU.add))
                dve.scalar_tensor_tensor(r, yb[:, pp, 1, :], gates[:, 1, tile(t)], hb[:], ALU.mult, ALU.add).then_inc(S["h2"], 1)
                dve.wait_ge(S["h2"], t + 1)
                st.fence()
                st.link(dve.bn_stats(st6[:], r))
                st.fence()
                st.link(dve.bn_aggr(mv[:, pp, :], st6[:]))
                dve.tensor_scalar(ve[:, pp:pp + 1], mv[:, pp, 1:2], EPS, None, ALU.add).then_inc(S["var"], 1)

            def normal(t, i):
                pp = i % 2
                dve.wait_ge(S["rstd"], t + 1)
                wait(dve, S["xnlo"], t - 1)
                wait(dve, S["tps"], t - 1)
                dve.tensor_scalar(xn[:, pp, :], res[:, tile(t), :].rearrange("p a d -> p (a d)"), mv[:, pp, 0:1], rs[:, pp:pp + 1],
                                  ALU.subtract, ALU.mult).then_inc(S["xn"], 1)

            def turned_low(t, i, gp):
                dve.wait_ge(S["xThi"], t + 1)
                dve.tensor_tensor(xT_lo[:, gp, i], xT[:, i % 2], xT_hi[:, gp, i].bitcast(F32), ALU.subtract).then_inc(S["xTlo"], 1)

            indices(0, 0)
            for i in range(G):
                residual(i, i)
                normal(i, i)
                turned_low(i, i, 0)

            def shift(g, kk):
                k = g * K + kk
                Q, i = kk // G, kk % G
                dve.wait_ge(S["lps"], k + 1)
                by_expert = p_l[kk % 2][:].rearrange("p (n s) -> p n s", s=SOFT_P)
                wait(dve, S["shifted"], k)
                st.did(dve.tensor_reduce(mb[:], by_expert, X, ALU.max))
                st.link(dve.tensor_reduce(mq[:, i, Q, :], p_l[kk % 2][:].rearrange("p (n s) -> p s n", s=SOFT_P), X, ALU.max))
                wait(dve, S["e"], k - 1)
                dve.tensor_tensor(sh[:, kk % 2, :].rearrange("p (n s) -> p n s", s=SOFT_P), by_expert,
                                  mb[:].rearrange("p (n a) -> p n a", a=1).broadcast_to([P, QE, SOFT_P]), ALU.subtract).then_inc(S["shifted"], 1)
                if Q == QN - 1:
                    st.did(dve.tensor_reduce(smax[:, tile(g * G + i), :].rearrange("p a s -> p (a s)"), mq[:, i].rearrange("p q s -> p s q"), X, ALU.max))

            def sums(g, kk):
                k = g * K + kk
                dve.wait_ge(S["e"], k + 1)
                wait(dve, S["r"], k)
                st.link(dve.tensor_reduce(su[:], e[:, kk % 2, :].rearrange("p (n s) -> p n s", s=SOFT_P), X, ALU.add))
                wait(dve, S["d"], k - 1)
                dve.reciprocal(ru[:, kk % 2, :], su[:]).then_inc(S["r"], 1)

            def drain_acc(g, Q):
                dve.wait_ge(S["xmm"], g * K + (Q + 1) * G)
                c = slice(Q * QS, (Q + 1) * QS)
                for h in range(DH):
                    ins = dve.tensor_tensor(acc[:, h, c], p_a[h][Q % 2][:], acc[:, h, c], ALU.add)
                ins.then_inc(S["accf"], 1)

            def run(g, gp):
                first = isinstance(g, int) and g == 0
                for kk in range(K):
                    if kk % G == 0:
                        Q = (kk - G - LAG) // G
                        if Q >= 0:
                            drain_acc(g, Q)
                        elif not first:
                            drain_acc(g - 1, Q + QN)
                    shift(g, kk)
                    if kk >= 1:
                        sums(g, kk - 1)
                    elif not first:
                        sums(g - 1, K - 1)
                    if more(g):
                        t0 = g * G + G
                        if kk == 0:
                            indices(g + 1, 1 - gp)
                        if at(kk, RESIDUAL):
                            i = tile_at(kk, RESIDUAL)
                            residual(t0 + i, i)
                        if at(kk, NORMAL):
                            i = tile_at(kk, NORMAL)
                            normal(t0 + i, i)
                        if at(kk, TURNED_LOW):
                            i = tile_at(kk, TURNED_LOW)
                            turned_low(t0 + i, i, 1 - gp)
            per = K * 3 + G + 5 * G
            over_groups(dve, run, st, per)
            sums(NG - 1, K - 1)
            drain_acc(NG - 1, QN - 2)
            drain_acc(NG - 1, QN - 1)


def soft_experts_phase(nc, io, acc, spare, yt_hi, yt_lo):
    ST = SOFT // P
    EP = P // SOFT_P
    with ExitStack() as ctx:
        s = Scope(ctx, nc, "sexp")
        ident, half = s.sb("ident", [P, P]), s.sb("half", [P, 1])
        eb = spare.rearrange("p (j d) -> p j d", j=ST)
        ew = s.sb("ew", [P, 2, EP, DH, D])
        xs, xl, xh, xhT, yv = s.sb("xs", [P, 2, DH, P]), s.sb("xl", [P, 2, D]), s.sb("xh", [P, 2, D]), s.sb("xhT", [P, 2, DH, P]), s.sb("yv", [P, D])
        st6, mv, ve, rs = s.sb("st6", [P, 6]), s.sb("mv", [P, 2]), s.sb("ve", [P, 2]), s.sb("rs", [P, 2])
        p_t, p_u, p_e = ([s.ps(f"{n}{k}") for k in range(2)] for n in "tue")
        names = "loaded w0 w1 half clip tps var rstd xl xh ups xhT eps ydone steps".split()
        S = {n: s.sem(n) for n in names}
        block = ctx.enter_context(nc.Block())

        def tiles(eng, run, st=None, per=0):
            run(0, 0)
            run(1, 1)
            s0 = 0 if st is None else st.base + st.n
            with eng.Fori(1, ST // 2) as j:
                if st is not None:
                    st.base, st.n = (j - 1) * (2 * per) + s0, 0
                run(j * 2, 0)
                run(j * 2 + 1, 1)

        @block.sync
        def _(sp):
            sp.dma_start(ident[:], io["consts"][:, C_ID:C_ID + P]).then_inc(S["loaded"], 16)
            for k in range(EP):
                src = io["expert_b"].rearrange("(j e) h -> e j h", e=EP)[k:k + 1]
                sp.dma_start(eb[32 * k:32 * k + 32], src.broadcast_to([32, ST, D])).then_inc(S["loaded"], 16)

            def run(j, jp):
                wait(sp, S["eps"], j - 1)
                for k in range(EP):
                    sp.dma_start(ew[:, jp, k], io["expert_w"][bass.ds(j * EP + k, 1)].rearrange("a (k p) h -> p (a k) h", p=P)).then_inc(S[f"w{jp}"], 16)
            tiles(sp, run)

        @block.tensor
        def _(pe):
            pe.wait_ge(S["loaded"], 16 * (1 + EP))

            def run(j, jp):
                pe.wait_ge(S["clip"], j + 1)
                wait(pe, S["xl"], j - 1)
                for k in range(DH):
                    mm = pe.transpose(p_t[jp][:, k * P:(k + 1) * P], xs[:, jp, k, :], ident[:])
                mm.then_inc(S["tps"], 1)
                pe.wait_ge(S["xh"], j + 1)
                wait(pe, S["xhT"], j - 1)
                for k in range(DH):
                    mm = pe.transpose(p_u[jp][:, k * P:(k + 1) * P], xh[:, jp, k * P:(k + 1) * P], ident[:])
                mm.then_inc(S["ups"], 1)
                pe.wait_ge(S["xhT"], j + 1)
                pe.wait_ge(S[f"w{jp}"], (j - jp) * 32 + 64)
                wait(pe, S["ydone"], j - 1)
                for n in range(EP):
                    for k in range(DH):
                        mm = pe.matmul(p_e[jp][32 * n:32 * n + 32, 0:D], xhT[:, jp, k, 32 * n:32 * n + 32], ew[:, jp, n, k, :],
                                       start=k == 0, stop=k == DH - 1, skip_group_check=True)
                mm.then_inc(S["eps"], 1)
            tiles(pe, run)

        @block.scalar
        def _(act):
            def run(j, jp):
                act.wait_ge(S["xl"], j + 1)
                wait(act, S["ups"], j - 1)
                act.activation(xh[:, jp, :], xl[:, jp, :], ACT.Tanh).then_inc(S["xh"], 1)
                act.wait_ge(S["ups"], j + 1)
                wait(act, S["eps"], j - 1)
                act.copy(xhT[:, jp].rearrange("p k n -> p (k n)"), p_u[jp][:, 0:D]).then_inc(S["xhT"], 1)
            tiles(act, run)

        @block.gpsimd
        def _(pool):
            pool.wait_ge(S["half"], 1)

            def run(j, jp):
                pool.wait_ge(S["var"], j + 1)
                pool.tensor_tensor(rs[:, jp:jp + 1], ve[:, jp:jp + 1], half[:], ALU.pow).then_inc(S["rstd"], 1)
            tiles(pool, run)

        @block.vector
        def _(dve):
            st = Steps(dve, S["steps"])
            dve.memset(half[:], -0.5).then_inc(S["half"], 1)
            dve.wait_ge(S["loaded"], 16 * (1 + EP))

            def run(j, jp):
                wait(dve, S["tps"], j - 1)
                dve.tensor_scalar(xs[:, jp], acc[:, :, bass.ds(j * P, P)], -33000.0, 65000.0, ALU.max, ALU.min).then_inc(S["clip"], 1)
                dve.wait_ge(S["tps"], j + 1)
                st.link(dve.bn_stats(st6[:], p_t[jp][:, 0:D]))
                st.fence()
                st.link(dve.bn_aggr(mv[:], st6[:]))
                dve.tensor_scalar(ve[:, jp:jp + 1], mv[:, 1:2], EPS, None, ALU.add).then_inc(S["var"], 1)
                dve.wait_ge(S["rstd"], j + 1)
                wait(dve, S["xh"], j - 1)
                dve.tensor_scalar(xl[:, jp, :], p_t[jp][:, 0:D], mv[:, 0:1], rs[:, jp:jp + 1], ALU.subtract, ALU.mult).then_inc(S["xl"], 1)
                dve.wait_ge(S["eps"], j + 1)
                yrow = yv[:].rearrange("p (a d) -> p a d", a=1)
                st.link(dve.tensor_tensor(yrow, p_e[jp][:, 0:D].rearrange("p (a d) -> p a d", a=1), eb[:, bass.ds(j, 1), :], ALU.add))
                st.link(dve.tensor_copy(yt_hi[:, bass.ds(j, 1), :], yrow))
                dve.tensor_tensor(yt_lo[:, bass.ds(j, 1), :], yrow, yt_hi[:, bass.ds(j, 1), :].bitcast(F32), ALU.subtract).then_inc(S["ydone"], 1)
            tiles(dve, run, st, 5)


def soft_combine_phase(nc, io, xT_dram, out, res, phi_hi, phi_lo, smax, yt_hi, yt_lo, e):
    ST = SOFT // P
    CT = 512
    SUB = CT // P
    NC = N_TOK // CT
    with ExitStack() as ctx:
        s = Scope(ctx, nc, "comb")
        sb = s.sb
        ident = sb("ident", [P, P])
        bcol = sb("bcol", [P, ST])
        neg = sb("neg", [P, P], F32R)
        same = sb("same", [P, P])
        xraw = sb("xraw", [P, CT])
        xT_hi, xT_lo = sb("xT_hi", [P, 2, DH, CT], F32R), sb("xT_lo", [P, 2, DH, CT], F32R)
        ms = sb("ms", [P, SUB, SOFT_P])
        mT = sb("mT", [P, CT], F32R)
        tot = sb("tot", [P, CT])
        rt = sb("rt", [P, CT])
        cc = sb("cc", [P, 2, CT])
        c_hi, c_lo = sb("c_hi", [P, 2, CT], F32R), sb("c_lo", [P, 2, CT], F32R)
        M2 = 2 * SOFT_P
        p_l = [s.ps(f"l{k}") for k in range(2)]
        p_y = [[s.ps(f"y{k}{h}") for h in range(2)] for k in range(2)]
        p_s, p_m = s.ps("s"), s.ps("m")
        names = "loaded setup xin xhi xlo ms mps mT lps e tot sps rt c chi clo ymm odone st steps".split()
        S = {n: s.sem(n) for n in names}
        block = ctx.enter_context(nc.Block())

        def chunks(eng, run, st=None, per=0):
            run(0, 0)
            run(1, 1)
            s0 = 0 if st is None else st.base + st.n
            with eng.Fori(1, NC // 2 - 1) as j:
                if st is not None:
                    st.base, st.n = (j - 1) * (2 * per) + s0, 0
                run(j * 2, 0)
                run(j * 2 + 1, 1)
                if st is not None:
                    assert st.n == 2 * per, (st.n, 2 * per)
            if st is not None:
                st.base, st.n = s0 + 2 * per * (NC // 2 - 2), 0
            run(NC - 2, 0)
            run(NC - 1, 1)

        def has(c):
            return not isinstance(c, int) or 0 <= c < NC

        @block.sync
        def _(sp):
            sp.dma_start(ident[:], io["consts"][:, C_ID:C_ID + P]).then_inc(S["loaded"], 16)
            sp.dma_start(same[:], io["consts"][:, C_PG:C_PG + P]).then_inc(S["loaded"], 16)
            sp.dma_start(bcol[:], io["phi_b"].rearrange("(j p) -> p j", p=P), allow_slow_non_contiguous=True).then_inc(S["loaded"], 16)

            def load(c):
                for h in range(DH):
                    wait(sp, S["xlo"], c * DH + h)
                    sp.dma_start(xraw[:], xT_dram[:, h, bass.ds(c * CT, CT)]).then_inc(S["xin"], 16)

            def store(c):
                sp.wait_ge(S["odone"], c + 1)
                sp.dma_start(out[bass.ds(c * CT, CT), :].rearrange("(a p) d -> p a d", p=P), res[:, bass.ds(c * SUB, SUB), :]).then_inc(S["st"], 16)
            load(0)

            def run(c, cp):
                if has(c + 1):
                    load(c + 1)
                if has(c - 1):
                    store(c - 1)
            chunks(sp, run)
            store(NC - 1)
            sp.wait_ge(S["st"], 16 * NC)

        @block.tensor
        def _(pe):
            pe.wait_ge(S["setup"], 1)

            def maxima(c):
                pe.wait_ge(S["ms"], c + 1)
                wait(pe, S["mT"], c)
                for a in range(SUB):
                    mm = pe.transpose(p_m[0:SOFT_P, a * P:(a + 1) * P], ms[:, a, :], ident[:])
                mm.then_inc(S["mps"], 1)
            maxima(0)

            def logits(c, cp, j):
                k = c * ST + j
                if j == 0:
                    pe.wait_ge(S["xlo"], (c + 1) * DH)
                    pe.wait_ge(S["mT"], c + 1)
                wait(pe, S["e"], k - 1)
                sl = slice(j * P, (j + 1) * P)
                m = slice(M2 * cp, M2 * cp + M2)
                pe.matmul(p_l[j % 2][:], neg[m, :], mT[m, :], start=True, stop=False)
                split_product(pe, p_l[j % 2][:], [(phi_hi[:, h, sl], phi_lo[:, h, sl], xT_hi[:, cp, h, :], xT_lo[:, cp, h, :])
                                                  for h in range(DH)], first=False).then_inc(S["lps"], 1)

            def combine(c, cp, j):
                k = c * ST + j
                pe.wait_ge(S["clo"], k + 1)
                if j == 0:
                    wait(pe, S["odone"], c - 1)
                for a in range(SUB):
                    cs = slice(a * P, (a + 1) * P)
                    for n, (lhs, rhs) in enumerate(((c_hi, yt_hi), (c_hi, yt_lo), (c_lo, yt_hi))):
                        mm = pe.matmul(p_y[cp][a // 2][:, (a % 2) * D:(a % 2 + 1) * D], lhs[:, j % 2, cs], rhs[:, j, :],
                                       start=j == 0 and a % 2 == 0 and n == 0, stop=j == ST - 1 and n == 2, skip_group_check=True)
                mm.then_inc(S["ymm"], 1)

            def run(c, cp):
                for j in range(ST):
                    logits(c, cp, j)
                    if has(c - 1):
                        combine(c - 1, 1 - cp, j)
                    if j == 8 and has(c + 1):
                        maxima(c + 1)
                pe.wait_ge(S["tot"], c + 1)
                wait(pe, S["rt"], c)
                pe.matmul(p_s[:], same[:], tot[:], start=True, stop=True).then_inc(S["sps"], 1)
            chunks(pe, run)
            for j in range(ST):
                combine(NC - 1, 1, j)

        @block.scalar
        def _(act):
            act.wait_ge(S["setup"], 1)

            def high(c, cp, h):
                act.wait_ge(S["xin"], (c * DH + h) * 16 + 16)
                wait(act, S["lps"], (c - 1) * ST)
                act.copy(xT_hi[:, cp, h, :], xraw[:]).then_inc(S["xhi"], 1)

            def maxima(c):
                wait(act, S["mps"], c)
                act.copy(ms[:], smax[:, bass.ds(c * SUB, SUB), :]).then_inc(S["ms"], 1)
            for h in range(DH):
                high(0, 0, h)
            maxima(0)

            def weights_high(c, j):
                k = c * ST + j
                act.wait_ge(S["c"], k + 1)
                wait(act, S["ymm"], k - 1)
                act.copy(c_hi[:, j % 2, :], cc[:, j % 2, :]).then_inc(S["chi"], 1)

            def run(c, cp):
                for j in range(ST):
                    k = c * ST + j
                    if has(c - 1):
                        weights_high(c - 1, j)
                    act.wait_ge(S["lps"], k + 1)
                    wait(act, S["c"], k - ST + 1)
                    act.activation(e[:, j, :], p_l[j % 2][:], ACT.Exp, bias=bcol[:, j:j + 1]).then_inc(S["e"], 1)
                    if has(c + 1):
                        if j in (5, 9):
                            high(c + 1, 1 - cp, (j - 5) // 4)
                        if j == 6:
                            maxima(c + 1)
            chunks(act, run)
            for j in range(ST):
                weights_high(NC - 1, j)

        @block.gpsimd
        def _(pool):
            def weights(c, j):
                k = c * ST + j
                if j == 0:
                    pool.wait_ge(S["rt"], c + 1)
                wait(pool, S["clo"], k - 1)
                pool.tensor_tensor(cc[:, j % 2, :], e[:, j, :], rt[:], ALU.mult).then_inc(S["c"], 1)

            def run(c, cp):
                if has(c - 1):
                    for j in range(ST):
                        weights(c - 1, j)
            chunks(pool, run)
            for j in range(ST):
                weights(NC - 1, j)

        @block.vector
        def _(dve):
            st = Steps(dve, S["steps"])
            dve.wait_ge(S["loaded"], 48)
            st.did(dve.tensor_scalar(neg[:], same[:], -1.0, None, ALU.mult))
            st.sync()
            dve.engine_nop().then_inc(S["setup"], 1)

            def low(c, cp, h):
                dve.wait_ge(S["xhi"], c * DH + h + 1)
                dve.tensor_tensor(xT_lo[:, cp, h, :], xraw[:], xT_hi[:, cp, h, :].bitcast(F32), ALU.subtract).then_inc(S["xlo"], 1)

            def maxima(c, cp):
                dve.wait_ge(S["mps"], c + 1)
                m = [slice(M2 * cp + SOFT_P * k, M2 * cp + SOFT_P * (k + 1)) for k in range(2)]
                st.link(dve.tensor_copy(mT[m[0], :], p_m[0:SOFT_P, :]))
                dve.tensor_tensor(mT[m[1], :], p_m[0:SOFT_P, :], mT[m[0], :].bitcast(F32), ALU.subtract).then_inc(S["mT"], 1)
            for h in range(DH):
                low(0, 0, h)
            maxima(0, 0)

            def weights_low(c, j):
                dve.wait_ge(S["chi"], c * ST + j + 1)
                dve.tensor_tensor(c_lo[:, j % 2, :], cc[:, j % 2, :], c_hi[:, j % 2, :].bitcast(F32), ALU.subtract).then_inc(S["clo"], 1)

            def finish(c, cp):
                dve.wait_ge(S["ymm"], (c + 1) * ST)
                for a in range(SUB):
                    rows = res[:, bass.ds(c * SUB + a, 1), :]
                    ins = dve.tensor_tensor(rows, p_y[cp][a // 2][:, (a % 2) * D:(a % 2 + 1) * D].rearrange("p (a d) -> p a d", a=1),
                                            rows, ALU.add)
                ins.then_inc(S["odone"], 1)

            def run(c, cp):
                for j in range(ST):
                    k = c * ST + j
                    if has(c - 1):
                        weights_low(c - 1, j)
                    dve.wait_ge(S["e"], k + 1)
                    if j == 1:
                        wait(dve, S["sps"], c)
                        st.did(dve.tensor_tensor(tot[:], e[:, 0, :], e[:, 1, :], ALU.add))
                    elif j > 1:
                        st.sync()
                        st.did(dve.tensor_tensor(tot[:], tot[:], e[:, j, :], ALU.add))
                    if has(c + 1):
                        if j in (7, 11):
                            low(c + 1, 1 - cp, (j - 7) // 4)
                        if j == 12:
                            maxima(c + 1, 1 - cp)
                st.sync()
                dve.sem_inc(S["tot"], 1)
                dve.wait_ge(S["sps"], c + 1)
                wait(dve, S["c"], c * ST)
                dve.reciprocal(rt[:], p_s[:]).then_inc(S["rt"], 1)
                if has(c - 1):
                    finish(c - 1, 1 - cp)
            chunks(dve, run, st, ST)
            for j in range(ST):
                weights_low(NC - 1, j)
            finish(NC - 1, 1)


NAMES = {
    "x": "x", "mask": "mask_BS_i1_0", "emb": "L0_tok_emb", "pca": "L0_tok_pca_lookup", "proj_w": "L0_tok_proj_w",
    "proj_b": "L0_tok_proj_b", "fus_w": "L0_tok_fus_w", "fus_b": "L0_tok_fus_b", "ln_g": "L0_tok_ln_g", "ln_b": "L0_tok_ln_b",
    "norm1": "L0_attn_norm1_scale", "norm2": "L0_attn_norm2_scale", "Wq": "L0_attn_Wq", "bq": "L0_attn_bq",
    "Wk": "L0_attn_Wk", "bk": "L0_attn_bk", "Wv": "L0_attn_Wv", "bv": "L0_attn_bv", "Wg": "L0_attn_Wg", "bg": "L0_attn_bg",
    "Wo": "L0_attn_Wo", "bo": "L0_attn_bo", "router_W": "L0_attn_router_W", "router_b": "L0_attn_router_b",
    "W1": "L0_attn_W1", "b1": "L0_attn_b1", "W2": "L0_attn_W2", "b2": "L0_attn_b2", "phi_w": "L0_ffn_phi_w",
    "phi_b": "L0_ffn_phi_b", "expert_w": "L0_ffn_expert_w", "expert_b": "L0_ffn_expert_b",
}


def tower(nc, io, out):
    with ExitStack() as ctx:
        def dram(name, shape, dt=F32):
            return nc.dram_tensor(name, shape, dt, kind="Internal").ap()
        feat_dram = dram("scratch_features", [64, N_TOK])
        xd_dram = dram("scratch_dispatched", [N_SLOT, D])
        yd_dram = dram("scratch_expert_rows", [N_SLOT + 1, D])
        xT_dram = dram("scratch_tokens_T", [P, DH, N_TOK])
        s = Scope(ctx, nc, "all")
        res = s.sb("res", [P, NT, D])
        gates = s.sb("gates", [P, TOP, NT])
        rows = s.sb("rows", [P, TOP, NT], U32)
        features_phase(nc, io, feat_dram, xd_dram, yd_dram)
        attention_phase(nc, io, feat_dram, xd_dram, res, gates, rows)
        expert_phase(nc, io, xd_dram, yd_dram)
        phi_hi, phi_lo = s.sb("phi_hi", [P, DH, SOFT], F32R), s.sb("phi_lo", [P, DH, SOFT], F32R)
        smax = s.sb("smax", [P, NT, SOFT_P])
        work = s.sb("work", [P, 2 * DH * SOFT])
        acc = work[:, 0:DH * SOFT].rearrange("p (k n) -> p k n", k=DH)
        spare = work[:, DH * SOFT:2 * DH * SOFT]
        soft_tables_phase(nc, io, phi_hi, phi_lo)
        soft_dispatch_phase(nc, io, yd_dram, xT_dram, res, gates, rows, phi_hi, phi_lo, smax, acc, spare)
        yt_hi, yt_lo = s.sb("yt_hi", [P, SOFT // P, D], F32R), s.sb("yt_lo", [P, SOFT // P, D], F32R)
        soft_experts_phase(nc, io, acc, spare, yt_hi, yt_lo)
        soft_combine_phase(nc, io, xT_dram, out, res, phi_hi, phi_lo, smax, yt_hi, yt_lo,
                           work[:].rearrange("p (j n) -> p j n", j=SOFT // P))


def kernel(**inputs):
    import concourse.bacc as bacc
    from concourse.bass_utils import run_bass_kernel_spmd

    nc = bacc.Bacc("TRN2", target_bir_lowering=False, num_devices=1)
    arrays, io = {}, {}
    for short, name in NAMES.items():
        arrays[name] = np.ascontiguousarray(inputs[name])
        io[short] = nc.dram_tensor(name, arrays[name].shape, mybir.dt.from_np(arrays[name].dtype), kind="ExternalInput").ap()
    for name, table in (("consts", constant_table()), ("rope", rotary_table())):
        arrays[name] = table
        io[name] = nc.dram_tensor(name, table.shape, F32, kind="ExternalInput").ap()
    out = nc.dram_tensor("out", [BATCH, SEQ, D], F32, kind="ExternalOutput").ap()
    tower(nc, io, out.rearrange("b s d -> (b s) d"))
    return run_bass_kernel_spmd(nc, [arrays], core_ids=[0]).results[0]["out"]
```

```python
from contextlib import ExitStack

import numpy as np

import concourse.bass as bass
from concourse import mybir

F32 = mybir.dt.float32
F32R = mybir.dt.float32r
BF16 = mybir.dt.bfloat16
I32 = mybir.dt.int32
U32 = mybir.dt.uint32
ALU = mybir.AluOpType
ACT = mybir.ActivationFunctionType
X = mybir.AxisListType.X

P = 128
BATCH, SEQ, D = 4, 2048, 256
N_TOK = BATCH * SEQ
NT = N_TOK // P
TPB = SEQ // P
DH = D // P
VOCAB, N_PCA = 28, 20
HEADS, DK, CHUNK = 16, 16, 64
HPH = HEADS // DH
HALF = DK // 2
K_DVE = 118
N_EXP, HID, TOP = 8, 1024, 2
CAP = int(1.25 * (N_TOK / N_EXP))
N_SLOT = N_EXP * CAP
DROPPED = 1 << 20
SOFT_E, SOFT_P = 64, 32
SOFT = SOFT_E * SOFT_P
EPS = 1e-5
BDW = P + HPH

C_ID, C_TRI, C_BD, C_W8, C_OFF, C_ROW, C_ISB, C_PG = 0, 128, 256, 392, 400, 408, 409, 410
C_END = C_PG + 128


def constant_table():
    t = np.zeros((P, C_END), np.float32)
    p = np.arange(P)
    t[:, C_ID:C_ID + P] = np.eye(P)
    t[:, C_TRI:C_TRI + P] = p[:, None] < p[None, :]
    t[:, C_BD:C_BD + P] = p[:, None] // DK == p[None, :] // DK
    t[:, C_BD + P:C_BD + BDW] = p[:, None] // DK == np.arange(HPH)[None, :]
    t[:, C_W8:C_W8 + N_EXP] = N_EXP - np.arange(N_EXP)
    t[:, C_OFF:C_OFF + N_EXP] = CAP * np.arange(N_EXP)
    t[:, C_ROW] = p % 32
    t[:, C_ISB] = p % 32 == VOCAB
    t[:, C_PG:C_PG + P] = p[:, None] % SOFT_P == p[None, :] % SOFT_P
    return t


def rotary_table():
    inv = (np.float32(1.0) / np.power(np.float32(10000.0), np.arange(HALF, dtype=np.float32) / np.float32(HALF)).astype(np.float32)).astype(np.float32)
    ang = np.arange(SEQ, dtype=np.float32)[:, None] * inv[None, :]
    return np.concatenate([np.cos(ang), np.sin(ang)], axis=1).astype(np.float32)


class Steps:

    def __init__(self, eng, sem):
        self.eng, self.sem, self.base, self.n = eng, sem, 0, 0

    def did(self, ins):
        ins.then_inc(self.sem, 1)
        self.n += 1

    def sync(self):
        self.eng.wait_ge(self.sem, self.base + self.n)

    def link(self, ins):
        self.did(ins)
        self.sync()

    def fence(self):
        self.eng.sem_inc(self.sem, 1)
        self.n += 1


def wait(eng, sem, value):
    if not isinstance(value, int) or value > 0:
        eng.wait_ge(sem, value)


class Scope:

    def __init__(self, ctx, nc, tag):
        self.ctx, self.nc, self.tag = ctx, nc, tag

    def sb(self, name, shape, dt=F32):
        return self.ctx.enter_context(self.nc.sbuf_tensor(f"{self.tag}_{name}", shape, dt))

    def ps(self, name, shape=(P, 512), dt=F32):
        return self.ctx.enter_context(self.nc.psum_tensor(f"{self.tag}_{name}", list(shape), dt))

    def sem(self, name):
        return self.ctx.enter_context(self.nc.semaphore(f"{self.tag}_{name}"))


def split_weights(st, raw, scaled, hi, lo, scale):
    if scale is not None:
        st.link(st.eng.tensor_scalar(scaled, raw, scale, None, ALU.mult))
    else:
        scaled = raw
    st.link(st.eng.tensor_copy(hi, scaled))
    st.did(st.eng.tensor_tensor(lo, scaled, hi.bitcast(F32), ALU.subtract))


def split_product(pe, out, parts, first=True, last=True):
    mm = None
    n = 3 * len(parts)
    i = 0
    for lhs_hi, lhs_lo, rhs_hi, rhs_lo in parts:
        for lhs, rhs in ((lhs_hi, rhs_hi), (lhs_hi, rhs_lo), (lhs_lo, rhs_hi)):
            mm = pe.matmul(out, lhs, rhs, start=first and i == 0, stop=last and i == n - 1)
            i += 1
    return mm


def attention_phase(nc, io, feat_dram, xd_dram, yd_dram, res, gates, rows):
    with ExitStack() as ctx:
        s = Scope(ctx, nc, "att")
        sb, ps, sem = s.sb, s.ps, s.sem
        cst = sb("cst", [P, C_END])
        rope = sb("rope", [P, NT, 2 * HALF])
        raw = sb("raw", [P, DH, 4 * D])
        w_hi = sb("w_hi", [P, DH, 4 * D], F32R)
        w_lo = sb("w_lo", [P, DH, 4 * D], F32R)
        raw_o = sb("raw_o", [P, DH, D])
        wo_hi = sb("wo_hi", [P, DH, D], F32R)
        wo_lo = sb("wo_lo", [P, DH, D], F32R)
        sc1 = sb("sc1", [P, DH])
        sc2 = sb("sc2", [P, DH])
        raw_r = sb("raw_r", [P, DH, N_EXP])
        w_r = sb("w_r", [P, DH, N_EXP])
        rb = sb("rb", [P, N_EXP])
        bias = sb("bias", [P, 5 * D])
        bias_hl = sb("bias_hl", [P, 5 * D], F32R)
        ones_f = sb("ones_f", [P, P])
        ones_r = sb("ones_r", [P, P], F32R)
        ones_b = sb("ones_b", [P, P], BF16)
        tri_b = sb("tri_b", [P, P], BF16)
        gain = sb("gain", [P, D])
        shift = sb("shift", [P, D])
        emb = sb("emb", [32, D])
        embT = sb("embT", [P, DH, 32])
        pcaT = sb("pcaT", [N_PCA, VOCAB])
        pjw = sb("pjw", [N_PCA, D])
        contT = sb("contT", [P, DH, 32])
        fus = sb("fus", [P, 2 * DH, D])
        mtab = sb("mtab", [64, D])
        half = sb("half", [P, 1])
        inv_d = sb("inv_d", [P, 1])
        minus = sb("minus", [P, 1])
        mr = sb("mr", [P, 1])
        nb1, nb2 = sb("nb1", [P, 2]), sb("nb2", [P, 2])
        room = res[:].rearrange("p t d -> p (t d)")
        ids, msk = (room[:, k * SEQ:(k + 1) * SEQ].bitcast(I32) for k in range(2))
        one, win, length = (room[:, k * SEQ:(k + 1) * SEQ] for k in (2, 3, 4))
        mpad, opad = (room[:, (5 + k) * SEQ + 2 * k:(6 + k) * SEQ + 2 * k + 2] for k in range(2))
        zero = sb("zero", [P, D])
        xln = sb("xln", [P, 4, D])
        feat = sb("feat", [64, 2, P])
        n1 = sb("n1", [P, 2, D])
        n1g = sb("n1g", [P, D])
        st1, st2 = sb("st1", [P, 6]), sb("st2", [P, 6])
        mv1, mv2 = sb("mv1", [P, 2, 2]), sb("mv2", [P, 2, 2])
        ve1, ve2, ms1, ms2 = (sb(n, [P, 2]) for n in ("ve1", "ve2", "ms1", "ms2"))
        rs1, rs2, rr1, rr2 = (sb(n, [P, 2]) for n in ("rs1", "rs2", "rr1", "rr2"))
        ssq1, ssq2 = sb("ssq1", [P, 2]), sb("ssq2", [P, 2])
        junk = sb("junk", [P, D])
        xa = sb("xa", [P, 2, D])
        xaT_hi = sb("xaT_hi", [P, DH, P], F32R)
        xaT_lo = sb("xaT_lo", [P, DH, P], F32R)
        ra, rb_, rp, mn = (sb(n, [P, 2 * D]) for n in ("ra", "rb2", "rp", "mn"))
        ex = sb("ex", [P, 2 * D])
        ph = sb("ph", [P, 2, 2 * D])
        v1 = sb("v1", [P, 2, DH, P + 1])
        th = sb("th", [P, 2, D])
        bd = sb("bd", [P, 2, DH, BDW])
        qT = sb("qT", [P, DH, P])
        dn, rdn = sb("dn", [P, DH, HPH]), sb("rdn", [P, DH, HPH])
        avg = sb("avg", [P, D])
        att = sb("att", [P, 2, D])
        atT_hi = sb("atT_hi", [P, DH, P], F32R)
        atT_lo = sb("atT_lo", [P, DH, P], F32R)
        x1 = sb("x1", [P, 2, D])
        xr = sb("xr", [P, 4, D])
        xrT = sb("xrT", [P, 2, DH, P])
        lg, ex_r, prob, eq, prob2, rank, place = (sb(n, [P, 2, N_EXP]) for n in ("lg", "ex_r", "prob", "eq", "prob2", "rank", "place"))
        pick = sb("pick", [P, TOP, 2, N_EXP])
        picked = sb("picked", [P, 2, N_EXP], BF16)
        sel = sb("sel", [P, TOP, 2, N_EXP])
        mx, sm, rsm, kx = (sb(n, [P, 2]) for n in ("mx", "sm", "rsm", "kx"))
        top = sb("top", [P, TOP, 2])
        tsum = sb("tsum", [P, 2])
        trec = sb("trec", [P, 2])
        rowf = sb("rowf", [P, TOP, 2])
        okf = sb("okf", [P, TOP, 2])
        gt = sb("gt", [P, TOP, 2])
        carry = sb("carry", [P, N_EXP])
        srow = sb("srow", [P, 2, TOP, 2], U32)
        p_tok, p_xt, p_qk, p_vg, p_kv, p_num, p_tr, p_wo = (ps(n) for n in ("tok", "xt", "qk", "vg", "kv", "num", "tr", "wo"))

        loaded, loaded2, setup = sem("loaded"), sem("loaded2"), sem("setup")
        tok_in, stored, cleared, filled = sem("tok_in"), sem("stored"), sem("cleared"), sem("filled")
        one_done, summed, averaged, win_done = sem("one_done"), sem("summed"), sem("averaged"), sem("win_done")
        su_pe, su_dve, su_fix = sem("su_pe"), sem("su_dve"), sem("su_fix")
        zeroed = sem("zeroed")
        names = ("rp tok var1 rstd1 norm1 h var2 rstd2 xln ssq1 rr1 xa xaT xaT_hi xaT_lo qk vg mn ex ph vth kv bd tq qT num "
                 "att atT atT_hi atT_lo wo x1 ssq2 rr2 xr xrT_ps xrT logit lread ex_r picked rank_ps rread rows steps psteps fence radd rope_read").split()
        S = {n: sem(n) for n in names}
        feat_in = [sem(f"feat_in{k}") for k in range(2)]
        scattered = [sem(f"scattered{k}") for k in range(4)]
        block = ctx.enter_context(nc.Block())
        ident = cst[:, C_ID:C_ID + P]
        N_LOAD = 16

        def supersteps(eng, step, st=None, per_quad=0, before_batch=None):
            if before_batch is not None:
                before_batch(0)
            for i in range(0, 11):
                step(i, i % 4)

            def run(q, at, base):
                if st is not None:
                    st.base, st.n = base, 0
                for u in range(4):
                    step(at + u, (3 + u) % 4)
                if st is not None:
                    assert st.n == per_quad, (st.n, per_quad)

            def start():
                return 0 if st is None else st.base + st.n

            def settle(value):
                if st is not None:
                    st.base, st.n = value, 0

            s0 = start()
            with eng.Fori(0, 2) as q:
                run(q, q * 4 + 11, q * per_quad + s0)
            settle(s0 + 2 * per_quad)
            s0 = start()
            extra = 0 if st is None or before_batch is None else before_batch.counted
            with eng.Fori(0, 2) as b:
                if before_batch is not None:
                    settle(b * (4 * per_quad + extra) + s0)
                    before_batch(b + 1)
                with eng.Fori(0, 4) as q:
                    run(q, b * 16 + q * 4 + 19, b * (4 * per_quad + extra) + q * per_quad + (s0 + extra))
            settle(s0 + 2 * (4 * per_quad + extra))
            if before_batch is not None:
                before_batch(3)
            s0 = start()
            with eng.Fori(0, 3) as q:
                run(q, q * 4 + 51, q * per_quad + s0)
            settle(s0 + 3 * per_quad)
            for i in range(63, NT + 8):
                step(i, i % 4)

        def has(t):
            return not isinstance(t, int) or 0 <= t < NT

        def pairs(e):
            return (e + 1) // 2

        def rpairs(a):
            return (a - 6) // 2

        def pairs_before(e, u):
            odd = (u - 5) % 2
            return (e - odd) // 2

        @block.sync
        def _(sp):
            def ld(dst, src, to=loaded, strided=False):
                sp.dma_start(dst, src, allow_slow_non_contiguous=strided).then_inc(to, 16)
            ld(cst[:], io["consts"], tok_in)
            for b in range(BATCH):
                ld(ids[32 * b:32 * b + 32, :], io["x"][b:b + 1, :].broadcast_to([32, SEQ]), tok_in)
                ld(msk[32 * b:32 * b + 32, :], io["mask"][b:b + 1, :].broadcast_to([32, SEQ]), tok_in)
            ld(pcaT[:], io["pca"].rearrange("v f -> f v"), strided=True)
            ld(pjw[:], io["proj_w"])
            ld(fus[:], io["fus_w"].rearrange("(k p) n -> p k n", p=P))
            ld(sc1[:], io["norm1"].rearrange("(k p) -> p k", p=P), strided=True)
            ld(sc2[:], io["norm2"].rearrange("(k p) -> p k", p=P), strided=True)
            for n, w in enumerate(("Wq", "Wk", "Wv", "Wg")):
                ld(raw[:, :, n * D:(n + 1) * D], io[w].rearrange("(k p) n -> p k n", p=P))
            ld(raw_o[:], io["Wo"].rearrange("(k p) n -> p k n", p=P))
            ld(raw_r[:], io["router_W"].rearrange("(k p) n -> p k n", p=P))
            for n, w in enumerate(("bq", "bk", "bv", "bg", "bo")):
                for r in (0, 32):
                    ld(bias[r:r + 1, n * D:(n + 1) * D], io[w].rearrange("(a n) -> a n", a=1))
            for dst, w in ((gain, "ln_g"), (shift, "ln_b")):
                ld(dst[:], io[w].rearrange("(a n) -> a n", a=1).broadcast_to([P, D]))
            ld(rb[:], io["router_b"].rearrange("(a n) -> a n", a=1).broadcast_to([P, N_EXP]))
            for b in range(BATCH):
                ld(rope[:, b * TPB:(b + 1) * TPB, :], io["rope"].rearrange("(t p) c -> p t c", p=P))
            sp.wait_ge(su_fix, 1)
            ld(emb[0:VOCAB, :], io["emb"])
            for k, (made, rows_of) in enumerate(((one_done, one), (win_done, win))):
                sp.wait_ge(made, 1)
                for b in range(BATCH):
                    ld(feat_dram[32 * k:32 * k + 32, b * SEQ:(b + 1) * SEQ], rows_of[32 * b:32 * b + 32, :], stored)
            sp.wait_ge(su_fix, 2)
            ld(contT[:, :, VOCAB], io["proj_b"].rearrange("(k p) -> p k", p=P), loaded2, True)
            sp.wait_ge(su_fix, 3)
            ld(mtab[VOCAB:VOCAB + 1, :], io["fus_b"].rearrange("(a n) -> a n", a=1), loaded2)

            sp.wait_ge(stored, 16 * 2 * BATCH)

            def step(i, u):
                if has(i):
                    if not isinstance(i, int) or i >= 2:
                        sp.wait_ge(S["tok"], i - 1)
                    sp.dma_start(feat[:, u % 2, :], feat_dram[:, bass.ds(i * P, P)]).then_inc(feat_in[u % 2], 16)
            supersteps(sp, step)

        N_TOK_IN = 16 * (1 + 2 * BATCH)
        N_LOADED = 16 * (6 + 4 + 2 + 10 + 3 + 4)

        @block.tensor
        def _(pe):
            pe.wait_ge(tok_in, 16)
            pe.wait_ge(loaded, N_LOADED)
            pe.wait_ge(su_dve, 1)
            for k in range(DH):
                mm = pe.transpose(p_tr[:, 32 * k:32 * k + 32], emb[:, k * P:(k + 1) * P], ident[0:32, 0:32])
            mm.then_inc(su_pe, 1)
            for k in range(DH):
                mm = pe.matmul(p_num[:, 32 * k:32 * k + VOCAB], pjw[:, k * P:(k + 1) * P], pcaT[:], start=True, stop=True)
            mm.then_inc(su_pe, 1)
            pe.wait_ge(su_dve, 2)
            pe.wait_ge(loaded2, 16)
            for k in range(DH):
                mm = pe.matmul(p_wo[0:32, 0:D], embT[:, k, :], fus[:, k, :], start=k == 0, stop=k == DH - 1)
            mm.then_inc(su_pe, 1)
            for k in range(DH):
                mm = pe.matmul(p_xt[0:32, 0:D], contT[:, k, :], fus[:, DH + k, :], start=k == 0, stop=k == DH - 1)
            mm.then_inc(su_pe, 1)
            pe.wait_ge(setup, 1)
            pe.wait_ge(loaded2, 32)

            def kv(t, u, ch):
                pp = u % 2
                if ch == 0:
                    pe.wait_ge(S["ph"], t + 1)
                    pe.wait_ge(S["vth"], t + 1)
                pe.wait_ge(zeroed, 1) if isinstance(t, int) and t == 0 else None
                wait(pe, S["bd"], 2 * t + ch)
                a = CHUNK * ch
                for h in range(DH):
                    mm = pe.matmul(p_kv[:, h * (P + 1):(h + 1) * (P + 1)],
                                   ph[a:a + CHUNK, pp, D + h * P:D + (h + 1) * P], v1[a:a + CHUNK, pp, h, :],
                                   start=False, stop=True, skip_group_check=True)
                mm.then_inc(S["kv"], 1)

            def step(i, u):
                a, b, c, d, e = i, i - 2, i - 3, i - 4, i - 5
                if has(c):
                    kv(c, (u - 3) % 4, 0)
                if has(b):
                    pe.wait_ge(S["xa"], b + 1)
                    wait(pe, S["xaT_lo"], b)
                    wait(pe, S["xrT"], b - 3)
                    for k in range(DH):
                        mm = pe.transpose(p_xt[:, k * P:(k + 1) * P], xa[:, (u - 2) % 2, k * P:(k + 1) * P], ident)
                    mm.then_inc(S["xaT"], 1)
                if has(d):
                    pe.wait_ge(S["att"], d + 1)
                    wait(pe, S["atT_lo"], d)
                    for k in range(DH):
                        mm = pe.transpose(p_tr[:, k * P:(k + 1) * P], att[:, u % 2, k * P:(k + 1) * P], ident)
                    mm.then_inc(S["atT"], 1)
                if has(c):
                    cp = (u - 3) % 2
                    wait(pe, S["att"], c)
                    for k in range(DH):
                        mm = pe.transpose(p_num[:, k * P:(k + 1) * P], ph[:, cp, k * P:(k + 1) * P], ident)
                    mm.then_inc(S["tq"], 1)
                    kv(c, (u - 3) % 4, 1)
                if has(e - 1) and u % 2 == 1:
                    wait(pe, S["rread"], rpairs(a - 1))
                    pe.wait_ge(S["xrT"], e)
                    wait(pe, S["norm1"], a if not isinstance(a, int) else min(a, NT))
                    for v in range(2):
                        for k in range(DH):
                            mm = pe.matmul(p_tok[:, D + v * N_EXP:D + (v + 1) * N_EXP], xrT[:, v, k, :], w_r[:, k, :],
                                           start=k == 0, stop=k == DH - 1)
                    mm.then_inc(S["logit"], 1)
                def project(q, bank, done):
                    c0 = q * 2 * D
                    pe.matmul(bank[:], ones_r[:], bias_hl[:, c0:c0 + 2 * D], start=True, stop=False)
                    split_product(pe, bank[:], [(xaT_hi[:, k, :], xaT_lo[:, k, :], w_hi[:, k, c0:c0 + 2 * D],
                                                 w_lo[:, k, c0:c0 + 2 * D]) for k in range(DH)],
                                  first=False).then_inc(S[done], 1)
                if has(b):
                    pe.wait_ge(S["xaT_lo"], b + 1)
                    pe.wait_ge(S["xaT_hi"], b + 1)
                    wait(pe, S["rope_read"], b)
                    project(0, p_qk, "qk")
                if has(c):
                    pe.wait_ge(S["qT"], c + 1)
                    pe.wait_ge(S["bd"], 2 * c + 2)
                    for ch in range(2):
                        for h in range(DH):
                            mm = pe.matmul(p_num[CHUNK * ch:CHUNK * ch + CHUNK, h * BDW:(h + 1) * BDW],
                                           qT[:, h, CHUNK * ch:CHUNK * ch + CHUNK], bd[:, ch, h, :], start=True, stop=True,
                                           skip_group_check=True)
                    mm.then_inc(S["num"], 1)
                if has(e - 1) and u % 2 == 1:
                    pe.wait_ge(S["picked"], pairs(e - 1))
                    wait(pe, S["norm1"], a if not isinstance(a, int) else min(a, NT))
                    o = D + 2 * N_EXP
                    pe.matmul(p_tok[:, o:o + 2 * N_EXP], tri_b[:], picked[:].rearrange("p a b -> p (a b)"), start=True, stop=True)
                    pe.matmul(p_tok[:, o + 2 * N_EXP:o + 4 * N_EXP], ones_b[:], picked[:].rearrange("p a b -> p (a b)"),
                              start=True, stop=True).then_inc(S["rank_ps"], 1)
                if has(a):
                    pe.wait_ge(feat_in[u % 2], (a - u % 2) * 8 + 16)
                    wait(pe, S["norm1"], a)
                    if u % 2 == 0:
                        wait(pe, S["rread"], rpairs(a))
                    pe.matmul(p_tok[:, 0:D], feat[:, u % 2, :], mtab[:], start=True, stop=True).then_inc(S["tok"], 1)
                if has(e):
                    pe.wait_ge(S["xr"], e + 1)
                    wait(pe, S["xaT_lo"], e + 4 if not isinstance(e, int) else min(e + 4, NT))
                    wait(pe, S["xrT"], e)
                    for k in range(DH):
                        mm = pe.transpose(p_xt[:, k * P:(k + 1) * P], xr[:, (u - 5) % 4, k * P:(k + 1) * P], ident)
                    mm.then_inc(S["xrT_ps"], 1)
                if has(b):
                    wait(pe, S["vth"], b)
                    project(1, p_vg, "vg")
                if has(d):
                    pe.wait_ge(S["atT_lo"], d + 1)
                    wait(pe, S["x1"], d)
                    pe.matmul(p_wo[:, 0:D], ones_r[:], bias_hl[:, 4 * D:5 * D], start=True, stop=False)
                    split_product(pe, p_wo[:, 0:D], [(atT_hi[:, k, :], atT_lo[:, k, :], wo_hi[:, k, :], wo_lo[:, k, :])
                                                     for k in range(DH)], first=False).then_inc(S["wo"], 1)
            def before(b):
                if isinstance(b, int) and b == 0:
                    return
                pe.wait_ge(zeroed, b + 1)
                pe.sem_inc(S["fence"], 1)
            before.counted = 0
            supersteps(pe, step, before_batch=before)

        @block.scalar
        def _(act):
            ZT = 8
            act.wait_ge(cleared, 1)
            act.wait_ge(tok_in, N_TOK_IN)
            act.wait_ge(loaded, N_LOADED)
            for k in range(N_SLOT // P // ZT):
                act.dma_start(xd_dram[k * P * ZT:(k + 1) * P * ZT, :].rearrange("(a p) d -> p a d", a=ZT),
                              zero[:].rearrange("p (a d) -> p a d", a=1).broadcast_to([P, ZT, D])).then_inc(filled, 16)
            act.dma_start(yd_dram[N_SLOT:N_SLOT + 1, :], zero[0:1, :]).then_inc(filled, 16)
            act.wait_ge(setup, 1)

            def step(i, u):
                a, a1, b, c, d, e = i, i - 1, i - 2, i - 3, i - 4, i - 5
                if has(b):
                    pp = (u - 2) % 2
                    act.wait_ge(S["xaT"], b + 1)
                    wait(act, S["vg"], b)
                    act.copy(xaT_hi[:].rearrange("p k n -> p (k n)"), p_xt[:, 0:D]).then_inc(S["xaT_hi"], 1)
                if has(d):
                    act.wait_ge(S["atT"], d + 1)
                    wait(act, S["wo"], d)
                    act.copy(atT_hi[:].rearrange("p k n -> p (k n)"), p_tr[:, 0:D]).then_inc(S["atT_hi"], 1)
                if has(c):
                    act.wait_ge(S["tq"], c + 1)
                    wait(act, S["num"], c)
                    act.copy(qT[:].rearrange("p k n -> p (k n)"), p_num[:, 0:D]).then_inc(S["qT"], 1)
                if has(e):
                    ep, slot = (u - 5) % 2, (u - 5) % 4
                    act.wait_ge(S["rr2"], e + 1)
                    wait(act, scattered[slot], (e - slot) * 8)
                    act.activation(xr[:, slot, :], x1[:, ep, :], ACT.Copy, scale=rr2[:, ep:ep + 1]).then_inc(S["xr"], 1)
                if has(e - 1) and u % 2 == 1:
                    act.wait_ge(S["lread"], pairs(e - 1))
                    act.activation(ex_r[:], lg[:], ACT.Exp).then_inc(S["ex_r"], 1)
                if has(a1):
                    pp = (u - 1) % 2
                    act.wait_ge(S["rstd2"], a1 + 1)
                    wait(act, S["x1"], a1 - 3)
                    wait(act, S["xa"], a1 - 3)
                    act.activation(xln[:, (u - 1) % 4, :], res[:, bass.ds(a1, 1), :].rearrange("p a d -> p (a d)"), ACT.Identity,
                                   scale=rs2[:, pp:pp + 1], bias=nb2[:, pp:pp + 1]).then_inc(S["xln"], 1)
                    act.wait_ge(S["xln"], a1 + 1)
                    act.activation(junk[:], xln[:, (u - 1) % 4, :], ACT.Square, accum_out=ssq1[:, pp:pp + 1]).then_inc(S["ssq1"], 1)
                if has(a1):
                    pp = (u - 1) % 2
                    act.wait_ge(S["rr1"], a1 + 1)
                    wait(act, S["xaT"], a1 - 1)
                    act.activation(xa[:, pp, :], xln[:, (u - 1) % 4, :], ACT.Copy, scale=rr1[:, pp:pp + 1]).then_inc(S["xa"], 1)
                if has(e):
                    act.wait_ge(S["xrT_ps"], e + 1)
                    if not isinstance(e, int) or e >= 2:
                        act.wait_ge(S["logit"], pairs_before(e, u))
                    act.copy(xrT[:, (u - 5) % 2, :, :].rearrange("p k n -> p (k n)"), p_xt[:, 0:D]).then_inc(S["xrT"], 1)
                if has(b):
                    pp = (u - 2) % 2
                    act.wait_ge(S["rp"], 2 * b + 2)
                    wait(act, S["ex"], b)
                    act.activation(mn[:], rp[:], ACT.Relu, scale=-1.0).then_inc(S["mn"], 1)
                    act.wait_ge(S["mn"], b + 1)
                    wait(act, S["ph"], b)
                    act.activation(ex[:], mn[:], ACT.Exp, scale=-1.0).then_inc(S["ex"], 1)
                    act.wait_ge(S["vg"], b + 1)
                    wait(act, S["kv"], 2 * (b - 1))
                    wait(act, S["att"], b - 1)
                    act.copy(v1[:, pp, :, 0:P], p_vg[:, 0:D].rearrange("p (k n) -> p k n", k=DH))
                    act.activation(th[:, pp, :], p_vg[:, D:2 * D], ACT.Tanh, scale=0.5).then_inc(S["vth"], 1)
                if has(a):
                    pp = u % 2
                    act.wait_ge(S["rstd1"], a + 1)
                    wait(act, S["h"], a - 1)
                    act.activation(n1[:, pp, :], p_tok[:, 0:D], ACT.Identity, scale=rs1[:, pp:pp + 1], bias=nb1[:, pp:pp + 1]
                                   ).then_inc(S["norm1"], 1)
                if has(d):
                    pp = u % 2
                    act.wait_ge(S["x1"], d + 1)
                    act.activation(junk[:], x1[:, pp, :], ACT.Square, accum_out=ssq2[:, pp:pp + 1]).then_inc(S["ssq2"], 1)
            supersteps(act, step)

        @block.gpsimd
        def _(pool):
            pst = Steps(pool, S["psteps"])
            pool.wait_ge(summed, 1)
            pool.tensor_tensor(win, win, length, ALU.mult).then_inc(averaged, 1)
            pool.wait_ge(setup, 1)
            pool.wait_ge(filled, 16 * (N_SLOT // P // 8 + 1))

            def rsqrt(out, src):
                return pool.tensor_tensor(out, src, half[:], ALU.pow)

            def norm(rs, nb, mv, ve, pp, done):
                c = slice(pp, pp + 1)
                pst.link(rsqrt(rs[:, c], ve[:, c]))
                pst.link(pool.tensor_tensor(mr[:], mv[:, pp, 0:1], rs[:, c], ALU.mult))
                pool.tensor_tensor(nb[:, c], mr[:], minus[:], ALU.mult).then_inc(S[done], 1)

            def step(i, u):
                a, a1, d, e = i, i - 1, i - 4, i - 5
                if has(a1):
                    pp = (u - 1) % 2
                    pool.wait_ge(S["var2"], a1 + 1)
                    wait(pool, S["xln"], a1 - 1)
                    wait(pool, S["rstd1"], a1 if not isinstance(a1, int) else min(a1, NT))
                    norm(rs2, nb2, mv2, ve2, pp, "rstd2")
                if has(a1):
                    pp = (u - 1) % 2
                    pool.wait_ge(S["ssq1"], a1 + 1)
                    pst.link(pool.tensor_tensor(ms1[:, pp:pp + 1], ssq1[:, pp:pp + 1], inv_d[:], ALU.mult))
                    rsqrt(rr1[:, pp:pp + 1], ms1[:, pp:pp + 1]).then_inc(S["rr1"], 1)
                if has(e - 2 - u % 2):
                    v = u % 2
                    if v == 0:
                        pool.wait_ge(S["rows"], pairs(e - 2))
                        pst.fence()
                    slot = (u - 8) % 4
                    for k in range(TOP):
                        pool.indirect_dma_start(xd_dram, bass.IndirectOffsetOnAxis(ap=srow[:, slot // 2, k, v:v + 1], axis=0),
                                                xr[:, slot, :], None, bounds_check=N_SLOT - 1,
                                                oob_is_err=False).then_inc(scattered[slot], 16)
                if has(a):
                    pp = u % 2
                    pool.wait_ge(S["var1"], a + 1)
                    wait(pool, S["norm1"], a - 1)
                    wait(pool, S["rstd2"], a)
                    norm(rs1, nb1, mv1, ve1, pp, "rstd1")
                if has(a):
                    pp = u % 2
                    pool.wait_ge(S["norm1"], a + 1)
                    pst.link(pool.tensor_tensor(n1g[:], n1[:, pp, :], gain[:], ALU.mult))
                    pool.tensor_tensor(res[:, bass.ds(a, 1), :].rearrange("p a d -> p (a d)"), n1g[:], shift[:], ALU.add).then_inc(S["h"], 1)
                if has(d):
                    pp = u % 2
                    pool.wait_ge(S["ssq2"], d + 1)
                    pst.link(pool.tensor_tensor(ms2[:, pp:pp + 1], ssq2[:, pp:pp + 1], inv_d[:], ALU.mult))
                    rsqrt(rr2[:, pp:pp + 1], ms2[:, pp:pp + 1]).then_inc(S["rr2"], 1)
                    r = res[:, bass.ds(d, 1), :].rearrange("p a d -> p (a d)")
                    pool.tensor_tensor(r, r, x1[:, pp, :], ALU.add).then_inc(S["radd"], 1)
            supersteps(pool, step, pst, per_quad=30)
            for k in range(4):
                pool.wait_ge(scattered[k], 32 * (NT // 4))

        @block.vector
        def _(dve):
            st = Steps(dve, S["steps"])
            for t, v in ((emb, 0.0), (contT, 0.0), (mtab, 0.0), (ones_f, 1.0), (v1, 1.0), (half, -0.5), (inv_d, 1.0 / D), (minus, -1.0),
                         (carry, 0.0), (p_kv, 0.0)):
                st.did(dve.memset(t[:], v))
            dve.memset(zero[:], 0.0).then_inc(cleared, 1)
            for pad in (mpad, opad):
                st.did(dve.memset(pad[:, 0:1], 0.0))
                st.did(dve.memset(pad[:, SEQ + 1:SEQ + 2], 0.0))
            st.sync()
            dve.engine_nop().then_inc(su_fix, 1)
            dve.tensor_copy(ones_r[:], ones_f[:]).then_inc(zeroed, 1)
            dve.wait_ge(tok_in, N_TOK_IN)
            row, isb = cst[:, C_ROW:C_ROW + 1], cst[:, C_ISB:C_ISB + 1]
            st.did(dve.tensor_copy(mpad[:, 1:SEQ + 1], msk))
            st.link(dve.tensor_scalar(one, ids, row, None, ALU.is_equal))
            st.link(dve.tensor_tensor(opad[:, 1:SEQ + 1], one, mpad[:, 1:SEQ + 1], ALU.mult))
            dve.tensor_scalar(one, one, isb, None, ALU.max).then_inc(one_done, 1)
            st.did(dve.tensor_tensor(length, mpad[:, 0:SEQ], mpad[:, 1:SEQ + 1], ALU.add))
            st.link(dve.tensor_tensor(win, opad[:, 0:SEQ], opad[:, 1:SEQ + 1], ALU.add))
            st.did(dve.tensor_tensor(length, length, mpad[:, 2:SEQ + 2], ALU.add))
            st.link(dve.tensor_tensor(win, win, opad[:, 2:SEQ + 2], ALU.add))
            st.link(dve.tensor_scalar(length, length, 1.0, None, ALU.max))
            dve.reciprocal(length, length).then_inc(summed, 1)
            dve.wait_ge(loaded, N_LOADED)
            st.link(dve.memset(bias_hl[:].bitcast(F32), 0.0))
            st.did(dve.tensor_copy(bias_hl[0:1, :], bias[0:1, :]))
            st.did(dve.tensor_copy(ones_b[:], ones_f[:]))
            st.did(dve.tensor_copy(tri_b[:], cst[:, C_TRI:C_TRI + P]))
            split_weights(st, raw_o[:], None, wo_hi[:], wo_lo[:], None)
            dve.wait_ge(averaged, 1)
            dve.tensor_scalar(win, win, isb, None, ALU.add).then_inc(win_done, 1)
            st.sync()
            st.eng = dve
            for k in range(DH):
                st.did(dve.tensor_scalar(w_r[:, k, :], raw_r[:, k, :], sc2[:, k:k + 1], None, ALU.mult))
            st.link(dve.tensor_copy(bias_hl[32:33, :], bias[32:33, :]))
            st.link(dve.tensor_tensor(bias[32:33, :], bias[32:33, :], bias_hl[32:33, :].bitcast(F32), ALU.subtract))
            st.link(dve.tensor_copy(bias_hl[32:33, :], bias[32:33, :]))
            for k in range(DH):
                split_weights(st, raw[:, k, :], raw[:, k, :], w_hi[:, k, :], w_lo[:, k, :], sc1[:, k:k + 1])
            st.sync()
            dve.engine_nop().then_inc(su_dve, 1)
            dve.wait_ge(su_pe, 2)
            st.did(dve.tensor_copy(embT[:].rearrange("p k v -> p (k v)"), p_tr[:, 0:64]))
            st.link(dve.tensor_copy(contT[:, :, 0:VOCAB], p_num[:, 0:64].rearrange("p (k v) -> p k v", k=DH)[:, :, 0:VOCAB]))
            dve.engine_nop().then_inc(su_fix, 1)
            dve.engine_nop().then_inc(su_dve, 1)
            dve.wait_ge(su_pe, 4)
            st.did(dve.tensor_copy(mtab[0:32, :], p_wo[0:32, 0:D]))
            st.link(dve.tensor_copy(mtab[32:64, :], p_xt[0:32, 0:D]))
            dve.engine_nop().then_inc(su_fix, 1)
            dve.engine_nop().then_inc(setup, 1)

            def step(i, u):
                a, a1, b, c, d, e = i, i - 1, i - 2, i - 3, i - 4, i - 5

                def masked_state(ch):
                    dve.wait_ge(S["kv"], 2 * c + 1 + ch)
                    if ch == 0:
                        wait(dve, S["num"], c)
                    v = p_kv[:, 0:DH * (P + 1)].rearrange("p (h n) -> p h n", h=DH)
                    m = cst[:, C_BD:C_BD + BDW].rearrange("p (a n) -> p a n", a=1)
                    dve.tensor_tensor(bd[:, ch, :, 0:P], v[:, :, 0:P], m[:, :, 0:P].broadcast_to([P, DH, P]), ALU.mult)
                    dve.tensor_tensor(bd[:, ch, :, P:BDW], v[:, :, P:P + 1].broadcast_to([P, DH, HPH]),
                                      m[:, :, P:BDW].broadcast_to([P, DH, HPH]), ALU.mult).then_inc(S["bd"], 1)

                def statistics(src, stt, mv, ve, pp, done):
                    st.fence()
                    st.link(dve.bn_stats(stt[:], src))
                    st.fence()
                    st.link(dve.bn_aggr(mv[:, pp, :], stt[:]))
                    dve.tensor_scalar(ve[:, pp:pp + 1], mv[:, pp, 1:2], EPS, None, ALU.add).then_inc(S[done], 1)

                if has(c):
                    masked_state(0)
                if has(b):
                    dve.wait_ge(S["xaT_hi"], b + 1)
                    dve.tensor_tensor(xaT_lo[:].rearrange("p k n -> p (k n)"), p_xt[:, 0:D],
                                      xaT_hi[:].bitcast(F32).rearrange("p k n -> p (k n)"), ALU.subtract).then_inc(S["xaT_lo"], 1)
                if has(d):
                    dve.wait_ge(S["atT_hi"], d + 1)
                    dve.tensor_tensor(atT_lo[:].rearrange("p k n -> p (k n)"), p_tr[:, 0:D],
                                      atT_hi[:].bitcast(F32).rearrange("p k n -> p (k n)"), ALU.subtract).then_inc(S["atT_lo"], 1)
                if has(a1):
                    dve.wait_ge(S["h"], a1 + 1)
                    wait(dve, S["rstd2"], a1 - 1)
                    statistics(res[:, bass.ds(a1, 1), :].rearrange("p a d -> p (a d)"), st2, mv2, ve2, (u - 1) % 2, "var2")
                if has(c):
                    masked_state(1)
                if has(e - 1) and u % 2 == 1:
                    route_logits(e - 1)
                    route_choice(e - 1)
                if has(e - 2) and u % 2 == 0:
                    route_rows(e - 2, u - 2)
                if has(b):
                    pp = (u - 2) % 2
                    dve.wait_ge(S["qk"], b + 1)
                    tab = rope[:, bass.ds(b, 1), :]
                    cos, sin = tab[:, :, 0:HALF], tab[:, :, HALF:2 * HALF]
                    src = p_qk[:].rearrange("p (g h i) -> p g h i", h=2, i=HALF)
                    dst = rb_[:].rearrange("p (g h i) -> p g h i", h=2, i=HALF)
                    G = 2 * HEADS
                    st.did(dve.tensor_tensor(ra[:].rearrange("p (g i) -> p g i", i=HALF), p_qk[:].rearrange("p (g i) -> p g i", i=HALF),
                                             cos.broadcast_to([P, 2 * G, HALF]), ALU.mult))
                    st.did(dve.tensor_tensor(dst[:, :, 0, :], src[:, :, 1, :], sin.broadcast_to([P, G, HALF]), ALU.mult))
                    dve.tensor_tensor(dst[:, :, 1, :], src[:, :, 0, :], sin.broadcast_to([P, G, HALF]), ALU.mult).then_inc(S["rope_read"], 1)
                    st.sync()
                    dve.wait_ge(S["rope_read"], b + 1)
                    av = ra[:].rearrange("p (g h i) -> p g h i", h=2, i=HALF)
                    ov = rp[:].rearrange("p (g h i) -> p g h i", h=2, i=HALF)
                    wait(dve, S["mn"], b)
                    wait(dve, S["ph"], b)
                    dve.tensor_tensor(ov[:, :, 0, :], av[:, :, 0, :], dst[:, :, 0, :], ALU.subtract).then_inc(S["rp"], 1)
                    dve.tensor_tensor(ov[:, :, 1, :], av[:, :, 1, :], dst[:, :, 1, :], ALU.add).then_inc(S["rp"], 1)
                cp = (u - 3) % 2
                nv = p_num[:, 0:DH * BDW].rearrange("p (h n) -> p h n", h=DH)
                if has(a):
                    dve.wait_ge(S["tok"], a + 1)
                    wait(dve, S["rstd1"], a - 1)
                    st.did(dve.bn_stats(st1[:], p_tok[:, 0:D]))
                if has(c):
                    dve.wait_ge(S["num"], c + 1)
                    st.did(dve.tensor_scalar(dn[:], nv[:, :, P:BDW], 2.0, 2e-6, ALU.mult, ALU.add))
                st.sync()
                if has(a):
                    st.fence()
                    st.did(dve.bn_aggr(mv1[:, u % 2, :], st1[:]))
                if has(c):
                    st.did(dve.reciprocal(rdn[:], dn[:]))
                st.sync()
                if has(a):
                    dve.tensor_scalar(ve1[:, u % 2:u % 2 + 1], mv1[:, u % 2, 1:2], EPS, None, ALU.add).then_inc(S["var1"], 1)
                if has(c):
                    for h in range(DH):
                        st.did(dve.tensor_tensor(avg[:, h * P:(h + 1) * P].rearrange("p (g i) -> p g i", i=DK),
                                                 nv[:, h, 0:P].rearrange("p (g i) -> p g i", i=DK),
                                                 rdn[:, h, :].rearrange("p (g a) -> p g a", a=1).broadcast_to([P, HPH, DK]), ALU.mult))
                    st.sync()
                    wait(dve, S["atT"], c - 1)
                    dve.scalar_tensor_tensor(att[:, cp, :], th[:, cp, :], 1.0, avg[:], ALU.add, ALU.mult).then_inc(S["att"], 1)
                if has(b):
                    pp = (u - 2) % 2
                    dve.wait_ge(S["ex"], b + 1)
                    dve.wait_ge(S["rp"], 2 * b + 2)
                    wait(dve, S["tq"], b - 1)
                    wait(dve, S["kv"], 2 * (b - 1))
                    dve.scalar_tensor_tensor(ph[:, pp, :], rp[:], 0.0, ex[:], ALU.max, ALU.add).then_inc(S["ph"], 1)
                if has(d):
                    pp = u % 2
                    dve.wait_ge(S["wo"], d + 1)
                    wait(dve, S["xr"], d - 1)
                    wait(dve, S["radd"], d - 1)
                    dve.tensor_tensor(x1[:, pp, :], p_wo[:, 0:D], xln[:, u % 4, :],
                                      ALU.add).then_inc(S["x1"], 1)

            def spread(t):
                return t.rearrange("p (a n) -> p a n", n=1).broadcast_to([P, 2, N_EXP])

            def route_logits(e):
                rbb = rb[:].rearrange("p (a n) -> p a n", a=1).broadcast_to([P, 2, N_EXP])
                dve.wait_ge(S["logit"], pairs(e))
                st.link(dve.tensor_tensor(lg[:], p_tok[:, D:D + 2 * N_EXP].rearrange("p (a n) -> p a n", a=2), rbb, ALU.add))
                st.link(dve.tensor_reduce(mx[:], lg[:], X, ALU.max))
                dve.tensor_tensor(lg[:], lg[:], spread(mx[:]), ALU.subtract).then_inc(S["lread"], 1)

            def route_choice(e):
                w8 = cst[:, C_W8:C_W8 + N_EXP].rearrange("p (a n) -> p a n", a=1).broadcast_to([P, 2, N_EXP])
                dve.wait_ge(S["ex_r"], pairs(e))
                st.link(dve.tensor_reduce(sm[:], ex_r[:], X, ALU.add))
                st.link(dve.reciprocal(rsm[:], sm[:]))
                st.link(dve.tensor_tensor(prob[:], ex_r[:], spread(rsm[:]), ALU.mult))
                for k, src in ((0, prob), (1, prob2)):
                    st.link(dve.tensor_reduce(top[:, k, :], src[:], X, ALU.max))
                    st.link(dve.tensor_tensor(eq[:], src[:], spread(top[:, k, :]), ALU.is_equal))
                    st.link(dve.tensor_tensor(eq[:], eq[:], w8, ALU.mult))
                    st.link(dve.tensor_reduce(kx[:], eq[:], X, ALU.max))
                    st.link(dve.tensor_tensor(pick[:, k, :, :], eq[:], spread(kx[:]), ALU.is_equal))
                    if k == 0:
                        st.link(dve.scalar_tensor_tensor(prob2[:], pick[:, 0, :, :], -2.0, prob[:], ALU.mult, ALU.add))
                dve.tensor_tensor(picked[:], pick[:, 0, :, :], pick[:, 1, :, :], ALU.add).then_inc(S["picked"], 1)
                st.link(dve.tensor_tensor(tsum[:], top[:, 0, :], top[:, 1, :], ALU.add))
                st.link(dve.reciprocal(trec[:], tsum[:]))
                st.link(dve.tensor_tensor(gt[:], top[:], trec[:].rearrange("p (a n) -> p a n", a=1).broadcast_to([P, TOP, 2]), ALU.mult))

            def route_rows(e, u):
                q = ((u - 5) % 4) // 2
                off = cst[:, C_OFF:C_OFF + N_EXP].rearrange("p (a n) -> p a n", a=1).broadcast_to([P, 2, N_EXP])
                dve.wait_ge(S["rank_ps"], pairs(e))
                o = D + 2 * N_EXP
                pre = p_tok[:, o:o + 2 * N_EXP].rearrange("p (a n) -> p a n", a=2)
                tot = p_tok[:, o + 2 * N_EXP:o + 4 * N_EXP].rearrange("p (a n) -> p a n", a=2)
                st.link(dve.tensor_tensor(rank[:, 0, :], pre[:, 0, :], carry[:], ALU.add))
                st.link(dve.tensor_tensor(carry[:], tot[:, 0, :], carry[:], ALU.add))
                st.link(dve.tensor_tensor(rank[:, 1, :], pre[:, 1, :], carry[:], ALU.add))
                dve.tensor_tensor(carry[:], tot[:, 1, :], carry[:], ALU.add).then_inc(S["rread"], 1)
                st.link(dve.tensor_scalar(place[:], rank[:], float(CAP), float(DROPPED), ALU.is_ge, ALU.mult))
                st.link(dve.tensor_tensor(place[:], place[:], rank[:], ALU.add))
                st.link(dve.tensor_tensor(place[:], place[:], off, ALU.add))
                for k in range(TOP):
                    st.did(dve.tensor_tensor(sel[:, k, :, :], pick[:, k, :, :], place[:], ALU.mult))
                st.sync()
                st.link(dve.tensor_reduce(rowf[:], sel[:], X, ALU.add))
                for v in range(2):
                    wait(dve, scattered[2 * q + v], (e - (u - 5) % 4) * 8)
                dve.tensor_copy(srow[:, q, :, :], rowf[:]).then_inc(S["rows"], 1)
                st.did(dve.tensor_scalar(okf[:], rowf[:], float(N_SLOT), None, ALU.is_lt))
                st.sync()
                t0 = e - 1
                for k in range(TOP):
                    st.did(dve.tensor_tensor(gates[:, k, bass.ds(t0, 2)], gt[:, k, :], okf[:, k, :], ALU.mult))
                    st.did(dve.tensor_scalar(rows[:, k, bass.ds(t0, 2)], rowf[:, k, :], float(N_SLOT), None, ALU.min))

            def before(b):
                if isinstance(b, int) and b == 0:
                    return
                dve.memset(p_kv[:, 0:DH * (P + 1)], 0.0).then_inc(zeroed, 1)
            before.counted = 0
            supersteps(dve, step, st, per_quad=K_DVE, before_batch=before)


class Signals:

    def __init__(self, scope):
        self.scope, self.sems, self.ahead = scope, {}, {}

    def make(self, names, ahead=0):
        for n in names.split():
            self.sems[n], self.ahead[n] = self.scope.sem(n), ahead

    def start(self, eng, names):
        for n in names.split():
            eng.sem_inc(self.sems[n], self.ahead[n])

    def wait(self, eng, name, value):
        eng.wait_ge(self.sems[name], value + self.ahead[name])

    def __getitem__(self, name):
        return self.sems[name]


def expert_phase(nc, io, xd_dram, yd_dram):
    R = 256
    NBE = CAP // R
    BP = 2 * NBE
    HT = HID // P
    with ExitStack() as ctx:
        s = Scope(ctx, nc, "moe")
        ident = s.sb("ident", [P, P])
        sc2 = s.sb("sc2", [P, DH])
        raw = s.sb("raw", [P, 2 * DH * HID])
        w_hi, w_lo = s.sb("w_hi", [P, 2, 2 * DH * HID], F32R), s.sb("w_lo", [P, 2, 2 * DH * HID], F32R)
        b1 = s.sb("b1", [P, 2, HT])
        b2 = s.sb("b2", [P, 2, D])
        xrow = s.sb("xrow", [P, 2, R // P, D])
        xT_hi, xT_lo = s.sb("xT_hi", [P, 2, DH, R], F32R), s.sb("xT_lo", [P, 2, DH, R], F32R)
        hid = s.sb("hid", [P, HT, R])
        h_hi, h_lo = s.sb("h_hi", [P, 2, HT, R], F32R), s.sb("h_lo", [P, 2, HT, R], F32R)
        y = s.sb("y", [P, 2, R // P, D])
        p_x = [s.ps(f"px{k}") for k in range(2)]
        p_h = [s.ps(f"ph{k}") for k in range(4)]
        p_y = [s.ps(f"py{k}") for k in range(2)]
        S = Signals(s)
        S.make("tables w_raw b_in x_in0 x_in1 w_hi w_part vsteps y_st0 y_st1")
        S.make("xT_ps x_hi x_lo hs_lo y_ps y_done y_free", 2)
        S.make("h_ps gelu", 4)
        engines = ctx.enter_context(nc.Block())
        HW = DH * HID
        w1 = [w[:, :, 0:HW].rearrange("p e (k n) -> p e k n", k=DH) for w in (w_hi, w_lo)]
        w2 = [w[:, :, HW:2 * HW].rearrange("p e (m n) -> p e m n", m=HT) for w in (w_hi, w_lo)]

        def pairs(eng, run):
            run(0)
            with eng.Fori(1, N_EXP // 2 - 1) as j:
                run(j)
            run(N_EXP // 2 - 1)

        def block(B):
            return not isinstance(B, int) or 0 <= B < N_EXP * NBE

        def expert(e):
            return not isinstance(e, int) or e < N_EXP

        @engines.sync
        def _(sp):
            def weights(e):
                sp.dma_start(raw[:, 0:HW].rearrange("p (k n) -> p k n", k=DH),
                             io["W1"][bass.ds(e, 1)].rearrange("a (k p) n -> p (a k) n", p=P)).then_inc(S["w_raw"], 16)
                sp.dma_start(raw[:, HW:2 * HW].rearrange("p (m n) -> p m n", m=HT),
                             io["W2"][bass.ds(e, 1)].rearrange("a (m p) n -> p (a m) n", p=P)).then_inc(S["w_raw"], 16)

            def biases(e, ep):
                sp.dma_start(b1[:, ep, :], io["b1"][bass.ds(e, 1)].rearrange("a (m p) -> p (a m)", p=P),
                             allow_slow_non_contiguous=True).then_inc(S["b_in"], 16)
                sp.dma_start(b2[:, ep, :], io["b2"][bass.ds(e, 1)].broadcast_to([P, D])).then_inc(S["b_in"], 16)

            sp.dma_start(ident[:], io["consts"][:, C_ID:C_ID + P]).then_inc(S["tables"], 16)
            sp.dma_start(sc2[:], io["norm2"].rearrange("(k p) -> p k", p=P), allow_slow_non_contiguous=True).then_inc(S["tables"], 16)
            weights(0)
            biases(0, 0)

            def run(j):
                for n in range(BP):
                    B, e = j * BP + n, j * 2 + n // NBE
                    S.wait(sp, "xT_ps", B - 1)
                    sp.dma_start(xrow[:, n % 2], xd_dram[bass.ds(B * R, R), :].rearrange("(a p) d -> p a d", p=P)
                                 ).then_inc(S[f"x_in{n % 2}"], 16)
                    if n % NBE == 1 and expert(e + 1):
                        sp.wait_ge(S["w_part"], (e + 1) * 4)
                        weights(e + 1)
                    if n % NBE == 2 and expert(e + 1):
                        S.wait(sp, "y_done", e * NBE)
                        biases(e + 1, (n // NBE + 1) % 2)
            pairs(sp, run)

        @engines.tensor
        def _(pe):
            S.start(pe, "xT_ps h_ps y_ps")
            pe.wait_ge(S["tables"], 32)

            def transposes(B, n):
                pp = n % 2
                pe.wait_ge(S[f"x_in{pp}"], (B - pp) * 8 + 16)
                S.wait(pe, "x_lo", B - 1)
                for k in range(DH):
                    for r in range(R // P):
                        mm = pe.transpose(p_x[pp][:, k * R + r * P:k * R + (r + 1) * P], xrow[:, pp, r, k * P:(k + 1) * P], ident[:])
                mm.then_inc(S["xT_ps"], 1)

            def first(B, n):
                pp, ep = n % 2, n // NBE
                S.wait(pe, "x_lo", B + 1)
                for m in range(HT):
                    S.wait(pe, "gelu", B * HT + m - 3)
                    c = slice(m * P, (m + 1) * P)
                    split_product(pe, p_h[m % 4][:, 0:R], [(w1[0][:, ep, k, c], w1[1][:, ep, k, c], xT_hi[:, pp, k, :],
                                                            xT_lo[:, pp, k, :]) for k in range(DH)]).then_inc(S["h_ps"], 1)

            def second(B, n):
                pp, ep = n % 2, n // NBE
                S.wait(pe, "hs_lo", B + 1)
                S.wait(pe, "y_done", B - 1)
                for r in range(R // P):
                    c = slice(r * P, (r + 1) * P)
                    mm = split_product(pe, p_y[pp][:, r * D:(r + 1) * D],
                                       [(h_hi[:, pp, m, c], h_lo[:, pp, m, c], w2[0][:, ep, m, :], w2[1][:, ep, m, :])
                                        for m in range(HT)])
                mm.then_inc(S["y_ps"], 1)

            transposes(0, 0)

            def run(j):
                for n in range(BP):
                    B = j * BP + n
                    if n % NBE == 0:
                        pe.wait_ge(S["w_part"], (j * 2 + n // NBE) * 4 + 4)
                    if block(B + 1):
                        transposes(B + 1, (n + 1) % BP)
                    first(B, n)
                    if block(B - 1):
                        second(B - 1, (n - 1) % BP)
            pairs(pe, run)
            second(N_EXP * NBE - 1, BP - 1)

        @engines.scalar
        def _(act):
            S.start(act, "x_hi gelu")

            def high(B, n):
                pp = n % 2
                S.wait(act, "xT_ps", B + 1)
                if not isinstance(B, int) or B > 1:
                    S.wait(act, "h_ps", (B - 1) * HT)
                act.copy(xT_hi[:, pp].rearrange("p k n -> p (k n)"), p_x[pp][:]).then_inc(S["x_hi"], 1)

            high(0, 0)

            def run(j):
                for n in range(BP):
                    B, pp, ep = j * BP + n, n % 2, n // NBE
                    if block(B + 1):
                        high(B + 1, (n + 1) % BP)
                    if n % NBE == 0:
                        act.wait_ge(S["b_in"], (j * 2 + ep) * 32 + 32)
                    S.wait(act, "hs_lo", B)
                    for m in range(HT):
                        S.wait(act, "h_ps", B * HT + m + 1)
                        act.activation(hid[:, m, :], p_h[m % 4][:, 0:R], ACT.Gelu, bias=b1[:, ep, m:m + 1]).then_inc(S["gelu"], 1)
            pairs(act, run)

        @engines.gpsimd
        def _(pool):
            S.start(pool, "y_free")

            def low(e, ep, piece):
                c = slice(piece * HID, (piece + 1) * HID)
                pool.wait_ge(S["w_hi"], e * 4 + piece + 1)
                pool.tensor_tensor(w_lo[:, ep, c], raw[:, c], w_hi[:, ep, c].bitcast(F32), ALU.subtract).then_inc(S["w_part"], 1)

            def store(B, n):
                S.wait(pool, "y_done", B + 1)
                pool.dma_start(yd_dram[bass.ds(B * R, R), :].rearrange("(a p) d -> p a d", p=P), y[:, n % 2]
                               ).then_inc(S[f"y_st{n % 2}"], 16)
                pool.wait_ge(S[f"y_st{n % 2}"], (B - n % 2) * 8 + 16)
                pool.sem_inc(S["y_free"], 1)
            for piece in range(4):
                low(0, 0, piece)

            def run(j):
                for n in range(BP):
                    B, e = j * BP + n, j * 2 + n // NBE
                    if n % NBE > 0 and expert(e + 1):
                        low(e + 1, (n // NBE + 1) % 2, n % NBE - 1)
                    if block(B - 1):
                        store(B - 1, (n - 1) % BP)
            pairs(pool, run)
            store(N_EXP * NBE - 1, BP - 1)

        @engines.vector
        def _(dve):
            S.start(dve, "x_lo hs_lo y_done")
            dve.wait_ge(S["tables"], 32)
            st = Steps(dve, S["vsteps"])

            def high(e, ep, piece):
                c = slice(piece * HID, (piece + 1) * HID)
                if piece == 0:
                    dve.wait_ge(S["w_raw"], e * 32 + 32)
                    if not isinstance(e, int) or e > 1:
                        S.wait(dve, "y_ps", (e - 1) * NBE)
                if piece < DH:
                    st.link(dve.tensor_scalar(raw[:, c], raw[:, c], sc2[:, piece:piece + 1], None, ALU.mult))
                dve.tensor_copy(w_hi[:, ep, c], raw[:, c]).then_inc(S["w_hi"], 1)

            def x_low(B, n):
                pp = n % 2
                S.wait(dve, "x_hi", B + 1)
                dve.tensor_tensor(xT_lo[:, pp].rearrange("p k n -> p (k n)"), p_x[pp][:],
                                  xT_hi[:, pp].rearrange("p k n -> p (k n)").bitcast(F32), ALU.subtract).then_inc(S["x_lo"], 1)

            def hidden(B, n):
                pp = n % 2
                S.wait(dve, "y_ps", B - 1)
                for q in range(2):
                    c = slice(q * HT // 2, (q + 1) * HT // 2)
                    S.wait(dve, "gelu", B * HT + (q + 1) * HT // 2)
                    st.link(dve.tensor_copy(h_hi[:, pp, c, :], hid[:, c, :]))
                    lo = dve.tensor_tensor(h_lo[:, pp, c, :], hid[:, c, :], h_hi[:, pp, c, :].bitcast(F32), ALU.subtract)
                lo.then_inc(S["hs_lo"], 1)

            def out_rows(B, n):
                pp, ep = n % 2, n // NBE
                S.wait(dve, "y_ps", B + 1)
                S.wait(dve, "y_free", B - 1)
                dve.tensor_tensor(y[:, pp], p_y[pp][:].rearrange("p (a d) -> p a d", d=D),
                                  b2[:, ep:ep + 1, :].broadcast_to([P, R // P, D]), ALU.add).then_inc(S["y_done"], 1)

            for piece in range(4):
                high(0, 0, piece)
            s0 = st.n
            K = 2 * BP + 2 * DH
            x_low(0, 0)

            def run(j):
                st.base, st.n = j * K + s0, 0
                for n in range(BP):
                    B, e = j * BP + n, j * 2 + n // NBE
                    if block(B + 1):
                        x_low(B + 1, (n + 1) % BP)
                    if n % NBE > 1 and expert(e + 1):
                        high(e + 1, (n // NBE + 1) % 2, n % NBE - 1)
                    hidden(B, n)
                    if block(B - 1):
                        out_rows(B - 1, (n - 1) % BP)
                    if n % NBE == 1 and expert(e + 1):
                        high(e + 1, (n // NBE + 1) % 2, 0)
                assert st.n == K or j == N_EXP // 2 - 1, st.n
            pairs(dve, run)
            out_rows(N_EXP * NBE - 1, BP - 1)


def soft_tables_phase(nc, io, phi_hi, phi_lo):
    ST = SOFT // P
    with ExitStack() as ctx:
        s = Scope(ctx, nc, "phi")
        ident, raw = s.sb("ident", [P, P]), s.sb("raw", [P, ST, D])
        banks = [s.ps(f"t{k}") for k in range(4)]
        loaded, turned, high, low = s.sem("loaded"), s.sem("turned"), s.sem("high"), s.sem("low")
        block = ctx.enter_context(nc.Block())
        arrived = [s.sem(f"arrived{q}") for q in range(ST // 4)]
        parts = [(k, q) for q in range(ST // 4) for k in range(DH)]
        cols = lambda n: slice(parts[n][1] * 512, parts[n][1] * 512 + 512)

        @block.sync
        def _(sp):
            sp.dma_start(ident[:], io["consts"][:, C_ID:C_ID + P]).then_inc(loaded, 16)
            src = io["phi_w"].rearrange("(j p) d -> p j d", p=P)
            for q, done in enumerate(arrived):
                sp.dma_start(raw[:, 4 * q:4 * q + 4], src[:, 4 * q:4 * q + 4]).then_inc(done, 16)

        @block.tensor
        def _(pe):
            pe.wait_ge(loaded, 16)
            for n, (k, q) in enumerate(parts):
                pe.wait_ge(arrived[q], 16)
                wait(pe, low, n - 3)
                for i in range(4):
                    mm = pe.transpose(banks[n % 4][:, i * P:(i + 1) * P], raw[:, 4 * q + i, k * P:(k + 1) * P], ident[:])
                mm.then_inc(turned, 1)

        @block.scalar
        def _(act):
            for n, (k, q) in enumerate(parts):
                act.wait_ge(turned, n + 1)
                act.copy(phi_hi[:, k, cols(n)], banks[n % 4][:]).then_inc(high, 1)

        @block.vector
        def _(dve):
            for n, (k, q) in enumerate(parts):
                dve.wait_ge(high, n + 1)
                dve.tensor_tensor(phi_lo[:, k, cols(n)], banks[n % 4][:], phi_hi[:, k, cols(n)].bitcast(F32), ALU.subtract).then_inc(low, 1)


def soft_dispatch_phase(nc, io, yd_dram, xT_dram, res, gates, rows, phi_hi, phi_lo, smax, acc, spare):
    G, QS = 4, 512
    QE = QS // SOFT_P
    K = G * SOFT // QS
    NG = NT // G
    QN = SOFT // QS
    LAG = 4
    with ExitStack() as ctx:
        s = Scope(ctx, nc, "disp")
        sb = s.sb
        ident = sb("ident", [P, P])
        ones_r = sb("ones_r", [P, P], F32R)
        ones_f = sb("ones_f", [P, P])
        bias_hl = sb("bias_hl", [P, SOFT], F32R)
        half = sb("half", [P, 1])
        idx = sb("idx", [P, 2, TOP, G], U32)
        yb = sb("yb", [P, 2, TOP, D])
        hb = sb("hb", [P, D])
        st6 = sb("st6", [P, 6])
        mv = sb("mv", [P, 2, 2])
        ve, rs = sb("ve", [P, 2]), sb("rs", [P, 2])
        xn = sb("xn", [P, 2, G, D])
        xT_hi, xT_lo = sb("xT_hi", [P, 2, G, DH, P], F32R), sb("xT_lo", [P, 2, G, DH, P], F32R)
        mb = sb("mb", [P, QE])
        mq = sb("mq", [P, G, SOFT // QS, SOFT_P])
        halves = sb("halves", [P, 2, QE, SOFT_P // 2])
        su, ru = sb("su", [P, QE]), sb("ru", [P, 2, QE])
        dd = sb("dd", [P, 4, QS])
        sh = spare[:, 0:2 * QS].rearrange("p (a n) -> p a n", a=2)
        e = spare[:, 2 * QS:6 * QS].rearrange("p (a n) -> p a n", a=4)
        xT = spare[:, 6 * QS:6 * QS + 2 * D].rearrange("p (a k n) -> p a k n", a=2, k=DH)
        brow = spare[:, 0:SOFT]
        p_l = [s.ps(f"l{k}") for k in range(2)]
        p_a = [[s.ps(f"a{k}{q}") for q in range(2)] for k in range(DH)]
        p_t = s.ps("t")
        names = ("loaded setup idx gat0 gat1 h2 var rstd xn tps xT32 xThi xTlo xst0 xst1 lps shifted e halved r d xmm accf steps fence").split()
        S = {n: s.sem(n) for n in names}
        block = ctx.enter_context(nc.Block())

        def over_groups(eng, run, st=None, per=0):
            run(0, 0)
            s0 = 0 if st is None else st.base + st.n
            with eng.Fori(0, NG // 2 - 1) as j:
                if st is not None:
                    st.base, st.n = j * (2 * per) + s0, 0
                run(j * 2 + 1, 1)
                run(j * 2 + 2, 0)
                if st is not None:
                    assert st.n == 2 * per, (st.n, 2 * per)
            if st is not None:
                st.base, st.n = s0 + 2 * per * (NG // 2 - 1), 0
            run(NG - 1, 1)

        def more(g):
            return not isinstance(g, int) or g < NG - 1

        FETCH, RESIDUAL, RSTD, NORMAL, TURN, TURNED, TURNED_LOW = 0, 3, 4, 5, 6, 7, 8
        EACH = 2

        def at(kk, stage):
            return kk >= stage and (kk - stage) % EACH == 0 and (kk - stage) // EACH < G

        def tile_at(kk, stage):
            return (kk - stage) // EACH

        def tile(t):
            return bass.ds(t, 1)

        @block.sync
        def _(sp):
            sp.dma_start(ident[:], io["consts"][:, C_ID:C_ID + P]).then_inc(S["loaded"], 16)
            for r in (0, 32):
                sp.dma_start(brow[r:r + 1, :], io["phi_b"].rearrange("(a n) -> a n", a=1)).then_inc(S["loaded"], 16)

            def store(t, i):
                sp.wait_ge(S["xT32"], t + 1)
                sp.dma_start(xT_dram[:, :, bass.ds(t * P, P)], xT[:, i % 2]).then_inc(S[f"xst{i % 2}"], 16)
            for i in range(G):
                store(i, i)

            def run(g, gp):
                if more(g):
                    for i in range(G):
                        store(g * G + G + i, i)
            over_groups(sp, run)
            for k in range(2):
                sp.wait_ge(S[f"xst{k}"], 16 * (NT // 2))

        @block.tensor
        def _(pe):
            pe.wait_ge(S["setup"], 1)

            def turn(t, i, gp):
                pe.wait_ge(S["xn"], t + 1)
                wait(pe, S["xThi"], t)
                for k in range(DH):
                    mm = pe.transpose(p_t[:, k * P:(k + 1) * P], xn[:, gp, i, k * P:(k + 1) * P], ident[:])
                mm.then_inc(S["tps"], 1)
            for i in range(G):
                turn(i, i, 0)

            def logits(g, gp, kk):
                k = g * K + kk
                Q, i = kk // G, kk % G
                pe.wait_ge(S["xTlo"], g * G + i + 1)
                wait(pe, S["shifted"], k - 1)
                c = slice(Q * QS, (Q + 1) * QS)
                pe.matmul(p_l[kk % 2][:], ones_r[:], bias_hl[:, c], start=True, stop=False)
                split_product(pe, p_l[kk % 2][:], [(xT_hi[:, gp, i, h, :], xT_lo[:, gp, i, h, :], phi_hi[:, h, c], phi_lo[:, h, c])
                                                   for h in range(DH)], first=False).then_inc(S["lps"], 1)

            def gather(g, gp, kk):
                k = g * K + kk
                Q, i = kk // G, kk % G
                q = Q % 2
                pe.wait_ge(S["d"], k + 1)
                if i == 0:
                    wait(pe, S["accf"], g * QN + Q - 1)
                for h in range(DH):
                    mm = pe.matmul(p_a[h][q][:], xn[:, gp, i, h * P:(h + 1) * P], dd[:, kk % 4, :], start=i == 0, stop=i == G - 1)
                mm.then_inc(S["xmm"], 1)

            def run(g, gp):
                for kk in range(K):
                    logits(g, gp, kk)
                    if kk >= LAG:
                        gather(g, gp, kk - LAG)
                    elif not isinstance(g, int) or g > 0:
                        gather(g - 1, 1 - gp, kk - LAG + K)
                    if more(g) and at(kk, TURN):
                        turn(g * G + G + tile_at(kk, TURN), tile_at(kk, TURN), 1 - gp)
            over_groups(pe, run)
            for kk in range(K - LAG, K):
                gather(NG - 1, 1, kk)

        @block.scalar
        def _(act):
            act.wait_ge(S["setup"], 1)

            def turned_high(t, i, gp):
                act.wait_ge(S["tps"], t + 1)
                wait(act, S[f"xst{i % 2}"], (t - i % 2) * 8)
                wait(act, S["xTlo"], t - 1)
                act.copy(xT[:, i % 2].rearrange("p k n -> p (k n)"), p_t[:, 0:D]).then_inc(S["xT32"], 1)
                wait(act, S["lps"], (t - i) * QN - K)
                act.copy(xT_hi[:, gp, i].rearrange("p k n -> p (k n)"), p_t[:, 0:D]).then_inc(S["xThi"], 1)
            for i in range(G):
                turned_high(i, i, 0)

            def run(g, gp):
                for kk in range(K):
                    k = g * K + kk
                    act.wait_ge(S["shifted"], k + 1)
                    wait(act, S["d"], k - 3)
                    act.activation(e[:, kk % 4, :], sh[:, kk % 2, :], ACT.Exp).then_inc(S["e"], 1)
                    if more(g):
                        if at(kk, TURNED):
                            i = tile_at(kk, TURNED)
                            turned_high(g * G + G + i, i, 1 - gp)
            over_groups(act, run)

        @block.gpsimd
        def _(pool):
            pool.wait_ge(S["setup"], 1)

            def fetch(t, i, gp, k):
                if i == 0:
                    pool.wait_ge(S["idx"], (t + G) // G)
                wait(pool, S["h2"], t - 1)
                pool.sem_inc(S["fence"], 1)
                pool.indirect_dma_start(yb[:, i % 2, k, :], None, yd_dram,
                                        bass.IndirectOffsetOnAxis(ap=idx[:, gp, k, i:i + 1], axis=0),
                                        bounds_check=N_SLOT, oob_is_err=False).then_inc(S[f"gat{i % 2}"], 16)

            def rstd(t, i):
                pool.wait_ge(S["var"], t + 1)
                pool.tensor_tensor(rs[:, i % 2:i % 2 + 1], ve[:, i % 2:i % 2 + 1], half[:], ALU.pow).then_inc(S["rstd"], 1)

            for i in range(G + 1):
                if i < G:
                    for k in range(TOP):
                        fetch(i, i, 0, k)
                if i > 0:
                    rstd(i - 1, i - 1)

            def halve(g, kk):
                k = g * K + kk
                pool.wait_ge(S["e"], k + 1)
                wait(pool, S["r"], k - 1)
                v = e[:, kk % 4, :].rearrange("p (n s) -> p n s", s=SOFT_P)
                pool.tensor_tensor(halves[:, kk % 2], v[:, :, 0:SOFT_P // 2], v[:, :, SOFT_P // 2:SOFT_P], ALU.add).then_inc(S["halved"], 1)

            def weight(g, kk):
                k = g * K + kk
                pool.wait_ge(S["r"], k + 1)
                wait(pool, S["xmm"], k - 3)
                pool.tensor_tensor(dd[:, kk % 4, :].rearrange("p (n s) -> p n s", s=SOFT_P), e[:, kk % 4, :].rearrange("p (n s) -> p n s", s=SOFT_P),
                                   ru[:, kk % 2, :].rearrange("p (n a) -> p n a", a=1).broadcast_to([P, QE, SOFT_P]), ALU.mult).then_inc(S["d"], 1)

            def run(g, gp):
                first = isinstance(g, int) and g == 0
                for kk in range(K):
                    if kk >= 1:
                        halve(g, kk - 1)
                    elif not first:
                        halve(g - 1, K - 1)
                    if kk >= 2:
                        weight(g, kk - 2)
                    elif not first:
                        weight(g - 1, kk - 2 + K)
                    if more(g):
                        t0 = g * G + G
                        for k in range(TOP):
                            if at(kk, FETCH + k):
                                i = tile_at(kk, FETCH + k)
                                fetch(t0 + i, i, 1 - gp, k)
                        if at(kk, RSTD):
                            i = tile_at(kk, RSTD)
                            rstd(t0 + i, i)
            over_groups(pool, run)
            halve(NG - 1, K - 1)
            weight(NG - 1, K - 2)
            weight(NG - 1, K - 1)

        @block.vector
        def _(dve):
            st = Steps(dve, S["steps"])
            st.did(dve.memset(acc[:], 0.0))
            st.did(dve.memset(half[:], -0.5))
            st.link(dve.memset(ones_f[:], 1.0))
            st.did(dve.tensor_copy(ones_r[:], ones_f[:]))
            st.link(dve.memset(bias_hl[:].bitcast(F32), 0.0))
            dve.wait_ge(S["loaded"], 48)
            st.did(dve.tensor_copy(bias_hl[0:1, :], brow[0:1, :]))
            st.link(dve.tensor_copy(bias_hl[32:33, :], brow[32:33, :]))
            st.link(dve.tensor_tensor(brow[32:33, :], brow[32:33, :], bias_hl[32:33, :].bitcast(F32), ALU.subtract))
            st.link(dve.tensor_copy(bias_hl[32:33, :], brow[32:33, :]))
            dve.engine_nop().then_inc(S["setup"], 1)

            def indices(g, gp):
                dve.tensor_copy(idx[:, gp], rows[:, :, bass.ds(g * G, G)]).then_inc(S["idx"], 1)

            def residual(t, i):
                pp = i % 2
                r = res[:, tile(t), :].rearrange("p a d -> p (a d)")
                dve.wait_ge(S[f"gat{pp}"], (t - pp) * 16 + 32)
                wait(dve, S["xn"], t - 1)
                st.link(dve.scalar_tensor_tensor(hb[:], yb[:, pp, 0, :], gates[:, 0, tile(t)], r, ALU.mult, ALU.add))
                dve.scalar_tensor_tensor(r, yb[:, pp, 1, :], gates[:, 1, tile(t)], hb[:], ALU.mult, ALU.add).then_inc(S["h2"], 1)
                dve.wait_ge(S["h2"], t + 1)
                st.fence()
                st.link(dve.bn_stats(st6[:], r))
                st.fence()
                st.link(dve.bn_aggr(mv[:, pp, :], st6[:]))
                dve.tensor_scalar(ve[:, pp:pp + 1], mv[:, pp, 1:2], EPS, None, ALU.add).then_inc(S["var"], 1)

            def normal(t, i, gp):
                pp = i % 2
                dve.wait_ge(S["rstd"], t + 1)
                wait(dve, S["xmm"], (t - i) * QN - K)
                dve.tensor_scalar(xn[:, gp, i, :], res[:, tile(t), :].rearrange("p a d -> p (a d)"), mv[:, pp, 0:1], rs[:, pp:pp + 1],
                                  ALU.subtract, ALU.mult).then_inc(S["xn"], 1)

            def turned_low(t, i, gp):
                dve.wait_ge(S["xThi"], t + 1)
                dve.tensor_tensor(xT_lo[:, gp, i], xT[:, i % 2], xT_hi[:, gp, i].bitcast(F32), ALU.subtract).then_inc(S["xTlo"], 1)

            indices(0, 0)
            for i in range(G + 1):
                if i < G:
                    residual(i, i)
                if i > 0:
                    normal(i - 1, i - 1, 0)
                    turned_low(i - 1, i - 1, 0)

            def softmax(g, kk):
                k = g * K + kk
                Q, i = kk // G, kk % G
                before = kk > 0 or not isinstance(g, int) or g > 0
                pp = (kk - 1) % 2
                dve.wait_ge(S["lps"], k + 1)
                by_expert = p_l[kk % 2][:].rearrange("p (n s) -> p n s", s=SOFT_P)
                wait(dve, S["shifted"], k)
                st.did(dve.tensor_reduce(mb[:], by_expert, X, ALU.max))
                maxima = st.base + st.n
                st.did(dve.tensor_reduce(mq[:, i, Q, :], p_l[kk % 2][:].rearrange("p (n s) -> p s n", s=SOFT_P), X, ALU.max))
                if before:
                    total(k - 1, pp)
                dve.wait_ge(S["steps"], maxima)
                wait(dve, S["e"], k - 1)
                dve.tensor_tensor(sh[:, kk % 2, :].rearrange("p (n s) -> p n s", s=SOFT_P), by_expert,
                                  mb[:].rearrange("p (n a) -> p n a", a=1).broadcast_to([P, QE, SOFT_P]), ALU.subtract).then_inc(S["shifted"], 1)
                if before:
                    invert(k - 1, pp)
                if Q == QN - 1:
                    st.sync()
                    st.did(dve.tensor_reduce(smax[:, tile(g * G + i), :].rearrange("p a s -> p (a s)"), mq[:, i].rearrange("p q s -> p s q"), X, ALU.max))

            def total(k, pp):
                dve.wait_ge(S["halved"], k + 1)
                wait(dve, S["r"], k)
                st.did(dve.tensor_reduce(su[:], halves[:, pp], X, ALU.add))

            def invert(k, pp):
                st.sync()
                wait(dve, S["d"], k - 1)
                dve.reciprocal(ru[:, pp, :], su[:]).then_inc(S["r"], 1)

            def drain_acc(g, Q):
                dve.wait_ge(S["xmm"], g * K + (Q + 1) * G)
                c = slice(Q * QS, (Q + 1) * QS)
                for h in range(DH):
                    ins = dve.tensor_tensor(acc[:, h, c], p_a[h][Q % 2][:], acc[:, h, c], ALU.add)
                ins.then_inc(S["accf"], 1)

            def run(g, gp):
                first = isinstance(g, int) and g == 0
                for kk in range(K):
                    if kk % G == LAG % G:
                        Q = (kk - G - LAG) // G
                        if Q >= 0:
                            drain_acc(g, Q)
                        elif not first:
                            drain_acc(g - 1, Q + QN)
                    softmax(g, kk)
                    if more(g):
                        t0 = g * G + G
                        if kk == 0:
                            indices(g + 1, 1 - gp)
                        if at(kk, RESIDUAL):
                            i = tile_at(kk, RESIDUAL)
                            residual(t0 + i, i)
                        if at(kk, NORMAL):
                            i = tile_at(kk, NORMAL)
                            normal(t0 + i, i, 1 - gp)
                        if at(kk, TURNED_LOW):
                            i = tile_at(kk, TURNED_LOW)
                            turned_low(t0 + i, i, 1 - gp)
            per = K * 3 + G + 5 * G
            over_groups(dve, run, st, per)
            total(NG * K - 1, (K - 1) % 2)
            invert(NG * K - 1, (K - 1) % 2)
            drain_acc(NG - 1, QN - 2)
            drain_acc(NG - 1, QN - 1)


def soft_experts_phase(nc, io, acc, spare, yt_hi, yt_lo):
    ST = SOFT // P
    EP = P // SOFT_P
    with ExitStack() as ctx:
        s = Scope(ctx, nc, "sexp")
        ident, half = s.sb("ident", [P, P]), s.sb("half", [P, 1])
        eb = spare.rearrange("p (j d) -> p j d", j=ST)
        ew = s.sb("ew", [P, 2, EP, DH, D])
        xs, xl, xh, xhT, yv = s.sb("xs", [P, 2, DH, P]), s.sb("xl", [P, 2, D]), s.sb("xh", [P, 2, D]), s.sb("xhT", [P, 2, DH, P]), s.sb("yv", [P, D])
        st6, mv, ve, rs = s.sb("st6", [P, 6]), s.sb("mv", [P, 2]), s.sb("ve", [P, 2]), s.sb("rs", [P, 2])
        p_t, p_u, p_e = ([s.ps(f"{n}{k}") for k in range(2)] for n in "tue")
        names = "loaded w0 w1 half clip tps var rstd xl xh ups xhT eps ydone steps".split()
        S = {n: s.sem(n) for n in names}
        block = ctx.enter_context(nc.Block())

        def tiles(eng, first, second, st=None, per=0, swap=False):
            def both(j, jp):
                if not swap:
                    first(j, jp)
                second(j - 1, 1 - jp)
                if swap:
                    first(j, jp)
            first(0, 0)
            both(1, 1)
            s0 = 0 if st is None else st.base + st.n
            with eng.Fori(1, ST // 2 - 1) as j:
                if st is not None:
                    st.base, st.n = (j - 1) * (2 * per) + s0, 0
                both(j * 2, 0)
                both(j * 2 + 1, 1)
                if st is not None:
                    assert st.n == 2 * per, st.n
            if st is not None:
                st.base, st.n = s0 + 2 * per * (ST // 2 - 2), 0
            both(ST - 2, 0)
            both(ST - 1, 1)
            second(ST - 1, 1)

        @block.sync
        def _(sp):
            sp.dma_start(ident[:], io["consts"][:, C_ID:C_ID + P]).then_inc(S["loaded"], 16)
            for k in range(EP):
                src = io["expert_b"].rearrange("(j e) h -> e j h", e=EP)[k:k + 1]
                sp.dma_start(eb[32 * k:32 * k + 32], src.broadcast_to([32, ST, D])).then_inc(S["loaded"], 16)

            def first(j, jp):
                wait(sp, S["eps"], j - 1)
                for k in range(EP):
                    sp.dma_start(ew[:, jp, k], io["expert_w"][bass.ds(j * EP + k, 1)].rearrange("a (k p) h -> p (a k) h", p=P)).then_inc(S[f"w{jp}"], 16)
            tiles(sp, first, lambda j, jp: None)

        @block.tensor
        def _(pe):
            pe.wait_ge(S["loaded"], 16 * (1 + EP))

            def first(j, jp):
                pe.wait_ge(S["clip"], j + 1)
                wait(pe, S["xl"], j - 1)
                for k in range(DH):
                    mm = pe.transpose(p_t[jp][:, k * P:(k + 1) * P], xs[:, jp, k, :], ident[:])
                mm.then_inc(S["tps"], 1)

            def second(j, jp):
                pe.wait_ge(S["xh"], j + 1)
                wait(pe, S["xhT"], j - 1)
                for k in range(DH):
                    mm = pe.transpose(p_u[jp][:, k * P:(k + 1) * P], xh[:, jp, k * P:(k + 1) * P], ident[:])
                mm.then_inc(S["ups"], 1)
                pe.wait_ge(S["xhT"], j + 1)
                pe.wait_ge(S[f"w{jp}"], (j - jp) * 32 + 64)
                wait(pe, S["ydone"], j - 1)
                for n in range(EP):
                    for k in range(DH):
                        mm = pe.matmul(p_e[jp][32 * n:32 * n + 32, 0:D], xhT[:, jp, k, 32 * n:32 * n + 32], ew[:, jp, n, k, :],
                                       start=k == 0, stop=k == DH - 1, skip_group_check=True)
                mm.then_inc(S["eps"], 1)
            tiles(pe, first, second)

        @block.scalar
        def _(act):
            def first(j, jp):
                act.wait_ge(S["xl"], j + 1)
                wait(act, S["ups"], j - 1)
                act.activation(xh[:, jp, :], xl[:, jp, :], ACT.Tanh).then_inc(S["xh"], 1)

            def second(j, jp):
                act.wait_ge(S["ups"], j + 1)
                wait(act, S["eps"], j - 1)
                act.copy(xhT[:, jp].rearrange("p k n -> p (k n)"), p_u[jp][:, 0:D]).then_inc(S["xhT"], 1)
            tiles(act, first, second, swap=True)

        @block.gpsimd
        def _(pool):
            pool.wait_ge(S["half"], 1)

            def first(j, jp):
                pool.wait_ge(S["var"], j + 1)
                pool.tensor_tensor(rs[:, jp:jp + 1], ve[:, jp:jp + 1], half[:], ALU.pow).then_inc(S["rstd"], 1)
            tiles(pool, first, lambda j, jp: None)

        @block.vector
        def _(dve):
            st = Steps(dve, S["steps"])
            dve.memset(half[:], -0.5).then_inc(S["half"], 1)
            dve.wait_ge(S["loaded"], 16 * (1 + EP))

            def clip(j, jp):
                wait(dve, S["tps"], j - 1)
                dve.tensor_scalar(xs[:, jp], acc[:, :, bass.ds(j * P, P)], -33000.0, 65000.0, ALU.max, ALU.min).then_inc(S["clip"], 1)
            clip(0, 0)

            def first(j, jp):
                dve.wait_ge(S["tps"], j + 1)
                wait(dve, S["xl"], j)
                st.link(dve.bn_stats(st6[:], p_t[jp][:, 0:D]))
                st.fence()
                st.link(dve.bn_aggr(mv[:], st6[:]))
                dve.tensor_scalar(ve[:, jp:jp + 1], mv[:, 1:2], EPS, None, ALU.add).then_inc(S["var"], 1)
                dve.wait_ge(S["rstd"], j + 1)
                wait(dve, S["xh"], j - 1)
                dve.tensor_scalar(xl[:, jp, :], p_t[jp][:, 0:D], mv[:, 0:1], rs[:, jp:jp + 1], ALU.subtract, ALU.mult).then_inc(S["xl"], 1)
                if not isinstance(j, int) or j < ST - 1:
                    clip(j + 1, 1 - jp)

            def second(j, jp):
                dve.wait_ge(S["eps"], j + 1)
                wait(dve, S["ydone"], j)
                yrow = yv[:].rearrange("p (a d) -> p a d", a=1)
                st.link(dve.tensor_tensor(yrow, p_e[jp][:, 0:D].rearrange("p (a d) -> p a d", a=1), eb[:, bass.ds(j, 1), :], ALU.add))
                st.link(dve.tensor_copy(yt_hi[:, bass.ds(j, 1), :], yrow))
                dve.tensor_tensor(yt_lo[:, bass.ds(j, 1), :], yrow, yt_hi[:, bass.ds(j, 1), :].bitcast(F32), ALU.subtract).then_inc(S["ydone"], 1)
            tiles(dve, first, second, st, 5)


def soft_combine_phase(nc, io, xT_dram, out, res, phi_hi, phi_lo, smax, yt_hi, yt_lo, e):
    ST = SOFT // P
    CT = 512
    SUB = CT // P
    NC = N_TOK // CT
    with ExitStack() as ctx:
        s = Scope(ctx, nc, "comb")
        sb = s.sb
        ident = sb("ident", [P, P])
        bcol = sb("bcol", [P, ST])
        neg = sb("neg", [P, P], F32R)
        same = sb("same", [P, P])
        xraw = sb("xraw", [P, CT])
        xT_hi, xT_lo = sb("xT_hi", [P, 2, DH, CT], F32R), sb("xT_lo", [P, 2, DH, CT], F32R)
        ms = sb("ms", [P, SUB, SOFT_P])
        mT = sb("mT", [P, CT], F32R)
        tot = sb("tot", [P, CT])
        rt = sb("rt", [P, CT])
        cc = sb("cc", [P, 2, CT])
        c_hi, c_lo = sb("c_hi", [P, 2, CT], F32R), sb("c_lo", [P, 2, CT], F32R)
        M2 = 2 * SOFT_P
        p_l = [s.ps(f"l{k}") for k in range(2)]
        p_y = [[s.ps(f"y{k}{h}") for h in range(2)] for k in range(2)]
        p_s, p_m = s.ps("s"), s.ps("m")
        names = "loaded setup xin xhi xlo ms mps mT lps e tot sps rt c chi clo ymm odone st steps".split()
        S = {n: s.sem(n) for n in names}
        block = ctx.enter_context(nc.Block())

        def chunks(eng, run, st=None, per=0):
            run(0, 0)
            run(1, 1)
            s0 = 0 if st is None else st.base + st.n
            with eng.Fori(1, NC // 2 - 1) as j:
                if st is not None:
                    st.base, st.n = (j - 1) * (2 * per) + s0, 0
                run(j * 2, 0)
                run(j * 2 + 1, 1)
                if st is not None:
                    assert st.n == 2 * per, (st.n, 2 * per)
            if st is not None:
                st.base, st.n = s0 + 2 * per * (NC // 2 - 2), 0
            run(NC - 2, 0)
            run(NC - 1, 1)

        def has(c):
            return not isinstance(c, int) or 0 <= c < NC

        @block.sync
        def _(sp):
            sp.dma_start(ident[:], io["consts"][:, C_ID:C_ID + P]).then_inc(S["loaded"], 16)
            sp.dma_start(same[:], io["consts"][:, C_PG:C_PG + P]).then_inc(S["loaded"], 16)
            sp.dma_start(bcol[:], io["phi_b"].rearrange("(j p) -> p j", p=P), allow_slow_non_contiguous=True).then_inc(S["loaded"], 16)

            def load(c):
                for h in range(DH):
                    wait(sp, S["xlo"], c * DH + h)
                    sp.dma_start(xraw[:], xT_dram[:, h, bass.ds(c * CT, CT)]).then_inc(S["xin"], 16)

            def store(c):
                sp.wait_ge(S["odone"], c + 1)
                sp.dma_start(out[bass.ds(c * CT, CT), :].rearrange("(a p) d -> p a d", p=P), res[:, bass.ds(c * SUB, SUB), :]).then_inc(S["st"], 16)
            load(0)

            def run(c, cp):
                if has(c + 1):
                    load(c + 1)
                if has(c - 2):
                    store(c - 2)
            chunks(sp, run)
            store(NC - 2)
            store(NC - 1)
            sp.wait_ge(S["st"], 16 * NC)

        @block.tensor
        def _(pe):
            pe.wait_ge(S["setup"], 1)

            def maxima(c):
                pe.wait_ge(S["ms"], c + 1)
                wait(pe, S["mT"], c)
                for a in range(SUB):
                    mm = pe.transpose(p_m[0:SOFT_P, a * P:(a + 1) * P], ms[:, a, :], ident[:])
                mm.then_inc(S["mps"], 1)
            maxima(0)

            def logits(c, cp, j):
                k = c * ST + j
                if j == 0:
                    pe.wait_ge(S["xlo"], (c + 1) * DH)
                    pe.wait_ge(S["mT"], c + 1)
                wait(pe, S["e"], k - 1)
                sl = slice(j * P, (j + 1) * P)
                m = slice(M2 * cp, M2 * cp + M2)
                pe.matmul(p_l[j % 2][:], neg[m, :], mT[m, :], start=True, stop=False)
                split_product(pe, p_l[j % 2][:], [(phi_hi[:, h, sl], phi_lo[:, h, sl], xT_hi[:, cp, h, :], xT_lo[:, cp, h, :])
                                                  for h in range(DH)], first=False).then_inc(S["lps"], 1)

            def combine(c, cp, j):
                k = c * ST + j
                pe.wait_ge(S["clo"], k + 1)
                if j == 0:
                    wait(pe, S["odone"], c - 1)
                for a in range(SUB):
                    cs = slice(a * P, (a + 1) * P)
                    for n, (lhs, rhs) in enumerate(((c_hi, yt_hi), (c_hi, yt_lo), (c_lo, yt_hi))):
                        mm = pe.matmul(p_y[cp][a // 2][:, (a % 2) * D:(a % 2 + 1) * D], lhs[:, j % 2, cs], rhs[:, j, :],
                                       start=j == 0 and a % 2 == 0 and n == 0, stop=j == ST - 1 and n == 2, skip_group_check=True)
                mm.then_inc(S["ymm"], 1)

            def run(c, cp):
                for j in range(ST):
                    logits(c, cp, j)
                    if j > 0 and has(c - 1):
                        combine(c - 1, 1 - cp, j - 1)
                    if j == 0 and has(c - 2):
                        combine(c - 2, cp, ST - 1)
                    if j == 8 and has(c + 1):
                        maxima(c + 1)
                pe.wait_ge(S["tot"], c + 1)
                wait(pe, S["rt"], c)
                pe.matmul(p_s[:], same[:], tot[:], start=True, stop=True).then_inc(S["sps"], 1)
            chunks(pe, run)
            combine(NC - 2, 0, ST - 1)
            for j in range(ST):
                combine(NC - 1, 1, j)

        @block.scalar
        def _(act):
            act.wait_ge(S["setup"], 1)

            def high(c, cp, h):
                act.wait_ge(S["xin"], (c * DH + h) * 16 + 16)
                wait(act, S["lps"], (c - 1) * ST)
                act.copy(xT_hi[:, cp, h, :], xraw[:]).then_inc(S["xhi"], 1)

            def maxima(c):
                wait(act, S["mps"], c)
                act.copy(ms[:], smax[:, bass.ds(c * SUB, SUB), :]).then_inc(S["ms"], 1)
            for h in range(DH):
                high(0, 0, h)
            maxima(0)

            def weights_high(c, j):
                k = c * ST + j
                act.wait_ge(S["c"], k + 1)
                wait(act, S["ymm"], k - 1)
                act.copy(c_hi[:, j % 2, :], cc[:, j % 2, :]).then_inc(S["chi"], 1)

            def run(c, cp):
                for j in range(ST):
                    k = c * ST + j
                    if has(c - 1):
                        weights_high(c - 1, j)
                    act.wait_ge(S["lps"], k + 1)
                    wait(act, S["c"], k - ST + 1)
                    act.activation(e[:, j, :], p_l[j % 2][:], ACT.Exp, bias=bcol[:, j:j + 1]).then_inc(S["e"], 1)
                    if has(c + 1):
                        if j in (5, 9):
                            high(c + 1, 1 - cp, (j - 5) // 4)
                        if j == 6:
                            maxima(c + 1)
            chunks(act, run)
            for j in range(ST):
                weights_high(NC - 1, j)

        @block.gpsimd
        def _(pool):
            def weights(c, j):
                k = c * ST + j
                if j == 0:
                    pool.wait_ge(S["rt"], c + 1)
                wait(pool, S["clo"], k - 1)
                pool.tensor_tensor(cc[:, j % 2, :], e[:, j, :], rt[:], ALU.mult).then_inc(S["c"], 1)

            def run(c, cp):
                if has(c - 1):
                    for j in range(ST):
                        weights(c - 1, j)
            chunks(pool, run)
            for j in range(ST):
                weights(NC - 1, j)

        @block.vector
        def _(dve):
            st = Steps(dve, S["steps"])
            dve.wait_ge(S["loaded"], 48)
            st.did(dve.tensor_scalar(neg[:], same[:], -1.0, None, ALU.mult))
            st.sync()
            dve.engine_nop().then_inc(S["setup"], 1)

            def low(c, cp, h):
                dve.wait_ge(S["xhi"], c * DH + h + 1)
                dve.tensor_tensor(xT_lo[:, cp, h, :], xraw[:], xT_hi[:, cp, h, :].bitcast(F32), ALU.subtract).then_inc(S["xlo"], 1)

            def maxima(c, cp):
                dve.wait_ge(S["mps"], c + 1)
                m = [slice(M2 * cp + SOFT_P * k, M2 * cp + SOFT_P * (k + 1)) for k in range(2)]
                st.link(dve.tensor_copy(mT[m[0], :], p_m[0:SOFT_P, :]))
                dve.tensor_tensor(mT[m[1], :], p_m[0:SOFT_P, :], mT[m[0], :].bitcast(F32), ALU.subtract).then_inc(S["mT"], 1)
            for h in range(DH):
                low(0, 0, h)
            maxima(0, 0)

            def weights_low(c, j):
                dve.wait_ge(S["chi"], c * ST + j + 1)
                dve.tensor_tensor(c_lo[:, j % 2, :], cc[:, j % 2, :], c_hi[:, j % 2, :].bitcast(F32), ALU.subtract).then_inc(S["clo"], 1)

            def finish(c, cp):
                dve.wait_ge(S["ymm"], (c + 1) * ST)
                for a in range(SUB):
                    rows = res[:, bass.ds(c * SUB + a, 1), :]
                    ins = dve.tensor_tensor(rows, p_y[cp][a // 2][:, (a % 2) * D:(a % 2 + 1) * D].rearrange("p (a d) -> p a d", a=1),
                                            rows, ALU.add)
                ins.then_inc(S["odone"], 1)

            def run(c, cp):
                for j in range(ST):
                    k = c * ST + j
                    if j == 2 and has(c - 2):
                        finish(c - 2, cp)
                    if has(c - 1):
                        weights_low(c - 1, j)
                    dve.wait_ge(S["e"], k + 1)
                    if j == 1:
                        wait(dve, S["sps"], c)
                        st.did(dve.tensor_tensor(tot[:], e[:, 0, :], e[:, 1, :], ALU.add))
                    elif j > 1:
                        st.sync()
                        st.did(dve.tensor_tensor(tot[:], tot[:], e[:, j, :], ALU.add))
                    if has(c + 1):
                        if j in (7, 11):
                            low(c + 1, 1 - cp, (j - 7) // 4)
                        if j == 12:
                            maxima(c + 1, 1 - cp)
                st.sync()
                dve.sem_inc(S["tot"], 1)
                dve.wait_ge(S["sps"], c + 1)
                wait(dve, S["c"], c * ST)
                dve.reciprocal(rt[:], p_s[:]).then_inc(S["rt"], 1)
            chunks(dve, run, st, ST)
            for j in range(ST):
                if j == 2:
                    finish(NC - 2, 0)
                weights_low(NC - 1, j)
            finish(NC - 1, 1)


NAMES = {
    "x": "x", "mask": "mask_BS_i1_0", "emb": "L0_tok_emb", "pca": "L0_tok_pca_lookup", "proj_w": "L0_tok_proj_w",
    "proj_b": "L0_tok_proj_b", "fus_w": "L0_tok_fus_w", "fus_b": "L0_tok_fus_b", "ln_g": "L0_tok_ln_g", "ln_b": "L0_tok_ln_b",
    "norm1": "L0_attn_norm1_scale", "norm2": "L0_attn_norm2_scale", "Wq": "L0_attn_Wq", "bq": "L0_attn_bq",
    "Wk": "L0_attn_Wk", "bk": "L0_attn_bk", "Wv": "L0_attn_Wv", "bv": "L0_attn_bv", "Wg": "L0_attn_Wg", "bg": "L0_attn_bg",
    "Wo": "L0_attn_Wo", "bo": "L0_attn_bo", "router_W": "L0_attn_router_W", "router_b": "L0_attn_router_b",
    "W1": "L0_attn_W1", "b1": "L0_attn_b1", "W2": "L0_attn_W2", "b2": "L0_attn_b2", "phi_w": "L0_ffn_phi_w",
    "phi_b": "L0_ffn_phi_b", "expert_w": "L0_ffn_expert_w", "expert_b": "L0_ffn_expert_b",
}


def tower(nc, io, out):
    with ExitStack() as ctx:
        def dram(name, shape, dt=F32):
            return nc.dram_tensor(name, shape, dt, kind="Internal").ap()
        feat_dram = dram("scratch_features", [64, N_TOK])
        xd_dram = dram("scratch_dispatched", [N_SLOT, D])
        yd_dram = dram("scratch_expert_rows", [N_SLOT + 1, D])
        xT_dram = dram("scratch_tokens_T", [P, DH, N_TOK])
        s = Scope(ctx, nc, "all")
        res = s.sb("res", [P, NT, D])
        gates = s.sb("gates", [P, TOP, NT])
        rows = s.sb("rows", [P, TOP, NT], U32)
        attention_phase(nc, io, feat_dram, xd_dram, yd_dram, res, gates, rows)
        expert_phase(nc, io, xd_dram, yd_dram)
        phi_hi, phi_lo = s.sb("phi_hi", [P, DH, SOFT], F32R), s.sb("phi_lo", [P, DH, SOFT], F32R)
        smax = s.sb("smax", [P, NT, SOFT_P])
        work = s.sb("work", [P, 2 * DH * SOFT])
        acc = work[:, 0:DH * SOFT].rearrange("p (k n) -> p k n", k=DH)
        spare = work[:, DH * SOFT:2 * DH * SOFT]
        soft_tables_phase(nc, io, phi_hi, phi_lo)
        soft_dispatch_phase(nc, io, yd_dram, xT_dram, res, gates, rows, phi_hi, phi_lo, smax, acc, spare)
        yt_hi, yt_lo = s.sb("yt_hi", [P, SOFT // P, D], F32R), s.sb("yt_lo", [P, SOFT // P, D], F32R)
        soft_experts_phase(nc, io, acc, spare, yt_hi, yt_lo)
        soft_combine_phase(nc, io, xT_dram, out, res, phi_hi, phi_lo, smax, yt_hi, yt_lo,
                           work[:].rearrange("p (j n) -> p j n", j=SOFT // P))


def kernel(**inputs):
    import concourse.bacc as bacc
    from concourse.bass_utils import run_bass_kernel_spmd

    nc = bacc.Bacc("TRN2", target_bir_lowering=False, num_devices=1)
    arrays, io = {}, {}
    for short, name in NAMES.items():
        arrays[name] = np.ascontiguousarray(inputs[name])
        io[short] = nc.dram_tensor(name, arrays[name].shape, mybir.dt.from_np(arrays[name].dtype), kind="ExternalInput").ap()
    for name, table in (("consts", constant_table()), ("rope", rotary_table())):
        arrays[name] = table
        io[name] = nc.dram_tensor(name, table.shape, F32, kind="ExternalInput").ap()
    out = nc.dram_tensor("out", [BATCH, SEQ, D], F32, kind="ExternalOutput").ap()
    tower(nc, io, out.rearrange("b s d -> (b s) d"))
    return run_bass_kernel_spmd(nc, [arrays], core_ids=[0]).results[0]["out"]
```
